# Optimizing a Trainium2 kernel written in Bass

```python
import numpy as np
import jax
import jax.numpy as jnp

def _softmax(x, axis=-1):
    return jax.nn.softmax(x, axis=axis)

def _gelu(x):
    return jax.nn.gelu(x, approximate=True)

def _silu(x):
    return jax.nn.silu(x)

def _sigmoid(x):
    return jax.nn.sigmoid(x)

def _layernorm(x, axis=-1, eps=1e-05):
    m = jnp.mean(x, axis=axis, keepdims=True)
    v = jnp.var(x, axis=axis, keepdims=True)
    return (x - m) / jnp.sqrt(v + eps)

def _scatter_add(tgt, idx, src, axis=0):
    return tgt.at[idx].add(src)

def _segment_sum(src, seg, n):
    return jax.ops.segment_sum(src, seg, n)
kernel_name = 'mk_gnn_resnorm_d4_gnn_r32_daa8ab'

def setup_inputs(seed: int=0):
    np.random.seed(seed)
    _w = jnp.asarray

    def _rec_inputs():
        import jax
        import jax.numpy as jnp
        _gk = jax.random.key(seed)
        x = -0.0002117 + 1 * jax.random.normal(jax.random.fold_in(_gk, 1), (3125, 256), jnp.float32)
        src = jax.random.randint(jax.random.fold_in(_gk, 2), (50000,), 0, 3125, jnp.int32)
        dst = jnp.minimum((3125 * jax.random.uniform(jax.random.fold_in(_gk, 3), (50000,)) ** 2.0).astype(jnp.int32), 99999)
        _o = jnp.argsort(dst, stable=True)
        src = src[_o]
        dst = dst[_o]
        edge_attr_64 = -5.3897e-05 + 0.999841 * jax.random.normal(jax.random.fold_in(_gk, 12), (50000, 64), jnp.float32)
        edge_weight = jax.random.uniform(jax.random.fold_in(_gk, 14), (50000,), jnp.float32, 0.0, 0.999998)
        edge_weight_n2 = jax.random.uniform(jax.random.fold_in(_gk, 15), (50000,), jnp.float32, 0.0, 0.999998)
        return (x, src, dst, edge_attr_64, edge_weight, edge_weight_n2)
    x, src, dst, edge_attr_64, edge_weight, edge_weight_n2 = _rec_inputs()

    def _L0_gnn_setup():
        import jax, jax.numpy as jnp
        import numpy as np
        N_NODES = 3125
        N_EDGES = 25000
        DIM = 256
        EPS = 1e-05
        key = jax.random.key(seed)
        ks = jax.random.split(key, 12)
        H = DIM
        s = 1.0 / np.sqrt(H)
        s2 = 1.0 / np.sqrt(2 * H)
        return {'feat': jax.random.normal(ks[0], (N_NODES, DIM), dtype=jnp.float32), 'src': jax.random.randint(ks[1], (N_EDGES,), 0, N_NODES, dtype=jnp.int32), 'dst': jax.random.randint(ks[2], (N_EDGES,), 0, N_NODES, dtype=jnp.int32), 'iw': jax.random.uniform(ks[3], (N_EDGES,), dtype=jnp.float32), 'ow': jax.random.uniform(ks[4], (N_EDGES,), dtype=jnp.float32), 'gamma': jnp.ones((DIM,), jnp.float32), 'beta': jnp.zeros((DIM,), jnp.float32), 'W_in': jax.random.uniform(ks[5], (H, H), jnp.float32, -s, s), 'b_in': jax.random.uniform(ks[6], (H,), jnp.float32, -s, s), 'W_out': jax.random.uniform(ks[7], (H, H), jnp.float32, -s, s), 'b_out': jax.random.uniform(ks[8], (H,), jnp.float32, -s, s), 'W_x2i': jax.random.uniform(ks[9], (2 * H, 2 * H), jnp.float32, -s2, s2), 'b_x2i': jax.random.uniform(ks[10], (2 * H,), jnp.float32, -s2, s2), 'W_h2h': jax.random.uniform(ks[11], (H, 2 * H), jnp.float32, -s, s)}
    _L0_gnn_all = _L0_gnn_setup()
    _L0_gnn_in = {k: v for k, v in _L0_gnn_all.items() if k in ('gamma', 'beta', 'W_in', 'b_in', 'W_out', 'b_out', 'W_x2i', 'b_x2i', 'W_h2h')}
    del _L0_gnn_all

    def _L1_gnn_setup():
        import jax, jax.numpy as jnp
        import numpy as np
        N_NODES = 50000
        N_EDGES = 12500
        D = 256
        EDGE_DIM = 64
        N_LAYERS = 3
        key = jax.random.key(seed)
        ks = jax.random.split(key, 8)
        sc = 1.0 / np.sqrt(D)
        x = jax.random.normal(ks[0], (N_NODES, D), dtype=jnp.float32)
        edge_attr = jax.random.normal(ks[1], (N_EDGES, EDGE_DIM), dtype=jnp.float32)
        edge_index = jax.random.randint(ks[2], (2, N_EDGES), 0, N_NODES, dtype=jnp.int64)
        Wl = jax.random.normal(ks[3], (N_LAYERS, D, D), dtype=jnp.float32) * sc
        bl = jax.random.normal(ks[4], (N_LAYERS, D), dtype=jnp.float32) * 0.01
        Wr = jax.random.normal(ks[5], (N_LAYERS, D, D), dtype=jnp.float32) * sc
        We = jax.random.normal(ks[6], (N_LAYERS, D, EDGE_DIM), dtype=jnp.float32) * (1.0 / np.sqrt(EDGE_DIM))
        be = jax.random.normal(ks[7], (N_LAYERS, D), dtype=jnp.float32) * 0.01
        return {'x': x, 'edge_attr': edge_attr, 'edge_index': edge_index, 'Wl': Wl, 'bl': bl, 'Wr': Wr, 'We': We, 'be': be}
    _L1_gnn_all = _L1_gnn_setup()
    _L1_gnn_in = {k: v for k, v in _L1_gnn_all.items() if k in ('Wl', 'bl', 'Wr', 'We', 'be')}
    del _L1_gnn_all

    def _L2_gnn_setup():
        import jax, jax.numpy as jnp
        import numpy as np
        N_NODES = 50000
        N_EDGES = 25000
        D_IN = 256
        D_H = 256

        def _gcn_conv(x, W, b, src, dst, n):
            h = x @ W
            ones = jnp.ones(src.shape[0], dtype=x.dtype)
            deg = jax.ops.segment_sum(ones, dst, num_segments=n)
            dinv = jnp.where(deg > 0, jax.lax.rsqrt(deg), 0.0)
            norm = dinv[src] * dinv[dst]
            msgs = h[src] * norm[:, None]
            out = jax.ops.segment_sum(msgs, dst, num_segments=n)
            return out + b
        key = jax.random.key(seed)
        ks = jax.random.split(key, 10)
        s = 1.0 / np.sqrt(D_H)
        x = jax.random.normal(ks[0], (N_NODES, D_IN), dtype=jnp.float32)
        edge_index = jax.random.randint(ks[1], (2, N_EDGES), 0, N_NODES, dtype=jnp.int64)
        return {'x': x, 'edge_index': edge_index, 'W_pre': jax.random.normal(ks[2], (D_IN, D_H), dtype=jnp.float32) * s, 'b_pre': jnp.zeros((D_H,), dtype=jnp.float32), 'W1': jax.random.normal(ks[3], (D_H, D_H), dtype=jnp.float32) * s, 'b1': jnp.zeros((D_H,), dtype=jnp.float32), 'W2': jax.random.normal(ks[4], (D_H, D_H), dtype=jnp.float32) * s, 'b2': jnp.zeros((D_H,), dtype=jnp.float32), 'W_post': jax.random.normal(ks[5], (D_H, D_H), dtype=jnp.float32) * s, 'b_post': jnp.zeros((D_H,), dtype=jnp.float32)}
    _L2_gnn_all = _L2_gnn_setup()
    _L2_gnn_in = {k: v for k, v in _L2_gnn_all.items() if k in ('W_pre', 'b_pre', 'W1', 'b1', 'W2', 'b2', 'W_post', 'b_post')}
    del _L2_gnn_all

    def _L3_gnn_setup():
        import jax, jax.numpy as jnp
        import numpy as np
        N_NODES = 50000
        N_EDGES = 25000
        IN_DIM = 256
        OUT_DIM = 256
        BN_EPS = 1e-05
        key = jax.random.key(seed)
        k1, k2, k3, k4 = jax.random.split(key, 4)
        x = jax.random.normal(k1, (N_NODES, IN_DIM), dtype=jnp.float32)
        edge_index = jax.random.randint(k2, (2, N_EDGES), 0, N_NODES, dtype=jnp.int64)
        W = jax.random.normal(k3, (IN_DIM, OUT_DIM), dtype=jnp.float32) * 0.05
        b = jnp.zeros((OUT_DIM,), dtype=jnp.float32)
        gamma = jnp.ones((OUT_DIM,), dtype=jnp.float32)
        beta = jnp.zeros((OUT_DIM,), dtype=jnp.float32)
        return {'x': x, 'edge_index': edge_index, 'W': W, 'b': b, 'gamma': gamma, 'beta': beta}
    _L3_gnn_all = _L3_gnn_setup()
    _L3_gnn_in = {k: v for k, v in _L3_gnn_all.items() if k in ('W', 'b', 'gamma', 'beta')}
    del _L3_gnn_all
    return {'x': x, 'src': src, 'dst': dst, 'edge_attr_64': edge_attr_64, 'edge_weight': edge_weight, 'edge_weight_n2': edge_weight_n2, 'L0_gnn_gamma': _L0_gnn_in['gamma'], 'L0_gnn_beta': _L0_gnn_in['beta'], 'L0_gnn_W_in': _L0_gnn_in['W_in'], 'L0_gnn_b_in': _L0_gnn_in['b_in'], 'L0_gnn_W_out': _L0_gnn_in['W_out'], 'L0_gnn_b_out': _L0_gnn_in['b_out'], 'L0_gnn_W_x2i': _L0_gnn_in['W_x2i'], 'L0_gnn_b_x2i': _L0_gnn_in['b_x2i'], 'L0_gnn_W_h2h': _L0_gnn_in['W_h2h'], 'L1_gnn_Wl': _L1_gnn_in['Wl'], 'L1_gnn_bl': _L1_gnn_in['bl'], 'L1_gnn_Wr': _L1_gnn_in['Wr'], 'L1_gnn_We': _L1_gnn_in['We'], 'L1_gnn_be': _L1_gnn_in['be'], 'L2_gnn_W_pre': _L2_gnn_in['W_pre'], 'L2_gnn_b_pre': _L2_gnn_in['b_pre'], 'L2_gnn_W1': _L2_gnn_in['W1'], 'L2_gnn_b1': _L2_gnn_in['b1'], 'L2_gnn_W2': _L2_gnn_in['W2'], 'L2_gnn_b2': _L2_gnn_in['b2'], 'L2_gnn_W_post': _L2_gnn_in['W_post'], 'L2_gnn_b_post': _L2_gnn_in['b_post'], 'L3_gnn_W': _L3_gnn_in['W'], 'L3_gnn_b': _L3_gnn_in['b'], 'L3_gnn_gamma': _L3_gnn_in['gamma'], 'L3_gnn_beta': _L3_gnn_in['beta']}

def reference(x, src, dst, edge_attr_64, edge_weight, edge_weight_n2, L0_gnn_gamma, L0_gnn_beta, L0_gnn_W_in, L0_gnn_b_in, L0_gnn_W_out, L0_gnn_b_out, L0_gnn_W_x2i, L0_gnn_b_x2i, L0_gnn_W_h2h, L1_gnn_Wl, L1_gnn_bl, L1_gnn_Wr, L1_gnn_We, L1_gnn_be, L2_gnn_W_pre, L2_gnn_b_pre, L2_gnn_W1, L2_gnn_b1, L2_gnn_W2, L2_gnn_b2, L2_gnn_W_post, L2_gnn_b_post, L3_gnn_W, L3_gnn_b, L3_gnn_gamma, L3_gnn_beta):
    import jax
    import jax.numpy as jnp

    def _L0_gnn_ref(feat, src, dst, iw, ow, gamma, beta, W_in, b_in, W_out, b_out, W_x2i, b_x2i, W_h2h):
        import jax, jax.numpy as jnp
        import numpy as np
        N_NODES = 3125
        N_EDGES = 25000
        DIM = 256
        EPS = 1e-05
        N = feat.shape[0]
        num_steps = 1
        mean = jnp.mean(feat, axis=0)
        var = jnp.var(feat, axis=0)
        h = (feat - mean) * jax.lax.rsqrt(var + EPS) * gamma + beta
        for _ in range(num_steps):
            feat_in = h @ W_in + b_in
            feat_out = h @ W_out + b_out
            a_in = jax.ops.segment_sum(feat_in[src] * iw[:, None], dst, num_segments=N)
            a_out = jax.ops.segment_sum(feat_out[dst] * ow[:, None], src, num_segments=N)
            a = jnp.concatenate((a_in, a_out), axis=1)
            xi = a @ W_x2i + b_x2i
            hh = h @ W_h2h
            i_i, i_n = jnp.split(xi, 2, axis=1)
            h_i, h_n = jnp.split(hh, 2, axis=1)
            input_gate = jax.nn.sigmoid(i_i + h_i)
            new_gate = jnp.tanh(i_n + h_n)
            h = new_gate + input_gate * (h - new_gate)
        return h

    def _L1_gnn_ref(x, edge_attr, edge_index, Wl, bl, Wr, We, be):
        import jax, jax.numpy as jnp
        import numpy as np
        N_NODES = 50000
        N_EDGES = 12500
        D = 256
        EDGE_DIM = 64
        N_LAYERS = 3
        src, dst = (edge_index[0], edge_index[1])
        n = x.shape[0]
        deg = jax.ops.segment_sum(jnp.ones((edge_index.shape[1],), x.dtype), dst, num_segments=n)
        inv_deg = (1.0 / jnp.maximum(deg, 1.0))[:, None]
        for l in range(Wl.shape[0]):
            e_msg = edge_attr @ We[l].T + be[l]
            msg = x[src] + e_msg
            agg = jax.ops.segment_sum(msg, dst, num_segments=n) * inv_deg
            x = jax.nn.relu(agg @ Wl[l].T + bl[l] + x @ Wr[l].T)
        return x

    def _L2_gnn_ref(x, edge_index, W_pre, b_pre, W1, b1, W2, b2, W_post, b_post):
        import jax, jax.numpy as jnp
        import numpy as np
        N_NODES = 50000
        N_EDGES = 25000
        D_IN = 256
        D_H = 256

        def _gcn_conv(x, W, b, src, dst, n):
            h = x @ W
            ones = jnp.ones(src.shape[0], dtype=x.dtype)
            deg = jax.ops.segment_sum(ones, dst, num_segments=n)
            dinv = jnp.where(deg > 0, jax.lax.rsqrt(deg), 0.0)
            norm = dinv[src] * dinv[dst]
            msgs = h[src] * norm[:, None]
            out = jax.ops.segment_sum(msgs, dst, num_segments=n)
            return out + b
        n = x.shape[0]
        loops = jnp.arange(n, dtype=edge_index.dtype)
        src = jnp.concatenate([edge_index[0], loops])
        dst = jnp.concatenate([edge_index[1], loops])
        h = x @ W_pre + b_pre
        h = _gcn_conv(h, W1, b1, src, dst, n)
        h = jax.nn.relu(h)
        h = _gcn_conv(h, W2, b2, src, dst, n)
        h = jax.nn.relu(h)
        y = h @ W_post + b_post
        return y

    def _L3_gnn_ref(x, edge_index, W, b, gamma, beta):
        import jax, jax.numpy as jnp
        import numpy as np
        N_NODES = 50000
        N_EDGES = 25000
        IN_DIM = 256
        OUT_DIM = 256
        BN_EPS = 1e-05
        N = x.shape[0]
        loops = jnp.arange(N, dtype=edge_index.dtype)
        src = jnp.concatenate([edge_index[0], loops])
        dst = jnp.concatenate([edge_index[1], loops])
        ones = jnp.ones(src.shape[0], dtype=x.dtype)
        deg = jax.ops.segment_sum(ones, dst, num_segments=N)
        dinv = jnp.where(deg > 0, jax.lax.rsqrt(deg), jnp.zeros_like(deg))
        norm = dinv[src] * dinv[dst]
        h = x @ W
        msg = h[src] * norm[:, None]
        out = jax.ops.segment_sum(msg, dst, num_segments=N) + b
        mean = jnp.mean(out, axis=0)
        var = jnp.mean(jnp.square(out - mean), axis=0)
        out = (out - mean) * jax.lax.rsqrt(var + BN_EPS) * gamma + beta
        return jax.nn.relu(out)
    edge_index = jnp.stack([src, dst])
    x = _layernorm(x + _L0_gnn_ref(x, src, dst, edge_weight, edge_weight_n2, L0_gnn_gamma, L0_gnn_beta, L0_gnn_W_in, L0_gnn_b_in, L0_gnn_W_out, L0_gnn_b_out, L0_gnn_W_x2i, L0_gnn_b_x2i, L0_gnn_W_h2h), axis=-1)
    x = _layernorm(x + _L1_gnn_ref(x, edge_attr_64, edge_index, L1_gnn_Wl, L1_gnn_bl, L1_gnn_Wr, L1_gnn_We, L1_gnn_be), axis=-1)
    x = _layernorm(x + _L2_gnn_ref(x, edge_index, L2_gnn_W_pre, L2_gnn_b_pre, L2_gnn_W1, L2_gnn_b1, L2_gnn_W2, L2_gnn_b2, L2_gnn_W_post, L2_gnn_b_post), axis=-1)
    x = _layernorm(x + _L3_gnn_ref(x, edge_index, L3_gnn_W, L3_gnn_b, L3_gnn_gamma, L3_gnn_beta), axis=-1)
    return x

_drawn_inputs = setup_inputs


def setup_inputs(seed=0):
    import zlib

    import numpy as np

    out = dict(_drawn_inputs(seed))
    spreads = {'L0_gnn_gamma': (1.0, 0.2),
     'L0_gnn_beta': (0.0, 0.1),
     'L2_gnn_b_pre': (0.0, 0.1),
     'L2_gnn_b1': (0.0, 0.1),
     'L2_gnn_b2': (0.0, 0.1),
     'L2_gnn_b_post': (0.0, 0.1),
     'L3_gnn_b': (0.0, 0.8),
     'L3_gnn_gamma': (1.0, 0.2),
     'L3_gnn_beta': (0.0, 0.1)}
    factors = {'L0_gnn_b_x2i': 6.753, 'L1_gnn_bl': 5.395, 'L1_gnn_be': 5.25}
    for name, (base, spread) in spreads.items():
        noise = np.random.default_rng([zlib.crc32(name.encode()), seed]).standard_normal(out[name].shape)
        drawn = base * np.exp(spread * noise) if base else spread * noise
        out[name] = jnp.asarray(drawn.astype(out[name].dtype))
    for name, factor in factors.items():
        out[name] = (out[name] * factor).astype(out[name].dtype)
    return out
```

```python
from contextlib import ExitStack

import concourse.bass as bass
from concourse import mybir

F32 = mybir.dt.float32
I32 = mybir.dt.int32
U32 = mybir.dt.uint32
ALU = mybir.AluOpType
ACT = mybir.ActivationFunctionType
AX = mybir.AxisListType

P = 125
EPS = 1e-5
WIDE = 4
EC = 8
PIECES = 5
SUMS = 4


def places(events):
    return {e: n + 1 for n, e in enumerate(events)}


def build_gnn(nc, x, src, dst, edge_attr, edge_w, edge_w2, gamma0, beta0, W_in, b_in, W_out, b_out, W_x2i, b_x2i,
              W_h2h, Wl, bl, Wr, We, be, W_pre, b_pre, W1, b1, W2, b2, W_post, b_post, W3, b3, gamma3, beta3, out):
    N, D = x.shape
    NT = N // P
    E, EA = edge_attr.shape
    ET = E // P
    CH = ET // EC
    AW = EA + 1
    COLS = WIDE * P
    LAYERS = Wl.shape[0]
    HALVES = D // 128
    RANGES = [(r * WIDE, min(WIDE, NT - r * WIDE)) for r in range(-(-NT // WIDE))]
    NR = len(RANGES)
    ROWS = NT // PIECES
    ZERO = NT * D
    SLAB = 128 * ZERO

    CELLS = -(-(N * N + P) // SLAB) * SLAB
    in_mat = nc.dram_tensor("in_mat", [CELLS, 2], F32, kind="Internal").ap()
    out_mat = nc.dram_tensor("out_mat", [CELLS, 1], F32, kind="Internal").ap()
    count_mat = nc.dram_tensor("count_mat", [N, N], F32, kind="Internal").ap()
    sum_tab = [nc.dram_tensor(f"sum_tab{q}", [N + P, AW], F32, kind="Internal").ap() for q in range(SUMS)]
    attr_val = nc.dram_tensor("attr_val", [P, ET * AW], F32, kind="Internal").ap()
    sums_T = nc.dram_tensor("sums_T", [AW, N], F32, kind="Internal").ap()
    deg_rows = nc.dram_tensor("deg_rows", [2, N], F32, kind="Internal").ap()

    STEPS = [(0, r, m) for r in range(NR) for m in ("in", "out")] + [(p, r, "count") for p in range(1, 7) for r in range(NR)]
    LAST_OF = {}
    for m, (p, r, _) in enumerate(STEPS):
        LAST_OF[p, r] = m
    EPI = [(p, r) for p in range(7) for r in range(NR)]
    OUTS = {0: ["O"], 1: ["O"], 2: ["O"], 3: ["O", "O2"], 4: ["O"], 5: ["O", "O2"], 6: []}
    TRS = {0: ["T"], 1: ["T"], 2: ["T"], 3: ["T", "T2", "H"], 4: [], 5: ["T2"], 6: []}
    AT = 3
    TR_AT = places(["w%d" % i for i in range(2 * LAYERS + LAYERS)] + [("feat", t) for t in range(NT)]
                   + [(0, r, "T") for r in range(NR)] + [("sums", r) for r in range(NR)] + ["deg"]
                   + [(p, r, s) for p, r in EPI if p for s in TRS[p]] + [("F", t) for t in range(NT)])
    OUT_AT = places(["mean", "var"] + [("feat", t) for t in range(NT)]
                    + [(p, r, s, k) for p, r in EPI for s in OUTS[p] for k in range(RANGES[r][1])])
    NORM = [(p, r) for p, r in EPI if p in (0, 3, 5)]
    GATE_AT = places([(p, r, k) for p, r in NORM for k in range(RANGES[r][1])])
    NORM_AT = places(NORM + [("F", t) for t in range(NT)])
    NAT_AT = places([("feat", t) for t in range(NT)]
                    + [(p, r, k) for p, r in EPI if 1 <= p <= 5 for k in range(RANGES[r][1])])
    AGR_AT = places([(p, r) for p, r in EPI if p >= 4])
    LOAD = {}
    landed = [0] * PIECES
    for m, (p, _, _) in enumerate(STEPS):
        for j in range(PIECES):
            n = m * PIECES + j
            s = n % 2 if p == 0 else j
            landed[s] += 16
            LOAD[m, j] = (s, landed[s])
    ROW_AT = {}
    rows_landed = [0, 0]
    for m, (p, _, _) in enumerate(STEPS):
        if p:
            rows_landed[m % 2] += 32 if p <= LAYERS else 16
            ROW_AT[m] = rows_landed[m % 2]

    with ExitStack() as ctx:
        def sb(name, shape, dt=F32):
            return ctx.enter_context(nc.sbuf_tensor(name, shape, dt))

        def sem(name):
            return ctx.enter_context(nc.semaphore(name))

        psum = ctx.enter_context(nc.psum_tensor("psum", [128, 8, 512], F32))
        X = sb("X", [128, NT * D])
        B = [sb(f"B{i}", [128, NT * D]) for i in range(3)]
        ring = sb("ring", [128, 5 * ROWS * COLS])
        agg = sb("agg", [128, 2, 2, COLS])
        xT = sb("xT", [128, 2, COLS])
        rowbuf = sb("rowbuf", [128, 4 * COLS])
        wl0 = sb("wl0", [128, 8 * 512])
        wl1 = sb("wl1", [128, LAYERS * 4 * D])
        wE = sb("wE", [AW, LAYERS * D])
        brow = sb("brow", [6, 2 * D])
        ident = sb("ident", [128, 128])
        gate = sb("gate", [128, 2, 512])
        cols = sb("cols", [128, 6, 2])
        small = sb("small", [128, 242])

        nat = lambda t_: t_[0:P, :].rearrange("p (t f) -> p t f", t=NT)
        Xn, Bn = nat(X), [nat(b) for b in B]
        outT = B[2][:, 0:2 * N].rearrange("p (h n) -> p h n", h=2)
        w3 = lambda t_, a, k, n: t_[:, a:a + k * n].rearrange("p (k n) -> p k n", k=k)
        w_io = w3(wl0, 0, 2, 512)
        w_x2i = w3(wl0, 1024, 4, 512)
        w_h2h = w3(wl0, 3072, 2, 512)
        w_pre, w_1, w_2, w_post = (w3(wl0, i * 512, 2, D) for i in range(4))
        w_3 = w3(wl0, 2048, 2, D)
        w_lT = [w3(wl1, (2 * l) * 512, 2, D) for l in range(LAYERS)]
        w_rT = [w3(wl1, (2 * l + 1) * 512, 2, D) for l in range(LAYERS)]
        bias_row = {"io": 0, "x2i": 1, 0: 2, 1: 3, 2: 4, "post": 5}
        c_pre, c_1, c_2, c_3, c_gamma, c_beta = (cols[:, i, :] for i in range(6))
        so = [0]

        def tiny(n, parts=P):
            so[0] += n
            return small[0:parts, so[0] - n:so[0]]
        mv = tiny(2 * WIDE).rearrange("p (k c) -> p k c", c=2)
        bn6 = tiny(6 * WIDE).rearrange("p (k c) -> p k c", c=6)
        std, rstd = tiny(WIDE), tiny(WIDE)
        eps = tiny(1, 128)
        deg, inv_deg, root, dinv = tiny(NT), tiny(NT), tiny(NT), tiny(NT)
        st6 = tiny(2 * NR * 6, 128).rearrange("p (h r c) -> p h r c", h=2, c=6)
        at_sum_now = [tiny(EC).bitcast(U32) for _ in range(2)]
        mv3 = gate[:, 0, 0:4].rearrange("p (h c) -> p h c", c=2)
        std3, scale3, shift3 = gate[:, 0, 4:6], gate[:, 0, 6:8], gate[:, 0, 8:10]

        acc = lambda m: psum[:, 2 * (m % 2):2 * (m % 2) + 2, 0:COLS]
        trp = psum[:, 4:6, 0:512]
        outp = lambda n: psum[0:P, 6 + n % 2, :]

        ro = [0]

        def carve(n):
            ro[0] += n
            return ring[0:P, ro[0] - n:ro[0]]
        by_tile = lambda a: a.rearrange("p (k n) -> p k n", k=EC)
        src_i, dst_i = carve(ET).bitcast(I32), carve(ET).bitcast(I32)
        weights3 = carve(3 * ET).rearrange("p (t c) -> p t c", c=3)
        src_f, dst_f, cell_in, cell_out, dump_in, dump_out, dump_dst = (carve(ET) for _ in range(7))
        cell_b, dst_b, same_cell, same_dst, before = (by_tile(carve(EC * P)) for _ in range(5))
        attr = [by_tile(carve(EC * AW)) for _ in range(2)]
        val_attr = [carve(EC * AW) for _ in range(2)]
        val_in = [by_tile(carve(EC * 2)) for _ in range(2)]
        val_out = [carve(EC) for _ in range(2)]
        at_in = [carve(EC).bitcast(U32) for _ in range(2)]
        at_out = [carve(EC).bitcast(U32) for _ in range(2)]
        n_cell, n_dst, go_in, go_out, go_dst, own = carve(EC), carve(EC), carve(EC), carve(EC), carve(EC), carve(1)
        lower = carve(P)
        w_e1, w_e2 = gate[0:P, 0, 0:ET], gate[0:P, 1, 0:ET]
        sc_val = [rowbuf[0:P, h * EC * AW:(h + 1) * EC * AW] for h in range(2)]
        at_sum = rowbuf[0:P, 2 * EC * AW:2 * EC * AW + ET].bitcast(U32)
        scale_row = lambda m, w: rowbuf[:, (m % 2) * COLS:(m % 2) * COLS + w]
        sums_row = lambda m, w: rowbuf[0:AW, (2 + m % 2) * COLS:(2 + m % 2) * COLS + w]
        cellT = psum[0:P, 0:2, 0:4 * P].rearrange("p b (k n) -> p b k n", k=4)
        dstT = psum[0:P, 2:4, 0:4 * P].rearrange("p b (k n) -> p b k n", k=4)
        sum_attr = psum[0:P, 4:6, 0:4 * AW].rearrange("p b (k n) -> p b k n", k=4)
        sum_w = psum[0:P, 6, 0:3 * EC].rearrange("p (k n) -> p k n", k=EC)
        raw_l = B[1][:, 0:LAYERS * 512].rearrange("p (l h n) -> p l h n", l=LAYERS, h=2)
        raw_r = B[1][:, LAYERS * 512:2 * LAYERS * 512].rearrange("p (l h n) -> p l h n", l=LAYERS, h=2)
        raw_e = B[1][:, 2 * LAYERS * 512:2 * LAYERS * 512 + LAYERS * 2 * EA].rearrange("p (l h n) -> p l h n", l=LAYERS, h=2)
        ones = agg[0:P, 0, 0, 0:P]
        gamma_b, beta_b, mean_b, var_b = agg[0:P, 1, 0, 0:D], agg[0:P, 1, 1, 0:D], agg[0:P, 0, 1, 0:D], agg[0:P, 0, 0, 128:128 + D]
        hT = lambda t: xT[:, t % 2, 0:2 * P].rearrange("p (h n) -> p h n", h=2)
        tab = [ring[0:P, q * NT * AW:(q + 1) * NT * AW].rearrange("p (t a) -> p t a", a=AW) for q in range(SUMS)]
        sumsT_s = ring[0:AW, SUMS * NT * AW:SUMS * NT * AW + N]
        degT_s = B[0][0:NT, 0:2 * 128].rearrange("p (c n) -> p c n", c=2)
        count_s = ring[0:P, 4 * ROWS * COLS:5 * ROWS * COLS].rearrange("p (t n) -> p t n", t=ROWS)

        def slot(m, j):
            p, r, what = STEPS[m]
            s, w = LOAD[m, j][0], RANGES[r][1] * P
            if what == "in":
                a = ring[0:P, s * 2 * ROWS * COLS:s * 2 * ROWS * COLS + 2 * ROWS * w]
                return a.rearrange("p (t n c) -> p t n c", t=ROWS, c=2)
            base = s * 2 * ROWS * COLS if p == 0 else s * ROWS * COLS
            return ring[0:P, base:base + ROWS * w].rearrange("p (t n) -> p t n", t=ROWS)

        names = ("zeros zero_in zero_out edges_in x_in w_in raw_in row_in mask_step masks prep edges_ready bcast cell_T eq_ready "
                 "sums_done vals_ready at_ready eq_step in_done out_sc_done sc_at w2_in link_s tr_done tr_read "
                 "out_done out_read agg_ready piece_used gates gate_used nat_ready agr_ready mv_ready std_ready norm_ready "
                 "ones_ready stat count_copied count_stored tab_in deg_step deg_rows_out outT_ready fin_ready y_stored "
                 "zero_sum ocol").split()
        S = {n: sem(n) for n in names}
        attr_stored = [sem(f"attr_stored{h}") for h in range(2)]
        attr_in = [sem(f"attr_in{h}") for h in range(2)]
        sc_in = [sem(f"sc_in{h}") for h in range(2)]
        sc_done = [sem(f"sc_done{q}") for q in range(SUMS)]
        load_in = [sem(f"load_in{s}") for s in range(PIECES)]
        rows_in = [sem(f"rows_in{s}") for s in range(2)]
        edge_attr_v = edge_attr.rearrange("(p t) a -> p t a", p=P)
        in_v = in_mat[0:N * N, :].rearrange("(t p d) c -> p t (d c)", p=P, d=N)
        out_v = out_mat[0:N * N, :].rearrange("(t p d) c -> p t (d c)", p=P, d=N)
        count_v = count_mat.rearrange("(t p) d -> p t d", p=P)
        wv = lambda w: w.rearrange("(k p) n -> p k n", p=128)

        def run_schedule(piece, stage, finish, degrees):
            before_ = None
            for m, (p, r, what) in enumerate(STEPS):
                if (p, r) == (1, 0):
                    degrees()
                new_pass = m > 0 and STEPS[m - 1][0] != p
                for j in range(PIECES):
                    if piece:
                        piece(m, j)
                    if before_:
                        for s in {0: ("A", "T"), 1: ("O",), 2: ("N",), 3: ("T2",)}.get(j, ()):
                            stage(*before_, s)
                if finish:
                    finish(m)
                if before_:
                    stage(*before_, "H")
                    stage(*before_, "O2")
                before_ = (p, r) if m == LAST_OF[p, r] else None
                if before_ and r == NR - 1:
                    for s in ("A", "T", "O", "N", "T2", "H", "O2"):
                        stage(*before_, s)
                    before_ = None

        block = ctx.enter_context(nc.Block())
        Z_IN, Z_OUT = 2 * CELLS // SLAB, CELLS // SLAB

        @block.sync
        def _(sp):
            for a, b in ((src_i, src), (dst_i, dst), (w_e1, edge_w), (w_e2, edge_w2)):
                sp.dma_start(a, b.rearrange("(p t) -> p t", p=P)).then_inc(S["edges_in"], 16)
            sp.dma_start(Xn, x.rearrange("(t p) f -> p t f", p=P)).then_inc(S["x_in"], 16)
            sp.dma_start(gamma_b, gamma0.unsqueeze(0).to_broadcast([P, D])).then_inc(S["x_in"], 16)
            sp.dma_start(beta_b, beta0.unsqueeze(0).to_broadcast([P, D])).then_inc(S["x_in"], 16)
            for l in range(LAYERS):
                sp.dma_start(raw_l[:, l], wv(Wl[l])).then_inc(S["raw_in"], 16)
                sp.dma_start(raw_r[:, l], wv(Wr[l])).then_inc(S["raw_in"], 16)
                sp.dma_start(raw_e[:, l], wv(We[l])).then_inc(S["raw_in"], 16)
            for a, w in ((w_io[:, :, 0:D], W_in), (w_io[:, :, D:2 * D], W_out), (w_x2i, W_x2i), (w_h2h, W_h2h)):
                sp.dma_start(a, wv(w)).then_inc(S["w_in"], 16)
            r1 = lambda v: v.unsqueeze(0)
            for a, v in ((brow[0:1, 0:D], b_in), (brow[0:1, D:2 * D], b_out), (brow[1:2, :], b_x2i),
                         (brow[2:3, 0:D], bl[0]), (brow[3:4, 0:D], bl[1]), (brow[4:5, 0:D], bl[2]), (brow[5:6, 0:D], b_post)):
                if a.shape[1] == D and v is b_in:
                    sp.wait_ge(S["ones_ready"], 2)
                sp.dma_start(a, r1(v)).then_inc(S["w_in"], 16)
            sp.dma_start(wE[EA:AW, :], be.rearrange("(a l) d -> a (l d)", a=1)).then_inc(S["w_in"], 16)
            def chunk(c, h, first):
                if not first:
                    sp.wait_ge(S["sums_done"], c - 1)
                sp.dma_start(attr[h][:, :, 0:EA], edge_attr_v[:, bass.ds(EC * c, EC), :]).then_inc(attr_in[h], 16)
            sp.wait_ge(S["prep"], 3)
            for h in range(2):
                chunk(h, h, True)
            with sp.Fori(1, CH // 2) as i:
                for h in range(2):
                    chunk(i * 2 + h, h, False)
            for m, (p, r, what) in enumerate(STEPS):
                t0, nt = RANGES[r]
                c0, w = t0 * P, nt * P
                if m == 0:
                    sp.wait_ge(S["in_done"], 16 * ET)
                    sp.wait_ge(S["out_sc_done"], 16 * ET)
                    for h in range(2):
                        sp.wait_ge(attr_stored[h], 8 * CH)
                if (p, r) == (1, 0):
                    sp.wait_ge(S["count_stored"], 16 * NR * PIECES)
                    for q in range(SUMS):
                        sp.wait_ge(sc_done[q], 16 * ET // SUMS)
                    sp.wait_ge(S["piece_used"], m * PIECES)
                    for q in range(SUMS):
                        sp.dma_start(tab[q], sum_tab[q][0:N, :].rearrange("(t p) a -> p t a", p=P)).then_inc(S["tab_in"], 16)
                    sp.wait_ge(S["tr_read"], TR_AT["deg"])
                    sp.dma_start(sums_T, sumsT_s).then_inc(S["deg_rows_out"], 16)
                    for c in range(2):
                        sp.dma_start(deg_rows[c].rearrange("(t p) -> t p", p=P), degT_s[:, c, 0:P]).then_inc(S["deg_rows_out"], 16)
                    sp.wait_ge(S["deg_rows_out"], 48)
                    sp.wait_ge(S["out_done"], OUT_AT[0, NR - 1, "O", RANGES[-1][1] - 1])
                    for i_, (a, wt) in enumerate(((w_pre, W_pre), (w_1, W1), (w_2, W2), (w_post, W_post), (w_3, W3))):
                        sp.dma_start(a, wv(wt)).then_inc(S["w2_in"], 16)
                if p:
                    if m >= 2 and STEPS[m - 2][0] >= 1:
                        sp.wait_ge(S["agg_ready"], m - 1)
                        sp.wait_ge(S["piece_used"], (m - 1) * PIECES)
                    row = 0 if p <= LAYERS else 1
                    sp.dma_start(scale_row(m, w), deg_rows[row:row + 1, c0:c0 + w].to_broadcast([128, w])).then_inc(rows_in[m % 2], 16)
                    if p <= LAYERS:
                        sp.dma_start(sums_row(m, w), sums_T[:, c0:c0 + w]).then_inc(rows_in[m % 2], 16)
                for j in range(PIECES):
                    n = m * PIECES + j
                    back = 2 if p == 0 else PIECES
                    if n >= back and not (p == 1 and r == 0):
                        sp.wait_ge(S["piece_used"], n - back + 1)
                        if p == 0:
                            q = n - 2
                            mm, jj = divmod(q, PIECES)
                            if STEPS[mm][2] == "in":
                                sp.wait_ge(S["count_copied"], (mm // 2) * PIECES + jj + 1)
                    k = 2 if what == "in" else 1
                    view = {"in": in_v, "out": out_v, "count": count_v}[what]
                    dst_ap = slot(m, j)
                    if what == "in":
                        dst_ap = dst_ap.rearrange("p t n c -> p t (n c)")
                    sp.dma_start(dst_ap, view[:, j * ROWS:(j + 1) * ROWS, k * c0:k * (c0 + w)]).then_inc(load_in[LOAD[m, j][0]], 16)
            for t in range(NT):
                sp.wait_ge(S["norm_ready"], NORM_AT["F", t])
                sp.dma_start(out[t * P:(t + 1) * P, :], Xn[:, t]).then_inc(S["y_stored"], 16)
            sp.wait_ge(S["y_stored"], 16 * NT)

        @block.gpsimd
        def _(pool):
            pool.memset(ident[:, :], 0.0).then_inc(S["mask_step"], 1)
            pool.memset(lower, 1.0).then_inc(S["mask_step"], 1)
            pool.iota(own, pattern=[[0, 1]], base=0, channel_multiplier=1, allow_small_or_imprecise_dtypes=True).then_inc(S["masks"], 1)
            pool.wait_ge(S["mask_step"], 2)
            pool.affine_select(out=ident[:, :], in_=ident[:, :], compare_op=ALU.not_equal, fill=1.0,
                               base=0, pattern=[[-1, 128]], channel_multiplier=1).then_inc(S["masks"], 1)
            pool.affine_select(out=lower, in_=lower, compare_op=ALU.is_gt, fill=0.0,
                               base=0, pattern=[[-1, P]], channel_multiplier=1).then_inc(S["masks"], 1)
            pool.wait_ge(S["zero_in"], 16 * Z_IN)
            pool.wait_ge(S["zero_out"], 16 * Z_OUT)

            def chunk(c, h, first):
                turn_in, turn_at = pool.to_reg(c * 3 + 3), pool.to_reg(c * 3 + 3)
                done = [pool.to_reg(c * (16 * EC) + 16 * k) for k in range(EC)]
                pool.wait_ge(S["masks"], 3)
                pool.wait_ge(S["vals_ready"], turn_in)
                pool.wait_ge(S["at_ready"], turn_at)
                for k in range(EC):
                    for s, mat, at, v in (("in_done", in_mat, at_in, val_in[h][:, k]),
                                          ("out_sc_done", out_mat, at_out, val_out[h][:, k:k + 1])):
                        if k or h or not first:
                            pool.wait_ge(S["masks"], 3)
                            pool.wait_ge(S[s], done[k])
                        pool.indirect_dma_start(out=mat, out_offset=bass.IndirectOffsetOnAxis(ap=at[h][:, k:k + 1], axis=0),
                                                in_=v, in_offset=None, compute_op=ALU.add).then_inc(S[s], 16)
            for h in range(2):
                chunk(h, h, True)
            with pool.Fori(1, CH // 2) as i:
                for h in range(2):
                    chunk(i * 2 + h, h, False)

            for h in range(2):
                pool.wait_ge(attr_stored[h], 8 * CH)
            pool.wait_ge(S["zero_sum"], 16 * SUMS)
            pool.dma_start(sc_val[0], attr_val[:, 0:EC * AW]).then_inc(sc_in[0], 16)

            def sums(c, h, first, last):
                done = [pool.to_reg(c * (16 * EC // SUMS) + 16 * g) for g in range(EC // SUMS)]
                here, turn = pool.to_reg((c + (2 - h)) * 8), pool.to_reg(c + 1)
                pool.wait_ge(S["masks"], 3)
                pool.wait_ge(sc_in[h], here)
                pool.wait_ge(S["sc_at"], turn)
                for k in range(EC):
                    if k >= SUMS or h or not first:
                        pool.wait_ge(S["masks"], 3)
                        pool.wait_ge(sc_done[k % SUMS], done[k // SUMS])
                    pool.indirect_dma_start(out=sum_tab[k % SUMS],
                                            out_offset=bass.IndirectOffsetOnAxis(ap=at_sum_now[h][:, k:k + 1], axis=0),
                                            in_=sc_val[h][:, k * AW:(k + 1) * AW], in_offset=None,
                                            compute_op=ALU.add).then_inc(sc_done[k % SUMS], 16)
                    if k == SUMS - 1 and not last:
                        pool.dma_start(sc_val[1 - h], attr_val[:, bass.ds((c + 1) * (EC * AW), EC * AW)]).then_inc(sc_in[1 - h], 16)
                        pool.tensor_copy(at_sum_now[1 - h], at_sum[:, bass.ds((c + 1) * EC, EC)]).then_inc(S["sc_at"], 1)
            pool.tensor_copy(at_sum_now[0], at_sum[:, 0:EC]).then_inc(S["sc_at"], 1)
            for h in range(2):
                sums(h, h, True, False)
            with pool.Fori(1, CH // 2 - 1) as i:
                for h in range(2):
                    sums(i * 2 + h, h, False, False)
            for h in range(2):
                sums(CH - 2 + h, h, False, h == 1)

        @block.scalar
        def _(act):
            act.wait_ge(S["zeros"], 1)
            for mat, n, s in ((in_mat, Z_IN, "zero_in"), (out_mat, Z_OUT, "zero_out")):
                flat = mat.rearrange("a b -> (a b)")
                for j in range(n):
                    act.dma_start(flat[j * SLAB:(j + 1) * SLAB].rearrange("(p a) -> p a", p=128), B[0][:, :]).then_inc(S[s], 16)
            for q in range(SUMS):
                act.dma_start(sum_tab[q].rearrange("(p a) b -> p (a b)", p=P), B[0][0:P, 0:(N + P) * AW // P]).then_inc(S["zero_sum"], 16)
            for i_, v in enumerate((b_pre, b1, b2, b3, gamma3, beta3)):
                act.dma_start(cols[:, i_, :], v.rearrange("(h p) -> p h", p=128), allow_slow_non_contiguous=True).then_inc(S["ocol"], 16)
            for i_ in range(2 * LAYERS):
                act.wait_ge(S["tr_done"], TR_AT["w%d" % i_])
                wt = (w_lT if i_ < LAYERS else w_rT)[i_ % LAYERS]
                act.activation(wt, trp[:, i_ % 2, :].rearrange("p (k n) -> p k n", k=2), ACT.Copy).then_inc(S["tr_read"], 1)
            for l in range(LAYERS):
                act.wait_ge(S["tr_done"], TR_AT["w%d" % (2 * LAYERS + l)])
                act.activation(wE[0:EA, l * D:(l + 1) * D], trp[0:EA, l % 2, 0:D], ACT.Copy).then_inc(S["tr_read"], 1)
            act.wait_ge(S["stat"], 1)
            act.activation(var_b, var_b, ACT.Sqrt, bias=eps[0:P, :]).then_inc(S["stat"], 1)
            for t in range(NT):
                act.wait_ge(S["tr_done"], TR_AT["feat", t])
                act.activation(hT(t), trp[:, t % 2, 0:2 * P].rearrange("p (h n) -> p h n", h=2), ACT.Copy).then_inc(S["tr_read"], 1)
                act.wait_ge(S["out_done"], OUT_AT["feat", t])
                if t == 0:
                    act.wait_ge(S["zero_out"], 16 * Z_OUT)
                    act.wait_ge(S["zero_in"], 16 * Z_IN)
                    act.wait_ge(S["zero_sum"], 16 * SUMS)
                act.activation(Bn[0][:, t], outp(t)[:, 0:D], ACT.Copy).then_inc(S["nat_ready"], 1)
                act.activation(Bn[1][:, t], outp(t)[:, D:2 * D], ACT.Copy).then_inc(S["out_read"], 1)
            act.wait_ge(S["edges_ready"], 1)

            def chunk(c, h, first):
                if h or not first:
                    act.wait_ge(S["cell_T"], c)
                now = bass.ds(EC * c, EC)
                act.activation(cell_b, cell_in[:, now].unsqueeze(2).to_broadcast([P, EC, P]), ACT.Copy).then_inc(S["bcast"], 1)
                act.activation(dst_b, dst_f[:, now].unsqueeze(2).to_broadcast([P, EC, P]), ACT.Copy).then_inc(S["bcast"], 1)
                act.wait_ge(S["sums_done"], c + 1)
                if not first:
                    act.wait_ge(S["in_done"], (c - 1) * (16 * EC))
                    act.wait_ge(S["out_sc_done"], (c - 1) * (16 * EC))
                    act.wait_ge(attr_stored[h], (c - h) * 8)
                act.activation(val_in[h], sum_w[:, :, 0:2], ACT.Copy).then_inc(S["vals_ready"], 1)
                act.activation(val_out[h], sum_w[:, :, 2], ACT.Copy).then_inc(S["vals_ready"], 1)
                act.activation(val_attr[h].rearrange("p (b k n) -> p b k n", b=2, k=4), sum_attr, ACT.Copy).then_inc(S["vals_ready"], 1)
                act.wait_ge(S["vals_ready"], c * 3 + 3)
                act.dma_start(attr_val[:, bass.ds(c * (EC * AW), EC * AW)], val_attr[h]).then_inc(attr_stored[h], 16)
            for h in range(2):
                chunk(h, h, True)
            with act.Fori(1, CH // 2) as i:
                for h in range(2):
                    chunk(i * 2 + h, h, False)

            def counts(m, j):
                if STEPS[m][2] != "in":
                    return
                q = (m // 2) * PIECES + j
                r = STEPS[m][1]
                w = RANGES[r][1] * P
                act.wait_ge(load_in[LOAD[m, j][0]], LOAD[m, j][1])
                if q:
                    act.wait_ge(S["count_stored"], 16 * q)
                act.activation(count_s[:, :, 0:w], slot(m, j)[:, :, :, 0], ACT.Copy).then_inc(S["count_copied"], 1)
                act.wait_ge(S["count_copied"], q + 1)
                c0 = RANGES[r][0] * P
                act.dma_start(count_v[:, j * ROWS:(j + 1) * ROWS, c0:c0 + w], count_s[:, :, 0:w]).then_inc(S["count_stored"], 16)

            def evac_T(p, r, s, to, col=None):
                w = RANGES[r][1] * P
                act.wait_ge(S["tr_done"], TR_AT[p, r, s])
                if col is None:
                    act.activation(to[:, :, 0:w], trp[:, :, 0:w], ACT.Copy).then_inc(S["tr_read"], 1)
                else:
                    act.activation(to[:, 0, 0:w], trp[:, 0, 0:w], ACT.Identity, bias=col[:, 0:1])
                    act.activation(to[:, 1, 0:w], trp[:, 1, 0:w], ACT.Identity, bias=col[:, 1:2]).then_inc(S["tr_read"], 1)

            def stage(p, r, s):
                t0, nt = RANGES[r]
                m = LAST_OF[p, r]
                w = nt * P
                if s == "A" and p in (4, 5):
                    act.wait_ge(S["agg_ready"], m + 1)
                    if (p, r) == (4, 0):
                        act.wait_ge(S["ocol"], 16 * 6)
                    c = c_1 if p == 4 else c_2
                    act.activation(agg[:, m % 2, 0, 0:w], agg[:, m % 2, 0, 0:w], ACT.Relu, bias=c[:, 0:1])
                    act.activation(agg[:, m % 2, 1, 0:w], agg[:, m % 2, 1, 0:w], ACT.Relu, bias=c[:, 1:2]).then_inc(S["agr_ready"], 1)
                if s == "A" and p == 6:
                    act.wait_ge(S["agg_ready"], m + 1)
                    for hh in range(2):
                        last = act.activation(outT[:, hh, t0 * P:t0 * P + w], agg[:, m % 2, hh, 0:w], ACT.Identity, bias=c_3[:, hh:hh + 1])
                    last.then_inc(S["agr_ready"], 1)
                if s == "T" and p <= 3:
                    evac_T(p, r, "T", xT)
                if s == "O" and p <= 5:
                    for k in range(nt):
                        n = OUT_AT[p, r, "O", k]
                        act.wait_ge(S["out_done"], n)
                        o = outp(n)
                        if p in (0, 3, 5):
                            g = GATE_AT[p, r, k]
                            if g > 2:
                                act.wait_ge(S["gate_used"], g - 2)
                        if p == 0:
                            act.activation(gate[0:P, k % 2, 0:D], o[:, 0:D], ACT.Sigmoid)
                            act.activation(gate[0:P, k % 2, D:2 * D], o[:, D:2 * D], ACT.Tanh).then_inc(S["gates"], 1)
                        elif p in (3, 5):
                            act.activation(gate[0:P, k % 2, 0:D], o[:, 0:D], ACT.Relu if p == 3 else ACT.Copy).then_inc(S["gates"], 1)
                        elif p in (1, 2):
                            act.activation(Bn[p - 1][:, t0 + k], o[:, 0:D], ACT.Relu).then_inc(S["nat_ready"], 1)
                        else:
                            act.activation(Bn[1][:, t0 + k], o[:, 0:D], ACT.Copy, scale=dinv[:, t0 + k:t0 + k + 1]).then_inc(S["nat_ready"], 1)
                if s == "N" and p in (0, 3, 5):
                    act.wait_ge(S["mv_ready"], NORM_AT[p, r])
                    act.activation(std[:, 0:nt], mv[:, 0:nt, 1], ACT.Sqrt, bias=eps[0:P, :]).then_inc(S["std_ready"], 1)
                if s == "T2" and p in (3, 5):
                    evac_T(p, r, "T2", xT)
                if s == "H" and p == 3:
                    if r == 0:
                        act.wait_ge(S["ocol"], 16 * 6)
                    evac_T(p, r, "H", agg[:, m % 2], c_pre)
                if s == "O2" and p in (3, 5):
                    for k in range(nt):
                        n = OUT_AT[p, r, "O2", k]
                        act.wait_ge(S["out_done"], n)
                        act.activation(Bn[0][:, t0 + k], outp(n)[:, 0:D], ACT.Copy, scale=dinv[:, t0 + k:t0 + k + 1]).then_inc(S["nat_ready"], 1)

            def degrees():
                for r, (t0, nt) in enumerate(RANGES):
                    act.wait_ge(S["tr_done"], TR_AT["sums", r])
                    act.activation(sumsT_s[:, t0 * P:(t0 + nt) * P], trp[0:AW, r % 2, 0:nt * P], ACT.Copy).then_inc(S["tr_read"], 1)
                act.wait_ge(S["deg_step"], SUMS)
                act.activation(root, deg, ACT.Sqrt, bias=1.0).then_inc(S["stat"], 1)

            run_schedule(counts, stage, None, degrees)

            act.wait_ge(S["fin_ready"], 1)
            act.activation(std3, mv3[:, :, 1], ACT.Sqrt, bias=eps).then_inc(S["fin_ready"], 1)
            act.wait_ge(S["fin_ready"], 3)
            for r, (t0, nt) in enumerate(RANGES):
                for hh in range(2):
                    v = outT[:, hh, t0 * P:(t0 + nt) * P]
                    last = act.activation(v, v, ACT.Relu, bias=shift3[:, hh:hh + 1], scale=scale3[:, hh:hh + 1])
                last.then_inc(S["outT_ready"], 1)
            for r, (t0, nt) in enumerate(RANGES):
                act.wait_ge(S["mv_ready"], len(NORM) + r + 1)
                act.activation(std[:, 0:nt], mv[:, 0:nt, 1], ACT.Sqrt, bias=eps[0:P, :]).then_inc(S["std_ready"], 1)

        @block.tensor
        def _(pe):
            pe.wait_ge(S["masks"], 3)
            pe.wait_ge(S["raw_in"], 16 * 3 * LAYERS)
            for i_ in range(2 * LAYERS):
                raw = (raw_l if i_ < LAYERS else raw_r)[:, i_ % LAYERS]
                if i_ >= 2:
                    pe.wait_ge(S["tr_read"], i_ - 1)
                for k in range(2):
                    for o in range(2):
                        last = pe.transpose(trp[:, i_ % 2, k * D + o * 128:k * D + (o + 1) * 128], raw[:, o, k * 128:(k + 1) * 128], ident[:, :])
                last.then_inc(S["tr_done"], 1)
            for l in range(LAYERS):
                pe.wait_ge(S["tr_read"], 2 * LAYERS + l - 1)
                for o in range(2):
                    last = pe.transpose(trp[0:EA, l % 2, o * 128:(o + 1) * 128], raw_e[:, l, o, :], ident[:, :])
                last.then_inc(S["tr_done"], 1)
            pe.wait_ge(S["ones_ready"], 1)
            pe.wait_ge(S["x_in"], 48)
            for t in range(NT):
                last = pe.matmul(outp(0)[:, 0:D], ones, Xn[:, t], start=t == 0, stop=t == NT - 1)
            last.then_inc(S["out_done"], 1)
            pe.wait_ge(S["ones_ready"], 3)
            for t in range(NT):
                last = pe.matmul(outp(1)[:, 0:D], ones, Bn[1][:, t], start=t == 0, stop=t == NT - 1)
            last.then_inc(S["out_done"], 1)
            pe.wait_ge(S["stat"], 3)
            pe.wait_ge(S["w_in"], 16 * 12)
            for t in range(NT + 1):
                if t < NT:
                    if t < 2:
                        pe.wait_ge(S["tr_read"], 3 * LAYERS)
                    else:
                        pe.wait_ge(S["tr_read"], TR_AT["feat", t - 2])
                    for hh in range(2):
                        last = pe.transpose(trp[:, t % 2, hh * P:(hh + 1) * P], Bn[2][:, t, hh * 128:(hh + 1) * 128], ident[0:P, 0:P])
                    last.then_inc(S["tr_done"], 1)
                if t:
                    u = t - 1
                    pe.wait_ge(S["tr_read"], TR_AT["feat", u])
                    if u >= 2:
                        pe.wait_ge(S["out_read"], u - 1)
                    for hh in range(2):
                        pe.matmul(outp(u), hT(u)[:, hh], w_io[:, hh], start=hh == 0, stop=False)
                    pe.matmul(outp(u), ident[0:6, 0:1].to_broadcast([6, P]), brow[:, :], start=False, stop=True).then_inc(S["out_done"], 1)

            pe.wait_ge(S["out_read"], NT)
            def chunk(c, h, first):
                pe.wait_ge(S["bcast"], c * 2 + 2)
                if h or not first:
                    pe.wait_ge(S["eq_ready"], c)
                for k in range(EC):
                    pe.transpose(cellT[:, k // 4, k % 4], cell_b[:, k], ident[0:P, 0:P])
                for k in range(EC):
                    last = pe.transpose(dstT[:, k // 4, k % 4], dst_b[:, k], ident[0:P, 0:P])
                last.then_inc(S["cell_T"], 1)
                pe.wait_ge(S["eq_ready"], c + 1)
                pe.wait_ge(attr_in[h], (c + (2 - h)) * 8)
                if h or not first:
                    pe.wait_ge(S["vals_ready"], c * 3)
                for k in range(EC):
                    pe.matmul(sum_w[:, k], same_cell[:, k], weights3[:, bass.ds(EC * c + k, 1), :], start=(k == 0), stop=True, skip_group_check=True)
                for k in range(EC):
                    last = pe.matmul(sum_attr[:, k // 4, k % 4], same_dst[:, k], attr[h][:, k], start=(k % 4 == 0), stop=True, skip_group_check=True)
                last.then_inc(S["sums_done"], 1)
            for h in range(2):
                chunk(h, h, True)
            with pe.Fori(1, CH // 2) as i:
                for h in range(2):
                    chunk(i * 2 + h, h, False)
            pe.wait_ge(S["vals_ready"], 3 * CH)

            SRC = {1: Xn, 2: Bn[0], 3: Bn[1], 4: Bn[0], 5: Bn[1], 6: Bn[0]}

            def piece(m, j):
                p, r, what = STEPS[m]
                t0, nt = RANGES[r]
                w = nt * P
                source = (Bn[0] if what == "in" else Bn[1]) if p == 0 else SRC[p]
                if j == 0:
                    if m >= 2:
                        pe.wait_ge(S["agg_ready"], m - 1)
                    if r == 0 and p == 1:
                        pe.wait_ge(S["norm_ready"], NORM_AT[0, NR - 1])
                    elif r == 0 and p > 1:
                        pe.wait_ge(S["nat_ready"], NAT_AT[p - 1, NR - 1, RANGES[-1][1] - 1])
                s, v = LOAD[m, j]
                pe.wait_ge(load_in[s], v)
                a = acc(m)
                rhs = slot(m, j)
                for i_ in range(ROWS):
                    t = j * ROWS + i_
                    for hh in range(2):
                        last = pe.matmul(a[:, hh, 0:w], source[:, t, hh * 128:(hh + 1) * 128],
                                         rhs[:, i_, :, 1] if what == "in" else rhs[:, i_, :],
                                         start=t == 0, stop=t == NT - 1, skip_group_check=True)
                    if t == 0 and p >= 4:
                        for hh in range(2):
                            for k in range(nt):
                                pe.matmul(a[:, hh, k * P:(k + 1) * P], source[:, t0 + k, hh * 128:(hh + 1) * 128], ident[0:P, 0:P],
                                          start=False, stop=False, skip_group_check=True)
                    if t == NT - 2 and 1 <= p <= LAYERS:
                        pe.wait_ge(rows_in[m % 2], ROW_AT[m])
                        for hh in range(2):
                            pe.matmul(a[:, hh, 0:w], wE[:, (p - 1) * D + hh * 128:(p - 1) * D + (hh + 1) * 128], sums_row(m, w),
                                      start=False, stop=False, skip_group_check=True)
                last.then_inc(S["piece_used"], 1)

            def transposes(p, r, s, from_):
                t0, nt = RANGES[r]
                pe.wait_ge(S["tr_read"], TR_AT[p, r, s] - 1)
                for hh in range(2):
                    for k in range(nt):
                        last = pe.transpose(trp[:, hh, k * P:(k + 1) * P], from_[:, t0 + k, hh * 128:(hh + 1) * 128], ident[0:P, 0:P])
                last.then_inc(S["tr_done"], 1)

            def stage(p, r, s):
                t0, nt = RANGES[r]
                m = LAST_OF[p, r]
                w = nt * P
                if s == "T" and p <= 3:
                    transposes(p, r, s, Bn[2] if p == 0 else SRC[p])
                if s == "T2" and p in (3, 5):
                    pe.wait_ge(S["norm_ready"], NORM_AT[p, r])
                    transposes(p, r, s, Xn)
                if s == "H" and p == 3:
                    if r == 0:
                        pe.wait_ge(S["w2_in"], 16 * 5)
                    pe.wait_ge(S["tr_read"], TR_AT[p, r, "T2"])
                    for o in range(2):
                        for hh in range(2):
                            last = pe.matmul(trp[:, o, 0:w], w_pre[:, hh, o * 128:(o + 1) * 128], xT[:, hh, 0:w], start=hh == 0, stop=hh == 1)
                    last.then_inc(S["tr_done"], 1)
                if s in OUTS[p]:
                    ag = agg[:, m % 2]
                    bias = None
                    if p == 0:
                        pe.wait_ge(S["agg_ready"], m + 1)
                        pe.wait_ge(S["tr_read"], TR_AT[p, r, "T"])
                        ops = [(agg[:, 0, hh], w_x2i[:, hh]) for hh in range(2)] + [(agg[:, 1, hh], w_x2i[:, 2 + hh]) for hh in range(2)] \
                            + [(xT[:, hh], w_h2h[:, hh]) for hh in range(2)]
                        bias = "x2i"
                    elif p <= 3 and s == "O":
                        pe.wait_ge(S["agg_ready"], m + 1)
                        pe.wait_ge(S["tr_read"], TR_AT[p, r, "T"])
                        ops = [(ag[:, hh], w_lT[p - 1][:, hh]) for hh in range(2)] + [(xT[:, hh], w_rT[p - 1][:, hh]) for hh in range(2)]
                        bias = p - 1
                    elif p == 3:
                        pe.wait_ge(S["tr_read"], TR_AT[p, r, "H"])
                        ops = [(ag[:, hh], w_1[:, hh]) for hh in range(2)]
                    elif p == 4:
                        pe.wait_ge(S["agr_ready"], AGR_AT[p, r])
                        ops = [(ag[:, hh], w_2[:, hh]) for hh in range(2)]
                    elif s == "O":
                        pe.wait_ge(S["agr_ready"], AGR_AT[p, r])
                        ops = [(ag[:, hh], w_post[:, hh]) for hh in range(2)]
                        bias = "post"
                    else:
                        pe.wait_ge(S["tr_read"], TR_AT[p, r, "T2"])
                        ops = [(xT[:, hh], w_3[:, hh]) for hh in range(2)]
                    n_out = 2 * D if p == 0 else D
                    for k in range(nt):
                        n = OUT_AT[p, r, s, k]
                        wait_out(n)
                        o = outp(n)[:, 0:n_out]
                        for q, (a, wt) in enumerate(ops):
                            last = pe.matmul(o, a[:, k * P:(k + 1) * P], wt, start=q == 0, stop=bias is None and q == len(ops) - 1)
                        if bias is not None:
                            b = bias_row[bias]
                            last = pe.matmul(o, ident[0:6, b:b + 1].to_broadcast([6, P]), brow[:, 0:n_out], start=False, stop=True)
                        last.then_inc(S["out_done"], 1)

            readers = {}
            for (p_, r_, s_, k_) in [e for e in OUT_AT if isinstance(e, tuple) and len(e) == 4]:
                n_ = OUT_AT[p_, r_, s_, k_]
                readers[n_] = ("gates", GATE_AT[p_, r_, k_]) if s_ == "O" and p_ in (0, 3, 5) else ("nat_ready", NAT_AT[p_, r_, k_])

            def wait_out(n):
                if n - 2 in readers:
                    s_, v_ = readers[n - 2]
                    pe.wait_ge(S[s_], v_)

            def degrees():
                for r, (t0, nt) in enumerate(RANGES):
                    pe.wait_ge(S["tr_read"], TR_AT["sums", r] - 2)
                    if r == 0:
                        pe.wait_ge(S["deg_step"], SUMS - 1)
                    for k in range(nt):
                        last = pe.transpose(trp[0:AW, r % 2, k * P:(k + 1) * P], tab[0][:, t0 + k], ident[0:P, 0:P])
                    last.then_inc(S["tr_done"], 1)
                pe.wait_ge(S["deg_step"], SUMS + 3)
                pe.wait_ge(S["tr_read"], TR_AT["sums", NR - 1])
                pe.transpose(trp[0:NT, 0, 0:P], inv_deg, ident[0:P, 0:P])
                pe.transpose(trp[0:NT, 1, 0:P], dinv, ident[0:P, 0:P]).then_inc(S["tr_done"], 1)

            run_schedule(piece, stage, None, degrees)
            for t in range(NT):
                r = t // WIDE
                pe.wait_ge(S["outT_ready"], r + 1)
                if t < 2:
                    pe.wait_ge(S["tr_read"], TR_AT["F", 0] - 1)
                else:
                    pe.wait_ge(S["gate_used"], len(GATE_AT) + t - 1)
                for hh in range(2):
                    last = pe.transpose(trp[0:P, t % 2, hh * 128:(hh + 1) * 128], outT[:, hh, t * P:(t + 1) * P], ident[:, :])
                last.then_inc(S["tr_done"], 1)

        @block.vector
        def _(dve):
            links = [0]

            def link(ins):
                links[0] += 1
                ins.then_inc(S["link_s"], 1)
                dve.wait_ge(S["link_s"], links[0])

            dve.memset(B[0][:, :], 0.0).then_inc(S["zeros"], 1)
            dve.memset(ones, 1.0).then_inc(S["ones_ready"], 1)
            dve.memset(eps, EPS)
            dve.memset(brow[:, :], 0.0).then_inc(S["ones_ready"], 1)
            dve.memset(weights3[:, :, 0], 1.0).then_inc(S["prep"], 1)
            dve.memset(attr[0][:, :, EA], 1.0).then_inc(S["prep"], 1)
            dve.memset(attr[1][:, :, EA], 1.0).then_inc(S["prep"], 1)
            dve.wait_ge(S["edges_in"], 64)
            dve.tensor_copy(src_f, src_i).then_inc(S["prep"], 1)
            dve.tensor_copy(dst_f, dst_i).then_inc(S["prep"], 1)
            dve.tensor_copy(weights3[:, :, 1], w_e1).then_inc(S["prep"], 1)
            dve.tensor_copy(weights3[:, :, 2], w_e2).then_inc(S["prep"], 1)
            dve.wait_ge(S["prep"], 7)
            dve.scalar_tensor_tensor(out=cell_in, in0=src_f, scalar=float(N), in1=dst_f, op0=ALU.mult, op1=ALU.add).then_inc(S["prep"], 1)
            dve.scalar_tensor_tensor(out=cell_out, in0=dst_f, scalar=float(N), in1=src_f, op0=ALU.mult, op1=ALU.add).then_inc(S["prep"], 1)
            dve.wait_ge(S["prep"], 9)
            dve.wait_ge(S["masks"], 3)
            for d, k, base in ((dump_in, cell_in, N * N), (dump_out, cell_out, N * N), (dump_dst, dst_f, N)):
                dve.tensor_scalar(d, k, -1.0, float(base), ALU.mult, ALU.add).then_inc(S["prep"], 1)
            dve.wait_ge(S["prep"], 12)
            for d in (dump_in, dump_out, dump_dst):
                dve.tensor_scalar(d, d, own, None, ALU.add).then_inc(S["prep"], 1)
            dve.wait_ge(S["prep"], 15)
            over = lambda v: v.unsqueeze(1).to_broadcast([P, NT, D])
            dve.wait_ge(S["out_done"], 1)
            link(dve.tensor_scalar(mean_b, outp(0)[:, 0:D], 1.0 / N, None, ALU.mult))
            link(dve.tensor_tensor(Bn[2], Xn, over(mean_b), ALU.subtract))
            dve.wait_ge(S["tr_done"], 3 * LAYERS)
            dve.tensor_tensor(Bn[1], Bn[2], Bn[2], ALU.mult).then_inc(S["ones_ready"], 1)
            dve.wait_ge(S["out_done"], 2)
            dve.tensor_scalar(var_b, outp(1)[:, 0:D], 1.0 / N, None, ALU.mult).then_inc(S["stat"], 1)
            dve.wait_ge(S["stat"], 2)
            link(dve.reciprocal(mean_b, var_b))
            link(dve.tensor_tensor(mean_b, mean_b, gamma_b, ALU.mult))
            link(dve.tensor_tensor(Bn[2], Bn[2], over(mean_b), ALU.mult))
            dve.tensor_tensor(Bn[2], Bn[2], over(beta_b), ALU.add).then_inc(S["stat"], 1)
            dve.wait_ge(S["stat"], 3)
            dve.memset(go_in, 0.0).then_inc(S["edges_ready"], 1)
            K = 7

            def chunk(c, h, first):
                now = bass.ds(EC * c, EC)
                dve.wait_ge(S["cell_T"], c + 1)
                if h or not first:
                    dve.wait_ge(S["sums_done"], c)
                own_ = lambda v: v[:, now].rearrange("p (b k) -> p b k", b=2).unsqueeze(3).to_broadcast([P, 2, 4, P])
                r4 = lambda v: v.rearrange("p (b k) n -> p b k n", b=2)
                dve.tensor_tensor(r4(same_cell), cellT, own_(cell_in), ALU.is_equal).then_inc(S["eq_step"], 1)
                dve.tensor_tensor(r4(same_dst), dstT, own_(dst_f), ALU.is_equal).then_inc(S["eq_ready"], 1)
                low = lower.unsqueeze(1).to_broadcast([P, EC, P])
                dve.wait_ge(S["eq_step"], c * K + 1)
                dve.tensor_tensor(before, same_cell, low, ALU.mult).then_inc(S["eq_step"], 1)
                dve.wait_ge(S["eq_step"], c * K + 2)
                dve.tensor_reduce(n_cell, before, AX.X, ALU.add).then_inc(S["eq_step"], 1)
                dve.wait_ge(S["eq_step"], c * K + 3)
                dve.wait_ge(S["eq_ready"], c + 1)
                dve.tensor_tensor(before, same_dst, low, ALU.mult).then_inc(S["eq_step"], 1)
                dve.wait_ge(S["eq_step"], c * K + 4)
                dve.tensor_reduce(n_dst, before, AX.X, ALU.add).then_inc(S["eq_step"], 1)
                dve.wait_ge(S["eq_step"], c * K + 5)
                dve.scalar_tensor_tensor(out=go_in, in0=n_cell, scalar=1.0, in1=dump_in[:, now], op0=ALU.min, op1=ALU.mult)
                dve.scalar_tensor_tensor(out=go_out, in0=n_cell, scalar=1.0, in1=dump_out[:, now], op0=ALU.min, op1=ALU.mult).then_inc(S["eq_step"], 1)
                dve.scalar_tensor_tensor(out=go_dst, in0=n_dst, scalar=1.0, in1=dump_dst[:, now], op0=ALU.min, op1=ALU.mult).then_inc(S["eq_step"], 1)
                dve.wait_ge(S["eq_step"], c * K + 7)
                if not first:
                    dve.wait_ge(S["in_done"], (c - 1) * (16 * EC))
                    dve.wait_ge(S["out_sc_done"], (c - 1) * (16 * EC))
                dve.tensor_tensor(at_in[h], go_in, cell_in[:, now], ALU.add).then_inc(S["at_ready"], 1)
                dve.tensor_tensor(at_out[h], go_out, cell_out[:, now], ALU.add).then_inc(S["at_ready"], 1)
                dve.tensor_tensor(at_sum[:, now], go_dst, dst_f[:, now], ALU.add).then_inc(S["at_ready"], 1)
                dve.wait_ge(S["at_ready"], c * 3 + 3)
            for h in range(2):
                chunk(h, h, True)
            with dve.Fori(1, CH // 2) as i:
                for h in range(2):
                    chunk(i * 2 + h, h, False)

            def finish(m):
                p, r, what = STEPS[m]
                w = RANGES[r][1] * P
                dve.wait_ge(S["piece_used"], (m + 1) * PIECES)
                if m >= 2:
                    p2, r2, _ = STEPS[m - 2]
                    if p2 == 0:
                        if r2 < r or p != 0:
                            dve.wait_ge(S["out_done"], OUT_AT[0, r2, "O", RANGES[r2][1] - 1])
                    elif p2 < 6:
                        dve.wait_ge(S["out_done"], OUT_AT[p2, r2, OUTS[p2][-1], RANGES[r2][1] - 1])
                    else:
                        dve.wait_ge(S["agr_ready"], AGR_AT[p2, r2])
                if p == 0:
                    dve.tensor_copy(agg[:, m % 2, :, 0:w], acc(m)[:, :, 0:w]).then_inc(S["agg_ready"], 1)
                else:
                    dve.wait_ge(rows_in[m % 2], ROW_AT[m])
                    dve.tensor_tensor(agg[:, m % 2, :, 0:w], acc(m)[:, :, 0:w],
                                      scale_row(m, w).unsqueeze(1).to_broadcast([128, 2, w]), ALU.mult).then_inc(S["agg_ready"], 1)

            def stage(p, r, s):
                t0, nt = RANGES[r]
                if s == "O" and p in (0, 3, 5):
                    for k in range(nt):
                        t = t0 + k
                        dve.wait_ge(S["gates"], GATE_AT[p, r, k])
                        g, n = gate[0:P, k % 2, 0:D], gate[0:P, k % 2, D:2 * D]
                        if p == 0:
                            h = Bn[2][:, t]
                            link(dve.tensor_tensor(h, h, n, ALU.subtract))
                            link(dve.tensor_tensor(h, h, g, ALU.mult))
                            dve.tensor_tensor(h, h, n, ALU.add).then_inc(S["gate_used"], 1)
                            dve.wait_ge(S["gate_used"], GATE_AT[p, r, k])
                            link(dve.tensor_tensor(Xn[:, t], Xn[:, t], h, ALU.add))
                        else:
                            dve.tensor_tensor(Xn[:, t], Xn[:, t], g, ALU.add).then_inc(S["gate_used"], 1)
                            dve.wait_ge(S["gate_used"], GATE_AT[p, r, k])
                        link(dve.bn_stats(bn6[:, k], Xn[:, t]))
                        last = dve.bn_aggr(mv[:, k], bn6[:, k])
                        if k == nt - 1:
                            last.then_inc(S["mv_ready"], 1)
                if s == "N" and p in (0, 3, 5):
                    dve.wait_ge(S["std_ready"], NORM_AT[p, r])
                    link(dve.reciprocal(rstd[:, 0:nt], std[:, 0:nt]))
                    for k in range(nt):
                        last = dve.tensor_scalar(Xn[:, t0 + k], Xn[:, t0 + k], mv[:, k, 0:1], rstd[:, k:k + 1], ALU.subtract, ALU.mult)
                    last.then_inc(S["norm_ready"], 1)
                if s == "A" and p == 6:
                    w = nt * P
                    dve.wait_ge(S["agr_ready"], AGR_AT[p, r])
                    for hh in range(2):
                        link(dve.bn_stats(st6[:, hh, r], outT[:, hh, t0 * P:t0 * P + w]))

            def degrees():
                dve.wait_ge(S["tab_in"], 16 * SUMS)
                for q in range(1, SUMS):
                    dve.tensor_tensor(tab[0], tab[0], tab[q], ALU.add).then_inc(S["deg_step"], 1)
                    dve.wait_ge(S["deg_step"], q)
                dve.tensor_copy(deg, tab[0][:, :, EA]).then_inc(S["deg_step"], 1)
                dve.wait_ge(S["deg_step"], SUMS)
                dve.tensor_scalar(inv_deg, deg, 1.0, None, ALU.max).then_inc(S["deg_step"], 1)
                dve.wait_ge(S["deg_step"], SUMS + 1)
                dve.reciprocal(inv_deg, inv_deg).then_inc(S["deg_step"], 1)
                dve.wait_ge(S["stat"], 4)
                dve.reciprocal(dinv, root).then_inc(S["deg_step"], 1)
                dve.wait_ge(S["tr_done"], TR_AT["deg"])
                dve.tensor_copy(degT_s[:, :, 0:P], trp[0:NT, 0:2, 0:P]).then_inc(S["tr_read"], 1)
                dve.wait_ge(S["tr_read"], TR_AT["deg"])
            run_schedule(None, stage, finish, degrees)

            for hh in range(2):
                last = dve.bn_aggr(mv3[:, hh], st6[:, hh].rearrange("p r c -> p (r c)"))
            last.then_inc(S["fin_ready"], 1)
            dve.wait_ge(S["fin_ready"], 2)
            link(dve.reciprocal(scale3, std3))
            link(dve.tensor_tensor(scale3, scale3, c_gamma, ALU.mult))
            link(dve.tensor_tensor(shift3, mv3[:, :, 0], scale3, ALU.mult))
            dve.tensor_tensor(shift3, c_beta, shift3, ALU.subtract).then_inc(S["fin_ready"], 1)
            for r, (t0, nt) in enumerate(RANGES):
                for k in range(nt):
                    t = t0 + k
                    dve.wait_ge(S["tr_done"], TR_AT["F", t])
                    dve.tensor_tensor(Xn[:, t], Xn[:, t], trp[0:P, t % 2, 0:D], ALU.add).then_inc(S["gate_used"], 1)
                    dve.wait_ge(S["gate_used"], len(GATE_AT) + t + 1)
                    link(dve.bn_stats(bn6[:, k], Xn[:, t]))
                    last = dve.bn_aggr(mv[:, k], bn6[:, k])
                last.then_inc(S["mv_ready"], 1)
                dve.wait_ge(S["std_ready"], len(NORM) + r + 1)
                link(dve.reciprocal(rstd[:, 0:nt], std[:, 0:nt]))
                for k in range(nt):
                    dve.tensor_scalar(Xn[:, t0 + k], Xn[:, t0 + k], mv[:, k, 0:1], rstd[:, k:k + 1], ALU.subtract, ALU.mult).then_inc(S["norm_ready"], 1)


_INS = ['x', 'src', 'dst', 'edge_attr_64', 'edge_weight', 'edge_weight_n2', 'L0_gnn_gamma', 'L0_gnn_beta', 'L0_gnn_W_in',
        'L0_gnn_b_in', 'L0_gnn_W_out', 'L0_gnn_b_out', 'L0_gnn_W_x2i', 'L0_gnn_b_x2i', 'L0_gnn_W_h2h', 'L1_gnn_Wl',
        'L1_gnn_bl', 'L1_gnn_Wr', 'L1_gnn_We', 'L1_gnn_be', 'L2_gnn_W_pre', 'L2_gnn_b_pre', 'L2_gnn_W1', 'L2_gnn_b1',
        'L2_gnn_W2', 'L2_gnn_b2', 'L2_gnn_W_post', 'L2_gnn_b_post', 'L3_gnn_W', 'L3_gnn_b', 'L3_gnn_gamma', 'L3_gnn_beta']


def kernel(**inputs):
    import numpy as _np
    import concourse.bacc as _bacc
    from concourse import mybir as _mybir
    from concourse.bass_utils import run_bass_kernel_spmd as _run

    nc = _bacc.Bacc("TRN2", target_bir_lowering=False, num_devices=1)
    arrays, args = {}, []
    for name in _INS:
        a = _np.ascontiguousarray(inputs[name])
        arrays[f"in_{name}"] = a
        args.append(nc.dram_tensor(f"in_{name}", a.shape, _mybir.dt.from_np(a.dtype), kind="ExternalInput").ap())
    out = nc.dram_tensor("out_0", arrays["in_x"].shape, F32, kind="ExternalOutput").ap()
    build_gnn(nc, *args, out)
    r = _run(nc, [arrays], core_ids=[0])
    return r.results[0]["out_0"]
```

```python
from contextlib import ExitStack

import concourse.bass as bass
from concourse import mybir

F32 = mybir.dt.float32
F16 = mybir.dt.float16
BF16 = mybir.dt.bfloat16
I32 = mybir.dt.int32
U32 = mybir.dt.uint32
ALU = mybir.AluOpType
ACT = mybir.ActivationFunctionType
AX = mybir.AxisListType

P = 125
EPS = 1e-5
WIDE = 4
EC = 8
QUAD = 4
PIECES = 5
SUMS = 4
EXACT = 2048


def places(events):
    return {e: n + 1 for n, e in enumerate(events)}


def build_gnn(nc, x, src, dst, edge_attr, edge_w, edge_w2, gamma0, beta0, W_in, b_in, W_out, b_out, W_x2i, b_x2i,
              W_h2h, Wl, bl, Wr, We, be, W_pre, b_pre, W1, b1, W2, b2, W_post, b_post, W3, b3, gamma3, beta3, out):
    N, D = x.shape
    NT = N // P
    E, EA = edge_attr.shape
    ET = E // P
    CH = ET // EC
    AW = EA + 1
    COLS = WIDE * P
    LAYERS = Wl.shape[0]
    HALVES = D // 128
    RANGES = [(r * WIDE, min(WIDE, NT - r * WIDE)) for r in range(-(-NT // WIDE))]
    NR = len(RANGES)
    ROWS = NT // PIECES
    ZERO, REPEAT = 1000, 6
    SLAB = 128 * ZERO * REPEAT

    CELLS = -(-(N * N + QUAD * P) // SLAB) * SLAB
    in_mat = nc.dram_tensor("in_mat", [CELLS, 2], F32, kind="Internal").ap()
    out_mat = nc.dram_tensor("out_mat", [CELLS, 1], F32, kind="Internal").ap()
    count_mat = nc.dram_tensor("count_mat", [N, N], F16, kind="Internal").ap()
    sum_tab = [nc.dram_tensor(f"sum_tab{q}", [N + P, AW], F32, kind="Internal").ap() for q in range(SUMS)]
    attr_val = nc.dram_tensor("attr_val", [P, ET * AW], F32, kind="Internal").ap()
    sums_T = nc.dram_tensor("sums_T", [AW, N], F32, kind="Internal").ap()
    deg_rows = nc.dram_tensor("deg_rows", [2, N], F32, kind="Internal").ap()

    STEPS = [(0, r, m) for r in range(NR) for m in ("in", "out")] + [(p, r, "count") for p in range(1, 7) for r in range(NR)]
    LAST_OF = {}
    for m, (p, r, _) in enumerate(STEPS):
        LAST_OF[p, r] = m
    EPI = [(p, r) for p in range(7) for r in range(NR)]
    OUTS = {0: ["O"], 1: ["O"], 2: ["O"], 3: ["O", "O2"], 4: ["O"], 5: ["O", "O2"], 6: []}
    TRS = {0: ["T"], 1: ["T"], 2: ["T"], 3: ["T", "T2", "H"], 4: [], 5: ["T2"], 6: []}
    AT = 3
    TR_AT = places(["w%d" % i for i in range(2 * LAYERS + LAYERS)] + [("feat", t) for t in range(NT)]
                   + [(0, r, "T") for r in range(NR)] + [("sums", r) for r in range(NR)] + ["deg", "most"]
                   + [e for q in range(1, 7) for e in ([("M", q, 0), ("M", q, 1)] if q > 1 else [])
                      + [(p, r, s) for p, r in EPI if p == q for s in TRS[p]]] + [("F", t) for t in range(NT)])
    OUT_AT = places(["mean", "var"] + [("feat", t) for t in range(NT)]
                    + [(p, r, s, k) for p, r in EPI for s in OUTS[p] for k in range(RANGES[r][1])])
    NORM = [(p, r) for p, r in EPI if p in (0, 3, 5)]
    GATE_AT = places([(p, r, k) for p, r in NORM for k in range(RANGES[r][1])])
    NORM_AT = places(NORM + [("F", t) for t in range(NT)])
    NAT_AT = places([("feat", t) for t in range(NT)]
                    + [(p, r, k) for p, r in EPI if 1 <= p <= 5 for k in range(RANGES[r][1])])
    AGR_AT = places([(p, r) for p, r in EPI if p >= 4])
    LOAD = {}
    for wide in (False, True):
        landed = [0] * PIECES
        for m, (p, _, _) in enumerate(STEPS):
            for j in range(PIECES):
                n = m * PIECES + j
                s = n % 2 if p == 0 or wide else j
                landed[s] += 16
                LOAD[wide, m, j] = (s, landed[s])
    ROW_AT = {}
    rows_landed = [0, 0]
    for m, (p, _, _) in enumerate(STEPS):
        if p:
            rows_landed[m % 2] += 32 if p <= LAYERS else 16
            ROW_AT[m] = rows_landed[m % 2]

    with ExitStack() as ctx:
        def sb(name, shape, dt=F32):
            return ctx.enter_context(nc.sbuf_tensor(name, shape, dt))

        def sem(name):
            return ctx.enter_context(nc.semaphore(name))

        psum = ctx.enter_context(nc.psum_tensor("psum", [128, 8, 512], F32))
        X = sb("X", [128, NT * D])
        B = [sb(f"B{i}", [128, NT * D]) for i in range(3)]
        ring = sb("ring", [128, 5 * ROWS * COLS])
        agg = sb("agg", [128, 2, 2, COLS])
        xT = sb("xT", [128, 2, COLS])
        rowbuf = sb("rowbuf", [128, 4 * COLS])
        wl0 = sb("wl0", [128, 8 * 512])
        wl1 = sb("wl1", [128, LAYERS * 4 * D])
        wE = sb("wE", [AW, LAYERS * D])
        brow = sb("brow", [6, 2 * D])
        ident = sb("ident", [128, 128])
        ident16 = sb("ident16", [128, 128], F16)
        gate = sb("gate", [128, 2, 512])
        cols = sb("cols", [128, 6, 2])
        small = sb("small", [128, 320])

        nat = lambda t_: t_[0:P, :].rearrange("p (t f) -> p t f", t=NT)
        Xn, Bn = nat(X), [nat(b) for b in B]
        K = 7
        parts = B[2][0:P, :].bitcast(F16).rearrange("p (c t f) -> p c t f", c=2, t=NT)
        outT = B[1][:, 0:2 * N].rearrange("p (h n) -> p h n", h=2)
        w3 = lambda t_, a, k, n: t_[:, a:a + k * n].rearrange("p (k n) -> p k n", k=k)
        w_io = w3(wl0, 0, 2, 512)
        w_x2i = w3(wl0, 1024, 4, 512)
        w_h2h = w3(wl0, 3072, 2, 512)
        w_pre, w_1, w_2, w_post = (w3(wl0, i * 512, 2, D) for i in range(4))
        w_3 = w3(wl0, 2048, 2, D)
        w_lT = [w3(wl1, (2 * l) * 512, 2, D) for l in range(LAYERS)]
        w_rT = [w3(wl1, (2 * l + 1) * 512, 2, D) for l in range(LAYERS)]
        bias_row = {"io": 0, "x2i": 1, 0: 2, 1: 3, 2: 4, "post": 5}
        c_pre, c_1, c_2, c_3, c_gamma, c_beta = (cols[:, i, :] for i in range(6))
        so = [0]

        def tiny(n, parts=P):
            so[0] += n
            return small[0:parts, so[0] - n:so[0]]
        mv = tiny(2 * WIDE).rearrange("p (k c) -> p k c", c=2)
        bn6 = tiny(6 * WIDE).rearrange("p (k c) -> p k c", c=6)
        std, rstd = tiny(WIDE), tiny(WIDE)
        eps = tiny(1, 128)
        deg, inv_deg, root, dinv = tiny(NT), tiny(NT), tiny(NT), tiny(NT)
        st6 = tiny(2 * NR * 6, 128).rearrange("p (h r c) -> p h r c", h=2, c=6)
        top = tiny(2 * NR)
        low_, most, top1 = tiny(1), tiny(1), tiny(1)
        scale, unscale, power, unused = tiny(1, 128), tiny(1, 128), tiny(1, 128), tiny(1, 128)
        flag = tiny(1).bitcast(I32)
        at_sum_now = [tiny(EC).bitcast(U32) for _ in range(2)]
        mv3 = gate[:, 0, 0:4].rearrange("p (h c) -> p h c", c=2)
        std3, scale3, shift3 = gate[:, 0, 4:6], gate[:, 0, 6:8], gate[:, 0, 8:10]

        acc = lambda m: psum[:, 2 * (m % 2):2 * (m % 2) + 2, 0:COLS]
        trp = psum[:, 4:6, 0:512]
        outp = lambda n: psum[0:P, 6 + n % 2, :]

        ro = [0]

        def carve(n):
            ro[0] += n
            return ring[0:P, ro[0] - n:ro[0]]
        by_tile = lambda a: a.rearrange("p (k n) -> p k n", k=EC)
        src_i, dst_i = carve(ET).bitcast(I32), carve(ET).bitcast(I32)
        weights = carve(5 * ET).bitcast(BF16).rearrange("p (t c) -> p t c", c=10)
        src_f, dst_f, cell_in, cell_out, dump_in, dump_out, dump_dst = (carve(ET) for _ in range(7))
        cell_b, dst_b, same_dst = (by_tile(carve(EC * P)) for _ in range(3))
        before_cell, before_dst = (by_tile(carve(EC * P // 2).bitcast(BF16)) for _ in range(2))
        attr = [by_tile(carve(EC * AW)) for _ in range(2)]
        val_attr = [carve(EC * AW) for _ in range(2)]
        val_in = [by_tile(carve(EC * 2)) for _ in range(2)]
        val_out = [carve(EC) for _ in range(2)]
        at_in = [carve(EC).bitcast(U32) for _ in range(2)]
        at_out = [carve(EC).bitcast(U32) for _ in range(2)]
        go_in, go_out, go_dst, own = carve(EC), carve(EC), carve(EC), carve(1)
        upper = carve(P // 2 + 1).bitcast(BF16)[:, 0:P]
        upper_f = xT[0:P, 0, 0:P]
        same_cell = agg[0:P].rearrange("p a b n -> p (a b n)")[:, 0:EC * QUAD * P // 2].bitcast(BF16).rearrange("p (k j n) -> p k j n", j=QUAD, n=P)
        w_e1, w_e2 = gate[0:P, 0, 0:ET], gate[0:P, 1, 0:ET]
        sc_val = [rowbuf[0:P, h * EC * AW:(h + 1) * EC * AW] for h in range(2)]
        zero_block = rowbuf[:, 0:ZERO]
        at_sum = rowbuf[0:P, 2 * EC * AW:2 * EC * AW + ET].bitcast(U32)
        scale_row = lambda m, w: rowbuf[:, (m % 2) * COLS:(m % 2) * COLS + w]
        sums_row = lambda m, w: rowbuf[0:AW, (2 + m % 2) * COLS:(2 + m % 2) * COLS + w]
        cellT = psum[0:P, 0:2, 0:4 * P].rearrange("p b (k n) -> p b k n", k=4)
        dstT = psum[0:P, 2:4, 0:4 * P].rearrange("p b (k n) -> p b k n", k=4)
        sum_attr = psum[0:P, 4:6, 0:4 * AW].rearrange("p b (k n) -> p b k n", k=4)
        sum_w = [psum[0:P, 6 + h, 0:10 * EC].rearrange("p (k n) -> p k n", k=EC) for h in range(2)]
        n_dst = [psum[0:P, 6 + h, 10 * EC:11 * EC] for h in range(2)]
        raw_l = B[1][:, 0:LAYERS * 512].rearrange("p (l h n) -> p l h n", l=LAYERS, h=2)
        raw_r = B[1][:, LAYERS * 512:2 * LAYERS * 512].rearrange("p (l h n) -> p l h n", l=LAYERS, h=2)
        raw_e = B[1][:, 2 * LAYERS * 512:2 * LAYERS * 512 + LAYERS * 2 * EA].rearrange("p (l h n) -> p l h n", l=LAYERS, h=2)
        ones = agg[0:P, 0, 0, 0:P]
        gamma_b, beta_b, mean_b, var_b = agg[0:P, 1, 0, 0:D], agg[0:P, 1, 1, 0:D], agg[0:P, 0, 1, 0:D], agg[0:P, 0, 0, 128:128 + D]
        hT = lambda t: xT[:, t % 2, 0:2 * P].rearrange("p (h n) -> p h n", h=2)
        tab = [ring[0:P, q * NT * AW:(q + 1) * NT * AW].rearrange("p (t a) -> p t a", a=AW) for q in range(SUMS)]
        sumsT_s = ring[0:AW, SUMS * NT * AW:SUMS * NT * AW + N]
        degT_s = B[0][0:NT, 0:2 * 128].rearrange("p (c n) -> p c n", c=2)
        count_s = ring[0:P, 4 * ROWS * COLS:5 * ROWS * COLS].bitcast(F16).rearrange("p (c t n) -> p c t n", c=2, t=ROWS)
        top_count = small[0:P, 320 - NR * PIECES:320]
        wE_s = gate[0:AW, 0, 256:512]

        def slot(m, j, wide=False):
            p, r, what = STEPS[m]
            s, w = LOAD[wide, m, j][0], RANGES[r][1] * P
            if what == "in" or wide:
                a = ring[0:P, s * 2 * ROWS * COLS:s * 2 * ROWS * COLS + 2 * ROWS * w]
                return a.rearrange("p (t n c) -> p t n c", t=ROWS, c=2)
            if p == 0:
                base = s * 2 * ROWS * COLS
                return ring[0:P, base:base + ROWS * w].rearrange("p (t n) -> p t n", t=ROWS)
            base = s * ROWS * COLS
            return ring[0:P, base:base + ROWS * COLS].bitcast(F16)[:, 0:ROWS * w].rearrange("p (t n) -> p t n", t=ROWS)

        names = ("zeros zero_in zero_out edges_in x_in w_in raw_in row_in mask_step masks prep edges_ready bcast cell_T eq_ready "
                 "sums_done vals_ready at_ready eq_step in_done out_sc_done sc_at w2_in link_s tr_done tr_read "
                 "out_done out_read agg_ready piece_used gates gate_used nat_ready agr_ready mv_ready std_ready norm_ready ident16_ready "
                 "ones_ready stat count_copied tab_in deg_step deg_rows_out outT_ready fin_ready y_stored "
                 "zero_sum ocol count_max flag_ready split_hi split_lo scale_ready wE_ready max_ready w_step").split()
        S = {n: sem(n) for n in names}
        count_stored = [sem(f"count_stored{h}") for h in range(2)]
        attr_stored = [sem(f"attr_stored{h}") for h in range(2)]
        attr_in = [sem(f"attr_in{h}") for h in range(2)]
        sc_in = [sem(f"sc_in{h}") for h in range(2)]
        sc_done = [sem(f"sc_done{q}") for q in range(SUMS)]
        load_in = [sem(f"load_in{s}") for s in range(PIECES)]
        rows_in = [sem(f"rows_in{s}") for s in range(2)]
        edge_attr_v = edge_attr.rearrange("(p t) a -> p t a", p=P)
        in_v = in_mat[0:N * N, :].rearrange("(t p d) c -> p t (d c)", p=P, d=N)
        out_v = out_mat[0:N * N, :].rearrange("(t p d) c -> p t (d c)", p=P, d=N)
        count_v = count_mat.rearrange("(t p) d -> p t d", p=P)
        wv = lambda w: w.rearrange("(k p) n -> p k n", p=128)

        def run_schedule(eng, piece, stage, finish=None, degrees=None, begin=None, end=None):
            def steps(passes, wide):
                before_ = None
                for m, (p, r, what) in enumerate(STEPS):
                    if p not in passes:
                        continue
                    if p and r == 0 and begin:
                        begin(p, wide)
                    for j in range(PIECES):
                        if piece:
                            piece(m, j, wide)
                        if before_:
                            for s in {0: ("A", "T"), 1: ("O",), 2: ("N",), 3: ("T2",)}.get(j, ()):
                                stage(*before_, s, wide)
                    if finish:
                        finish(m)
                    if before_:
                        for s in ("H", "O2", "X"):
                            stage(*before_, s, wide)
                    before_ = (p, r) if m == LAST_OF[p, r] else None
                    if before_ and r == NR - 1:
                        for s in ("A", "T", "O", "N", "T2", "H", "O2", "X"):
                            stage(*before_, s, wide)
                        before_ = None

            steps((0,), False)
            if degrees:
                degrees()
            eng.wait_ge(S["flag_ready"], 1)
            largest = eng.value_load(flag[0:1, 0:1], min_val=0, max_val=E)
            with eng.If(largest < EXACT):
                steps(range(1, 7), False)
                if end:
                    end(False)
            with eng.Else():
                steps(range(1, 7), True)
                if end:
                    end(True)

        SRC = {1: Xn, 2: Bn[0], 3: Bn[1], 4: Bn[0], 5: Bn[1], 6: Bn[0]}
        block = ctx.enter_context(nc.Block())
        Z_IN, Z_OUT = 2 * CELLS // SLAB, CELLS // SLAB

        @block.sync
        def _(sp):
            for a, b in ((src_i, src), (dst_i, dst), (w_e1, edge_w), (w_e2, edge_w2)):
                sp.dma_start(a, b.rearrange("(p t) -> p t", p=P)).then_inc(S["edges_in"], 16)
            sp.dma_start(Xn, x.rearrange("(t p) f -> p t f", p=P)).then_inc(S["x_in"], 16)
            sp.dma_start(gamma_b, gamma0.unsqueeze(0).to_broadcast([P, D])).then_inc(S["x_in"], 16)
            sp.dma_start(beta_b, beta0.unsqueeze(0).to_broadcast([P, D])).then_inc(S["x_in"], 16)
            for l in range(LAYERS):
                sp.dma_start(raw_l[:, l], wv(Wl[l])).then_inc(S["raw_in"], 16)
                sp.dma_start(raw_r[:, l], wv(Wr[l])).then_inc(S["raw_in"], 16)
                sp.dma_start(raw_e[:, l], wv(We[l])).then_inc(S["raw_in"], 16)
            for a, w in ((w_io[:, :, 0:D], W_in), (w_io[:, :, D:2 * D], W_out), (w_x2i, W_x2i), (w_h2h, W_h2h)):
                sp.dma_start(a, wv(w)).then_inc(S["w_in"], 16)
            r1 = lambda v: v.unsqueeze(0)
            for a, v in ((brow[0:1, 0:D], b_in), (brow[0:1, D:2 * D], b_out), (brow[1:2, :], b_x2i),
                         (brow[2:3, 0:D], bl[0]), (brow[3:4, 0:D], bl[1]), (brow[4:5, 0:D], bl[2]), (brow[5:6, 0:D], b_post)):
                if a.shape[1] == D and v is b_in:
                    sp.wait_ge(S["ones_ready"], 2)
                sp.dma_start(a, r1(v)).then_inc(S["w_in"], 16)
            sp.dma_start(wE[EA:AW, :], be.rearrange("(a l) d -> a (l d)", a=1)).then_inc(S["w_in"], 16)
            def chunk(c, h, first):
                if not first:
                    sp.wait_ge(S["sums_done"], c - 1)
                sp.dma_start(attr[h][:, :, 0:EA], edge_attr_v[:, bass.ds(EC * c, EC), :]).then_inc(attr_in[h], 16)
            sp.wait_ge(S["prep"], 3)
            for h in range(2):
                chunk(h, h, True)
            with sp.Fori(1, CH // 2) as i:
                for h in range(2):
                    chunk(i * 2 + h, h, False)
            def piece(m, j, wide):
                p, r, what = STEPS[m]
                t0, nt = RANGES[r]
                c0, w = t0 * P, nt * P
                if (m, j) == (0, 0):
                    sp.wait_ge(S["in_done"], 16 * ET)
                    sp.wait_ge(S["out_sc_done"], 16 * ET)
                    for h in range(2):
                        sp.wait_ge(attr_stored[h], 8 * CH)
                if p and j == 0:
                    if m >= 2 and STEPS[m - 2][0] >= 1:
                        sp.wait_ge(S["agg_ready"], m - 1)
                        sp.wait_ge(S["piece_used"], (m - 1) * PIECES)
                    row = 0 if p <= LAYERS else 1
                    sp.dma_start(scale_row(m, w), deg_rows[row:row + 1, c0:c0 + w].to_broadcast([128, w])).then_inc(rows_in[m % 2], 16)
                    if p <= LAYERS:
                        sp.dma_start(sums_row(m, w), sums_T[:, c0:c0 + w]).then_inc(rows_in[m % 2], 16)
                n = m * PIECES + j
                back = 2 if p == 0 or wide else PIECES
                if n >= back and not ((p, r) == (1, 0) and j < back):
                    sp.wait_ge(S["piece_used"], n - back + 1)
                    mm, jj = divmod(n - 2, PIECES)
                    if p == 0 and STEPS[mm][2] == "in":
                        sp.wait_ge(S["count_copied"], (mm // 2) * PIECES + jj + 1)
                both = what == "in" or wide
                view = in_v if both else {"out": out_v, "count": count_v}[what]
                to = slot(m, j, wide)
                if both:
                    to, c0, w = to.rearrange("p t n c -> p t (n c)"), 2 * c0, 2 * w
                sp.dma_start(to, view[:, j * ROWS:(j + 1) * ROWS, c0:c0 + w]).then_inc(load_in[LOAD[wide, m, j][0]], 16)

            def degrees():
                for c in range(2):
                    sp.wait_ge(count_stored[c], 16 * ((NR * PIECES + 1 - c) // 2))
                for q in range(SUMS):
                    sp.wait_ge(sc_done[q], 16 * ET // SUMS)
                sp.wait_ge(S["piece_used"], 2 * NR * PIECES)
                for q in range(SUMS):
                    sp.dma_start(tab[q], sum_tab[q][0:N, :].rearrange("(t p) a -> p t a", p=P)).then_inc(S["tab_in"], 16)
                sp.wait_ge(S["tr_read"], TR_AT["deg"])
                sp.dma_start(sums_T, sumsT_s).then_inc(S["deg_rows_out"], 16)
                for c in range(2):
                    sp.dma_start(deg_rows[c].rearrange("(t p) -> t p", p=P), degT_s[:, c, 0:P]).then_inc(S["deg_rows_out"], 16)
                sp.wait_ge(S["deg_rows_out"], 48)
                sp.wait_ge(S["out_done"], OUT_AT[0, NR - 1, "O", RANGES[-1][1] - 1])
                for a, wt in ((w_pre, W_pre), (w_1, W1), (w_2, W2), (w_post, W_post), (w_3, W3)):
                    sp.dma_start(a, wv(wt)).then_inc(S["w2_in"], 16)

            def end(wide):
                for t in range(NT):
                    sp.wait_ge(S["norm_ready"], NORM_AT["F", t])
                    sp.dma_start(out[t * P:(t + 1) * P, :], Xn[:, t]).then_inc(S["y_stored"], 16)
                sp.wait_ge(S["y_stored"], 16 * NT)

            run_schedule(sp, piece, lambda *_: None, degrees=degrees, end=end)

        @block.gpsimd
        def _(pool):
            pool.memset(ident[:, :], 0.0).then_inc(S["mask_step"], 1)
            pool.memset(upper_f, 1.0).then_inc(S["mask_step"], 1)
            pool.iota(own, pattern=[[0, 1]], base=0, channel_multiplier=1, allow_small_or_imprecise_dtypes=True).then_inc(S["masks"], 1)
            pool.wait_ge(S["mask_step"], 2)
            pool.affine_select(out=ident[:, :], in_=ident[:, :], compare_op=ALU.not_equal, fill=1.0,
                               base=0, pattern=[[-1, 128]], channel_multiplier=1).then_inc(S["masks"], 1)
            pool.affine_select(out=upper_f, in_=upper_f, compare_op=ALU.is_gt, fill=0.0,
                               base=0, pattern=[[1, P]], channel_multiplier=-1).then_inc(S["masks"], 1)
            pool.wait_ge(S["masks"], 3)
            pool.tensor_copy(upper, upper_f).then_inc(S["ident16_ready"], 1)
            pool.tensor_copy(ident16[:, :], ident[:, :]).then_inc(S["ident16_ready"], 1)
            pool.wait_ge(S["zero_in"], 16 * Z_IN)
            pool.wait_ge(S["zero_out"], 16 * Z_OUT)

            def chunk(c, h, first):
                turn = pool.to_reg(c * 5 + 5)
                done = [pool.to_reg(c * (16 * EC) + 16 * k) for k in range(0, EC, QUAD)]
                pool.wait_ge(S["masks"], 3)
                pool.wait_ge(S["at_ready"], turn)
                for quad in range(EC // QUAD):
                    for s, mat, at, v in (("in_done", in_mat, at_in, val_in[h]),
                                          ("out_sc_done", out_mat, at_out, val_out[h].unsqueeze(2))):
                        if quad or h or not first:
                            pool.wait_ge(S["masks"], 3)
                            pool.wait_ge(S[s], done[quad])
                        for k in range(QUAD * quad, QUAD * quad + QUAD):
                            pool.indirect_dma_start(out=mat, out_offset=bass.IndirectOffsetOnAxis(ap=at[h][:, k:k + 1], axis=0),
                                                    in_=v[:, k], in_offset=None, compute_op=ALU.add).then_inc(S[s], 16)
            for h in range(2):
                chunk(h, h, True)
            with pool.Fori(1, CH // 2) as i:
                for h in range(2):
                    chunk(i * 2 + h, h, False)

            for h in range(2):
                pool.wait_ge(attr_stored[h], 8 * CH)
            pool.wait_ge(S["zero_sum"], 16 * SUMS)
            pool.dma_start(sc_val[0], attr_val[:, 0:EC * AW]).then_inc(sc_in[0], 16)

            def sums(c, h, first, last):
                done = [pool.to_reg(c * (16 * EC // SUMS) + 16 * g) for g in range(EC // SUMS)]
                here, turn = pool.to_reg((c + (2 - h)) * 8), pool.to_reg(c + 1)
                pool.wait_ge(S["masks"], 3)
                pool.wait_ge(sc_in[h], here)
                pool.wait_ge(S["sc_at"], turn)
                for k in range(EC):
                    if k >= SUMS or h or not first:
                        pool.wait_ge(S["masks"], 3)
                        pool.wait_ge(sc_done[k % SUMS], done[k // SUMS])
                    pool.indirect_dma_start(out=sum_tab[k % SUMS],
                                            out_offset=bass.IndirectOffsetOnAxis(ap=at_sum_now[h][:, k:k + 1], axis=0),
                                            in_=sc_val[h][:, k * AW:(k + 1) * AW], in_offset=None,
                                            compute_op=ALU.add).then_inc(sc_done[k % SUMS], 16)
                    if k == SUMS - 1 and not last:
                        pool.dma_start(sc_val[1 - h], attr_val[:, bass.ds((c + 1) * (EC * AW), EC * AW)]).then_inc(sc_in[1 - h], 16)
                        pool.tensor_copy(at_sum_now[1 - h], at_sum[:, bass.ds((c + 1) * EC, EC)]).then_inc(S["sc_at"], 1)
            pool.tensor_copy(at_sum_now[0], at_sum[:, 0:EC]).then_inc(S["sc_at"], 1)
            for h in range(2):
                sums(h, h, True, False)
            with pool.Fori(1, CH // 2 - 1) as i:
                for h in range(2):
                    sums(i * 2 + h, h, False, False)
            for h in range(2):
                sums(CH - 2 + h, h, False, h == 1)

        @block.scalar
        def _(act):
            act.wait_ge(S["zeros"], 1)
            for mat, n, s in ((in_mat, Z_IN, "zero_in"), (out_mat, Z_OUT, "zero_out")):
                flat = mat.rearrange("a b -> (a b)")
                for j in range(n):
                    act.dma_start(flat[j * SLAB:(j + 1) * SLAB].rearrange("(p k a) -> p k a", p=128, k=REPEAT),
                                  zero_block.unsqueeze(1).to_broadcast([128, REPEAT, ZERO])).then_inc(S[s], 16)
            for q in range(SUMS):
                half = (N + P) * AW // P // 2
                act.dma_start(sum_tab[q].rearrange("(p a) b -> p (a b)", p=P).rearrange("p (k a) -> p k a", k=2),
                              zero_block[0:P, 0:half].unsqueeze(1).to_broadcast([P, 2, half])).then_inc(S["zero_sum"], 16)
            for i_, v in enumerate((b_pre, b1, b2, b3, gamma3, beta3)):
                act.dma_start(cols[:, i_, :], v.rearrange("(h p) -> p h", p=128), allow_slow_non_contiguous=True).then_inc(S["ocol"], 16)
            for i_ in range(2 * LAYERS):
                act.wait_ge(S["tr_done"], TR_AT["w%d" % i_])
                wt = (w_lT if i_ < LAYERS else w_rT)[i_ % LAYERS]
                act.activation(wt, trp[:, i_ % 2, :].rearrange("p (k n) -> p k n", k=2), ACT.Copy).then_inc(S["tr_read"], 1)
            for l in range(LAYERS):
                act.wait_ge(S["tr_done"], TR_AT["w%d" % (2 * LAYERS + l)])
                act.activation(wE[0:EA, l * D:(l + 1) * D], trp[0:EA, l % 2, 0:D], ACT.Copy).then_inc(S["tr_read"], 1)
            act.wait_ge(S["stat"], 1)
            act.activation(var_b, var_b, ACT.Sqrt, bias=eps[0:P, :]).then_inc(S["stat"], 1)
            for t in range(NT):
                act.wait_ge(S["tr_done"], TR_AT["feat", t])
                act.activation(hT(t), trp[:, t % 2, 0:2 * P].rearrange("p (h n) -> p h n", h=2), ACT.Copy).then_inc(S["tr_read"], 1)
                act.wait_ge(S["out_done"], OUT_AT["feat", t])
                act.activation(Bn[0][:, t], outp(t)[:, 0:D], ACT.Copy).then_inc(S["nat_ready"], 1)
                act.activation(Bn[1][:, t], outp(t)[:, D:2 * D], ACT.Copy).then_inc(S["out_read"], 1)
            act.wait_ge(S["edges_ready"], 1)

            def spread(c):
                now = bass.ds(EC * c, EC)
                act.activation(cell_b, cell_in[:, now].unsqueeze(2).to_broadcast([P, EC, P]), ACT.Copy).then_inc(S["bcast"], 1)
                act.activation(dst_b, dst_f[:, now].unsqueeze(2).to_broadcast([P, EC, P]), ACT.Copy).then_inc(S["bcast"], 1)

            def chunk(c, h, first, last=False):
                if not last:
                    act.wait_ge(S["cell_T"], c + 1)
                    spread(c + 1)
                act.wait_ge(S["sums_done"], c + 1)
                if not first:
                    act.wait_ge(attr_stored[h], (c - h) * 8)
                act.activation(val_attr[h].rearrange("p (b k n) -> p b k n", b=2, k=4), sum_attr, ACT.Copy).then_inc(S["vals_ready"], 1)
                act.wait_ge(S["vals_ready"], c + 1)
                act.dma_start(attr_val[:, bass.ds(c * (EC * AW), EC * AW)], val_attr[h]).then_inc(attr_stored[h], 16)
            spread(0)
            for h in range(2):
                chunk(h, h, True)
            with act.Fori(1, CH // 2 - 1) as i:
                for h in range(2):
                    chunk(i * 2 + h, h, False)
            for h in range(2):
                chunk(CH - 2 + h, h, False, h == 1)

            def counts(m, j, wide):
                if STEPS[m][2] != "in":
                    return
                q = (m // 2) * PIECES + j
                r = STEPS[m][1]
                w = RANGES[r][1] * P
                s, v = LOAD[wide, m, j]
                act.wait_ge(load_in[s], v)
                if q >= 2:
                    act.wait_ge(count_stored[q % 2], 16 * (q // 2))
                    act.wait_ge(S["count_max"], q - 1)
                act.activation(count_s[:, q % 2, :, 0:w], slot(m, j)[:, :, :, 0], ACT.Copy).then_inc(S["count_copied"], 1)
                act.wait_ge(S["count_copied"], q + 1)
                c0 = RANGES[r][0] * P
                act.dma_start(count_v[:, j * ROWS:(j + 1) * ROWS, c0:c0 + w], count_s[:, q % 2, :, 0:w]).then_inc(count_stored[q % 2], 16)

            def evac_T(p, r, s, to, col=None):
                w = RANGES[r][1] * P
                act.wait_ge(S["tr_done"], TR_AT[p, r, s])
                if col is None:
                    act.activation(to[:, :, 0:w], trp[:, :, 0:w], ACT.Copy).then_inc(S["tr_read"], 1)
                else:
                    act.activation(to[:, 0, 0:w], trp[:, 0, 0:w], ACT.Identity, bias=col[:, 0:1])
                    act.activation(to[:, 1, 0:w], trp[:, 1, 0:w], ACT.Identity, bias=col[:, 1:2]).then_inc(S["tr_read"], 1)

            def stage(p, r, s, wide):
                t0, nt = RANGES[r]
                m = LAST_OF[p, r]
                w = nt * P
                if s == "A" and p in (4, 5):
                    act.wait_ge(S["agg_ready"], m + 1)
                    if (p, r) == (4, 0):
                        act.wait_ge(S["ocol"], 16 * 6)
                    c = c_1 if p == 4 else c_2
                    act.activation(agg[:, m % 2, 0, 0:w], agg[:, m % 2, 0, 0:w], ACT.Relu, bias=c[:, 0:1])
                    act.activation(agg[:, m % 2, 1, 0:w], agg[:, m % 2, 1, 0:w], ACT.Relu, bias=c[:, 1:2]).then_inc(S["agr_ready"], 1)
                if s == "A" and p == 6:
                    act.wait_ge(S["agg_ready"], m + 1)
                    for hh in range(2):
                        last = act.activation(outT[:, hh, t0 * P:t0 * P + w], agg[:, m % 2, hh, 0:w], ACT.Identity, bias=c_3[:, hh:hh + 1])
                    last.then_inc(S["agr_ready"], 1)
                if s == "T" and p <= 3:
                    evac_T(p, r, "T", xT)
                if s == "O" and p <= 5:
                    for k in range(nt):
                        n = OUT_AT[p, r, "O", k]
                        act.wait_ge(S["out_done"], n)
                        o = outp(n)
                        if p in (0, 3, 5):
                            g = GATE_AT[p, r, k]
                            if g > 2:
                                act.wait_ge(S["gate_used"], g - 2)
                        if p == 0:
                            act.activation(gate[0:P, k % 2, 0:D], o[:, 0:D], ACT.Sigmoid)
                            act.activation(gate[0:P, k % 2, D:2 * D], o[:, D:2 * D], ACT.Tanh).then_inc(S["gates"], 1)
                        elif p in (3, 5):
                            act.activation(gate[0:P, k % 2, 0:D], o[:, 0:D], ACT.Relu if p == 3 else ACT.Copy).then_inc(S["gates"], 1)
                        elif p in (1, 2):
                            act.activation(Bn[p - 1][:, t0 + k], o[:, 0:D], ACT.Relu).then_inc(S["nat_ready"], 1)
                        else:
                            act.activation(Bn[1][:, t0 + k], o[:, 0:D], ACT.Copy, scale=dinv[:, t0 + k:t0 + k + 1]).then_inc(S["nat_ready"], 1)
                if s == "N" and p in (0, 3, 5):
                    act.wait_ge(S["mv_ready"], NORM_AT[p, r])
                    act.activation(std[:, 0:nt], mv[:, 0:nt, 1], ACT.Sqrt, bias=eps[0:P, :]).then_inc(S["std_ready"], 1)
                if s == "T2" and p in (3, 5):
                    evac_T(p, r, "T2", xT)
                if s == "H" and p == 3:
                    if r == 0:
                        act.wait_ge(S["ocol"], 16 * 6)
                    evac_T(p, r, "H", agg[:, m % 2], c_pre)
                if s == "O2" and p in (3, 5):
                    for k in range(nt):
                        n = OUT_AT[p, r, "O2", k]
                        act.wait_ge(S["out_done"], n)
                        act.activation(Bn[0][:, t0 + k], outp(n)[:, 0:D], ACT.Copy, scale=dinv[:, t0 + k:t0 + k + 1]).then_inc(S["nat_ready"], 1)

            def degrees():
                for r, (t0, nt) in enumerate(RANGES):
                    act.wait_ge(S["tr_done"], TR_AT["sums", r])
                    act.activation(sumsT_s[:, t0 * P:(t0 + nt) * P], trp[0:AW, r % 2, 0:nt * P], ACT.Copy).then_inc(S["tr_read"], 1)
                act.wait_ge(S["deg_step"], SUMS)
                act.activation(root, deg, ACT.Sqrt, bias=1.0).then_inc(S["stat"], 1)

            def begin(p, wide):
                if wide:
                    return
                if p == 1:
                    act.wait_ge(S["norm_ready"], NORM_AT[0, NR - 1])
                else:
                    act.wait_ge(S["nat_ready"], NAT_AT[p - 1, NR - 1, RANGES[-1][1] - 1])
                act.wait_ge(S["scale_ready"], p)
                act.wait_ge(S["piece_used"], (7 * (p - 1) + 14) * PIECES)
                for j in range(PIECES):
                    now = slice(j * ROWS, (j + 1) * ROWS)
                    act.activation(parts[:, 0, now], SRC[p][:, now], ACT.Copy, scale=scale[0:P, :]).then_inc(S["split_hi"], 1)

            def end(wide):
                finish_layer3()

            def finish_layer3():
                act.wait_ge(S["fin_ready"], 1)
                act.activation(std3, mv3[:, :, 1], ACT.Sqrt, bias=eps).then_inc(S["fin_ready"], 1)
                act.wait_ge(S["fin_ready"], 3)
                for r, (t0, nt) in enumerate(RANGES):
                    for hh in range(2):
                        v = outT[:, hh, t0 * P:(t0 + nt) * P]
                        last = act.activation(v, v, ACT.Relu, bias=shift3[:, hh:hh + 1], scale=scale3[:, hh:hh + 1])
                    last.then_inc(S["outT_ready"], 1)
                for r, (t0, nt) in enumerate(RANGES):
                    act.wait_ge(S["mv_ready"], len(NORM) + r + 1)
                    act.activation(std[:, 0:nt], mv[:, 0:nt, 1], ACT.Sqrt, bias=eps[0:P, :]).then_inc(S["std_ready"], 1)

            run_schedule(act, counts, stage, degrees=degrees, begin=begin, end=end)

        @block.tensor
        def _(pe):
            pe.wait_ge(S["masks"], 3)
            pe.wait_ge(S["ident16_ready"], 2)
            pe.wait_ge(S["raw_in"], 16 * 3 * LAYERS)
            for i_ in range(2 * LAYERS):
                raw = (raw_l if i_ < LAYERS else raw_r)[:, i_ % LAYERS]
                if i_ >= 2:
                    pe.wait_ge(S["tr_read"], i_ - 1)
                for k in range(2):
                    for o in range(2):
                        last = pe.transpose(trp[:, i_ % 2, k * D + o * 128:k * D + (o + 1) * 128], raw[:, o, k * 128:(k + 1) * 128], ident[:, :])
                last.then_inc(S["tr_done"], 1)
            for l in range(LAYERS):
                pe.wait_ge(S["tr_read"], 2 * LAYERS + l - 1)
                for o in range(2):
                    last = pe.transpose(trp[0:EA, l % 2, o * 128:(o + 1) * 128], raw_e[:, l, o, :], ident[:, :])
                last.then_inc(S["tr_done"], 1)
            pe.wait_ge(S["ones_ready"], 1)
            pe.wait_ge(S["x_in"], 48)
            for t in range(NT):
                last = pe.matmul(outp(0)[:, 0:D], ones, Xn[:, t], start=t == 0, stop=t == NT - 1)
            last.then_inc(S["out_done"], 1)
            pe.wait_ge(S["ones_ready"], 3)
            for t in range(NT):
                last = pe.matmul(outp(1)[:, 0:D], ones, Bn[1][:, t], start=t == 0, stop=t == NT - 1)
            last.then_inc(S["out_done"], 1)
            pe.wait_ge(S["stat"], 3)
            pe.wait_ge(S["w_in"], 16 * 12)
            for t in range(NT + 1):
                if t < NT:
                    if t < 2:
                        pe.wait_ge(S["tr_read"], 3 * LAYERS)
                    else:
                        pe.wait_ge(S["tr_read"], TR_AT["feat", t - 2])
                    for hh in range(2):
                        last = pe.transpose(trp[:, t % 2, hh * P:(hh + 1) * P], Bn[2][:, t, hh * 128:(hh + 1) * 128], ident[0:P, 0:P])
                    last.then_inc(S["tr_done"], 1)
                if t:
                    u = t - 1
                    pe.wait_ge(S["tr_read"], TR_AT["feat", u])
                    if u >= 2:
                        pe.wait_ge(S["out_read"], u - 1)
                    for hh in range(2):
                        pe.matmul(outp(u), hT(u)[:, hh], w_io[:, hh], start=hh == 0, stop=False)
                    pe.matmul(outp(u), ident[0:6, 0:1].to_broadcast([6, P]), brow[:, :], start=False, stop=True).then_inc(S["out_done"], 1)

            pe.wait_ge(S["out_read"], NT)
            def chunk(c, h, first):
                pe.wait_ge(S["bcast"], c * 2 + 2)
                if h or not first:
                    pe.wait_ge(S["eq_ready"], c)
                    pe.wait_ge(S["eq_step"], c * K)
                for k in range(EC):
                    pe.transpose(cellT[:, k // 4, k % 4], cell_b[:, k], ident[0:P, 0:P])
                for k in range(EC):
                    last = pe.transpose(dstT[:, k // 4, k % 4], dst_b[:, k], ident[0:P, 0:P])
                last.then_inc(S["cell_T"], 1)
                if not first:
                    pe.wait_ge(S["at_ready"], (c - 1) * 5)
                for a in range(EC):
                    q = a // QUAD * QUAD
                    if a == q:
                        pe.wait_ge(S["eq_step"], c * K + 1 + a // QUAD)
                    for b in range(q, q + QUAD):
                        n = 10 if b < a else 9
                        pe.matmul(sum_w[h][:, a, 0:n], same_cell[:, b, a - q], weights[:, bass.ds(EC * c + b, 1), 0:n],
                                  start=(a == 0 and b == 0), stop=False, skip_group_check=True)
                pe.wait_ge(S["eq_ready"], c + 1)
                pe.wait_ge(attr_in[h], (c + (2 - h)) * 8)
                if h or not first:
                    pe.wait_ge(S["vals_ready"], c)
                for k in range(EC):
                    pe.matmul(sum_attr[:, k // 4, k % 4], same_dst[:, k], attr[h][:, k], start=(k % 4 == 0), stop=True, skip_group_check=True)
                pe.wait_ge(S["eq_step"], c * K + 4)
                for k in range(EC):
                    pe.matmul(sum_w[h][:, k, 9:10], before_cell[:, k], weights[:, 0, 0:1], start=False, stop=True, skip_group_check=True)
                    last = pe.matmul(n_dst[h][:, k:k + 1], before_dst[:, k], weights[:, 0, 0:1], start=False, stop=True, skip_group_check=True)
                last.then_inc(S["sums_done"], 1)
            for h in range(2):
                chunk(h, h, True)
            with pe.Fori(1, CH // 2) as i:
                for h in range(2):
                    chunk(i * 2 + h, h, False)
            pe.wait_ge(S["vals_ready"], CH)
            pe.wait_ge(S["at_ready"], 5 * CH)

            def piece(m, j, wide):
                p, r, what = STEPS[m]
                t0, nt = RANGES[r]
                w = nt * P
                source = (Bn[0] if what == "in" else Bn[1]) if p == 0 else SRC[p]
                if j == 0:
                    if m >= 2:
                        pe.wait_ge(S["agg_ready"], m - 1)
                    if r == 0 and p == 1 and wide:
                        pe.wait_ge(S["norm_ready"], NORM_AT[0, NR - 1])
                    elif r == 0 and p > 1 and wide:
                        pe.wait_ge(S["nat_ready"], NAT_AT[p - 1, NR - 1, RANGES[-1][1] - 1])
                s, v = LOAD[wide, m, j]
                pe.wait_ge(load_in[s], v)
                a = acc(m)
                rhs = slot(m, j, wide)
                if p and r == 0 and not wide:
                    pe.wait_ge(S["split_lo"], (p - 1) * PIECES + j + 1)
                for i_ in range(ROWS):
                    t = j * ROWS + i_
                    for hh in range(2):
                        f = slice(hh * 128, (hh + 1) * 128)
                        if p and not wide:
                            for c in range(2):
                                last = pe.matmul(a[:, hh, 0:w], parts[:, c, t, f], rhs[:, i_, :],
                                                 start=t == 0 and c == 0, stop=t == NT - 1 and c == 1, skip_group_check=True)
                        else:
                            moving = rhs[:, i_, :, 1] if what == "in" else rhs[:, i_, :, 0] if wide else rhs[:, i_, :]
                            last = pe.matmul(a[:, hh, 0:w], source[:, t, f], moving,
                                             start=t == 0, stop=t == NT - 1, skip_group_check=True)
                    if t == NT - 2 and p >= 4:
                        for hh in range(2):
                            for k in range(nt):
                                f = slice(hh * 128, (hh + 1) * 128)
                                for own_rows, one in ([(source[:, t0 + k, f], ident)] if wide else
                                                      [(parts[:, c, t0 + k, f], ident16) for c in range(2)]):
                                    pe.matmul(a[:, hh, k * P:(k + 1) * P], own_rows, one[0:P, 0:P],
                                              start=False, stop=False, skip_group_check=True)
                    if t == NT - 2 and 1 <= p <= LAYERS:
                        pe.wait_ge(rows_in[m % 2], ROW_AT[m])
                        pe.wait_ge(S["wE_ready"], p)
                        for hh in range(2):
                            pe.matmul(a[:, hh, 0:w], wE_s[:, hh * 128:(hh + 1) * 128], sums_row(m, w),
                                      start=False, stop=False, skip_group_check=True)
                last.then_inc(S["piece_used"], 1)

            def transposes(p, r, s, from_):
                t0, nt = RANGES[r]
                pe.wait_ge(S["tr_read"], TR_AT[p, r, s] - 1)
                for hh in range(2):
                    for k in range(nt):
                        last = pe.transpose(trp[:, hh, k * P:(k + 1) * P], from_[:, t0 + k, hh * 128:(hh + 1) * 128], ident[0:P, 0:P])
                last.then_inc(S["tr_done"], 1)

            def stage(p, r, s, wide):
                t0, nt = RANGES[r]
                m = LAST_OF[p, r]
                w = nt * P
                if s == "T" and p <= 3:
                    transposes(p, r, s, Bn[2] if p == 0 else SRC[p])
                if s == "T2" and p in (3, 5):
                    pe.wait_ge(S["norm_ready"], NORM_AT[p, r])
                    transposes(p, r, s, Xn)
                if s == "H" and p == 3:
                    if r == 0:
                        pe.wait_ge(S["w2_in"], 16 * 5)
                    pe.wait_ge(S["tr_read"], TR_AT[p, r, "T2"])
                    for o in range(2):
                        for hh in range(2):
                            last = pe.matmul(trp[:, o, 0:w], w_pre[:, hh, o * 128:(o + 1) * 128], xT[:, hh, 0:w], start=hh == 0, stop=hh == 1)
                    last.then_inc(S["tr_done"], 1)
                if s in OUTS[p]:
                    ag = agg[:, m % 2]
                    bias = None
                    if p == 0:
                        pe.wait_ge(S["agg_ready"], m + 1)
                        pe.wait_ge(S["tr_read"], TR_AT[p, r, "T"])
                        ops = [(agg[:, 0, hh], w_x2i[:, hh]) for hh in range(2)] + [(agg[:, 1, hh], w_x2i[:, 2 + hh]) for hh in range(2)] \
                            + [(xT[:, hh], w_h2h[:, hh]) for hh in range(2)]
                        bias = "x2i"
                    elif p <= 3 and s == "O":
                        pe.wait_ge(S["agg_ready"], m + 1)
                        pe.wait_ge(S["tr_read"], TR_AT[p, r, "T"])
                        ops = [(ag[:, hh], w_lT[p - 1][:, hh]) for hh in range(2)] + [(xT[:, hh], w_rT[p - 1][:, hh]) for hh in range(2)]
                        bias = p - 1
                    elif p == 3:
                        pe.wait_ge(S["tr_read"], TR_AT[p, r, "H"])
                        ops = [(ag[:, hh], w_1[:, hh]) for hh in range(2)]
                    elif p == 4:
                        pe.wait_ge(S["agr_ready"], AGR_AT[p, r])
                        ops = [(ag[:, hh], w_2[:, hh]) for hh in range(2)]
                    elif s == "O":
                        pe.wait_ge(S["agr_ready"], AGR_AT[p, r])
                        ops = [(ag[:, hh], w_post[:, hh]) for hh in range(2)]
                        bias = "post"
                    else:
                        pe.wait_ge(S["tr_read"], TR_AT[p, r, "T2"])
                        ops = [(xT[:, hh], w_3[:, hh]) for hh in range(2)]
                    n_out = 2 * D if p == 0 else D
                    for k in range(nt):
                        n = OUT_AT[p, r, s, k]
                        wait_out(n)
                        o = outp(n)[:, 0:n_out]
                        for q, (a, wt) in enumerate(ops):
                            last = pe.matmul(o, a[:, k * P:(k + 1) * P], wt, start=q == 0, stop=bias is None and q == len(ops) - 1)
                        if bias is not None:
                            b = bias_row[bias]
                            last = pe.matmul(o, ident[0:6, b:b + 1].to_broadcast([6, P]), brow[:, 0:n_out], start=False, stop=True)
                        last.then_inc(S["out_done"], 1)

            readers = {}
            for (p_, r_, s_, k_) in [e for e in OUT_AT if isinstance(e, tuple) and len(e) == 4]:
                n_ = OUT_AT[p_, r_, s_, k_]
                readers[n_] = ("gates", GATE_AT[p_, r_, k_]) if s_ == "O" and p_ in (0, 3, 5) else ("nat_ready", NAT_AT[p_, r_, k_])

            def wait_out(n):
                if n - 2 in readers:
                    s_, v_ = readers[n - 2]
                    pe.wait_ge(S[s_], v_)

            def degrees():
                for r, (t0, nt) in enumerate(RANGES):
                    pe.wait_ge(S["tr_read"], TR_AT["sums", r] - 2)
                    if r == 0:
                        pe.wait_ge(S["deg_step"], SUMS - 1)
                    for k in range(nt):
                        last = pe.transpose(trp[0:AW, r % 2, k * P:(k + 1) * P], tab[0][:, t0 + k], ident[0:P, 0:P])
                    last.then_inc(S["tr_done"], 1)
                pe.wait_ge(S["deg_step"], SUMS + 3)
                pe.wait_ge(S["tr_read"], TR_AT["sums", NR - 1])
                pe.transpose(trp[0:NT, 0, 0:P], inv_deg, ident[0:P, 0:P])
                pe.transpose(trp[0:NT, 1, 0:P], dinv, ident[0:P, 0:P]).then_inc(S["tr_done"], 1)
                pe.wait_ge(S["tr_read"], TR_AT["deg"])
                pe.wait_ge(S["deg_step"], SUMS + 4)
                pe.transpose(trp[0:1, 0, 0:P], top1, ident[0:P, 0:P]).then_inc(S["tr_done"], 1)

            def begin(p, wide):
                if p == 1:
                    return
                pe.wait_ge(S["tr_read"], TR_AT["M", p, 0] - 1)
                pe.wait_ge(S["max_ready"], p - 1)
                pe.transpose(trp[0:1, 0, 0:P], top1, ident[0:P, 0:P]).then_inc(S["tr_done"], 1)
                pe.wait_ge(S["tr_read"], TR_AT["M", p, 0])
                pe.matmul(trp[:, 1, 0:1], ident[0:1, 0:1].to_broadcast([1, 128]), most[0:1, :], start=True, stop=True).then_inc(S["tr_done"], 1)

            def end(wide):
                finish_layer3()

            def finish_layer3():
                for t in range(NT):
                    r = t // WIDE
                    pe.wait_ge(S["outT_ready"], r + 1)
                    if t < 2:
                        pe.wait_ge(S["tr_read"], TR_AT["F", 0] - 1)
                    else:
                        pe.wait_ge(S["gate_used"], len(GATE_AT) + t - 1)
                    for hh in range(2):
                        last = pe.transpose(trp[0:P, t % 2, hh * 128:(hh + 1) * 128], outT[:, hh, t * P:(t + 1) * P], ident[:, :])
                    last.then_inc(S["tr_done"], 1)

            run_schedule(pe, piece, stage, degrees=degrees, begin=begin, end=end)

        @block.vector
        def _(dve):
            links = [0]

            def link(ins):
                links[0] += 1
                ins.then_inc(S["link_s"], 1)
                dve.wait_ge(S["link_s"], links[0])

            dve.memset(zero_block, 0.0).then_inc(S["zeros"], 1)
            dve.memset(ones, 1.0).then_inc(S["ones_ready"], 1)
            dve.memset(eps, EPS)
            dve.memset(scale, 1024.0)
            dve.memset(unscale, 1.0 / 1024.0)
            dve.memset(brow[:, :], 0.0).then_inc(S["ones_ready"], 1)
            dve.memset(weights, 0.0).then_inc(S["w_step"], 1)
            dve.wait_ge(S["w_step"], 1)
            dve.memset(weights[:, :, 0:10:9], 1.0).then_inc(S["prep"], 1)
            dve.memset(attr[0][:, :, EA], 1.0).then_inc(S["prep"], 1)
            dve.memset(attr[1][:, :, EA], 1.0).then_inc(S["prep"], 1)
            dve.wait_ge(S["edges_in"], 64)
            dve.tensor_copy(src_f, src_i).then_inc(S["prep"], 1)
            dve.tensor_copy(dst_f, dst_i).then_inc(S["prep"], 1)
            step = 1
            for part in range(3):
                for w_e, col in ((w_e1, 3 + part), (w_e2, 6 + part)):
                    dve.tensor_copy(weights[:, :, col], w_e).then_inc(S["w_step"], 1)
                dve.wait_ge(S["w_step"], step + 2)
                if part < 2:
                    for w_e, col in ((w_e1, 3 + part), (w_e2, 6 + part)):
                        dve.tensor_tensor(w_e, w_e, weights[:, :, col], ALU.subtract).then_inc(S["w_step"], 1)
                    dve.wait_ge(S["w_step"], step + 4)
                step += 4
            dve.wait_ge(S["prep"], 5)
            dve.scalar_tensor_tensor(out=cell_in, in0=src_f, scalar=float(N), in1=dst_f, op0=ALU.mult, op1=ALU.add).then_inc(S["prep"], 1)
            dve.scalar_tensor_tensor(out=cell_out, in0=dst_f, scalar=float(N), in1=src_f, op0=ALU.mult, op1=ALU.add).then_inc(S["prep"], 1)
            dve.wait_ge(S["prep"], 7)
            dve.wait_ge(S["masks"], 3)
            for d, k, base in ((dump_in, cell_in, N * N), (dump_out, cell_out, N * N), (dump_dst, dst_f, N)):
                dve.tensor_scalar(d, k, -1.0, float(base), ALU.mult, ALU.add).then_inc(S["prep"], 1)
            dve.wait_ge(S["prep"], 10)
            for d in (dump_in, dump_out):
                for q in range(QUAD):
                    dq = d.rearrange("p (t q) -> p t q", q=QUAD)[:, :, q]
                    dve.tensor_scalar(dq, dq, own, float(P * q), ALU.add, ALU.add).then_inc(S["prep"], 1)
            dve.tensor_scalar(dump_dst, dump_dst, own, None, ALU.add).then_inc(S["prep"], 1)
            dve.wait_ge(S["prep"], 11 + 2 * QUAD)
            over = lambda v: v.unsqueeze(1).to_broadcast([P, NT, D])
            dve.wait_ge(S["out_done"], 1)
            link(dve.tensor_scalar(mean_b, outp(0)[:, 0:D], 1.0 / N, None, ALU.mult))
            link(dve.tensor_tensor(Bn[2], Xn, over(mean_b), ALU.subtract))
            dve.wait_ge(S["tr_done"], 3 * LAYERS)
            dve.tensor_tensor(Bn[1], Bn[2], Bn[2], ALU.mult).then_inc(S["ones_ready"], 1)
            dve.wait_ge(S["out_done"], 2)
            dve.tensor_scalar(var_b, outp(1)[:, 0:D], 1.0 / N, None, ALU.mult).then_inc(S["stat"], 1)
            dve.wait_ge(S["stat"], 2)
            link(dve.reciprocal(mean_b, var_b))
            link(dve.tensor_tensor(mean_b, mean_b, gamma_b, ALU.mult))
            link(dve.tensor_tensor(Bn[2], Bn[2], over(mean_b), ALU.mult))
            dve.tensor_tensor(Bn[2], Bn[2], over(beta_b), ALU.add).then_inc(S["stat"], 1)
            dve.wait_ge(S["stat"], 3)
            dve.memset(go_in, 0.0).then_inc(S["edges_ready"], 1)

            def chunk(c, h, first):
                now = bass.ds(EC * c, EC)
                dve.wait_ge(S["cell_T"], c + 1)
                if h or not first:
                    dve.wait_ge(S["sums_done"], c)
                for q in range(EC // QUAD):
                    own_cell = cell_in[:, bass.ds(EC * c + QUAD * q, QUAD)].unsqueeze(2).unsqueeze(3).to_broadcast([P, QUAD, QUAD, P])
                    dve.tensor_tensor(same_cell[:, QUAD * q:QUAD * q + QUAD], cellT[:, q].unsqueeze(1).to_broadcast([P, QUAD, QUAD, P]),
                                      own_cell, ALU.is_equal).then_inc(S["eq_step"], 1)
                dve.tensor_tensor(same_dst.rearrange("p (b k) n -> p b k n", b=2), dstT,
                                  dst_f[:, now].rearrange("p (b k) -> p b k", b=2).unsqueeze(3).to_broadcast([P, 2, 4, P]),
                                  ALU.is_equal).then_inc(S["eq_ready"], 1)
                dve.wait_ge(S["eq_step"], c * K + 2)
                own_tile = same_cell.rearrange("p (q k) j n -> p q (k j) n", q=2)[:, :, 0:QUAD * QUAD:QUAD + 1]
                dve.tensor_tensor(before_cell.rearrange("p (q k) n -> p q k n", q=2), own_tile,
                                  upper.unsqueeze(1).unsqueeze(1).to_broadcast([P, 2, QUAD, P]), ALU.mult).then_inc(S["eq_step"], 1)
                dve.wait_ge(S["eq_ready"], c + 1)
                dve.tensor_tensor(before_dst, same_dst, upper.unsqueeze(1).to_broadcast([P, EC, P]), ALU.mult).then_inc(S["eq_step"], 1)
                dve.wait_ge(S["sums_done"], c + 1)
                n_cell = sum_w[h][:, :, 9]
                dve.scalar_tensor_tensor(out=go_in, in0=n_cell, scalar=1.0, in1=dump_in[:, now], op0=ALU.min, op1=ALU.mult).then_inc(S["eq_step"], 1)
                dve.scalar_tensor_tensor(out=go_out, in0=n_cell, scalar=1.0, in1=dump_out[:, now], op0=ALU.min, op1=ALU.mult).then_inc(S["eq_step"], 1)
                dve.scalar_tensor_tensor(out=go_dst, in0=n_dst[h], scalar=1.0, in1=dump_dst[:, now], op0=ALU.min, op1=ALU.mult).then_inc(S["eq_step"], 1)
                if not first:
                    dve.wait_ge(S["in_done"], (c - 1) * (16 * EC))
                    dve.wait_ge(S["out_sc_done"], (c - 1) * (16 * EC))
                dve.tensor_reduce(val_in[h], sum_w[h][:, :, 0:6].rearrange("p k (c i) -> p k c i", i=3), AX.X, ALU.add).then_inc(S["at_ready"], 1)
                dve.tensor_reduce(val_out[h], sum_w[h][:, :, 6:9], AX.X, ALU.add).then_inc(S["at_ready"], 1)
                dve.wait_ge(S["eq_step"], c * K + 7)
                dve.tensor_tensor(at_in[h], go_in, cell_in[:, now], ALU.add).then_inc(S["at_ready"], 1)
                dve.tensor_tensor(at_out[h], go_out, cell_out[:, now], ALU.add).then_inc(S["at_ready"], 1)
                dve.tensor_tensor(at_sum[:, now], go_dst, dst_f[:, now], ALU.add).then_inc(S["at_ready"], 1)
                dve.wait_ge(S["at_ready"], c * 5 + 5)
            for h in range(2):
                chunk(h, h, True)
            with dve.Fori(1, CH // 2) as i:
                for h in range(2):
                    chunk(i * 2 + h, h, False)

            def finish(m):
                p, r, what = STEPS[m]
                w = RANGES[r][1] * P
                dve.wait_ge(S["piece_used"], (m + 1) * PIECES)
                if m >= 2:
                    p2, r2, _ = STEPS[m - 2]
                    if p2 == 0:
                        if r2 < r or p != 0:
                            dve.wait_ge(S["out_done"], OUT_AT[0, r2, "O", RANGES[r2][1] - 1])
                    elif p2 < 6:
                        dve.wait_ge(S["out_done"], OUT_AT[p2, r2, OUTS[p2][-1], RANGES[r2][1] - 1])
                    else:
                        dve.wait_ge(S["agr_ready"], AGR_AT[p2, r2])
                if p == 0:
                    dve.tensor_copy(agg[:, m % 2, :, 0:w], acc(m)[:, :, 0:w]).then_inc(S["agg_ready"], 1)
                else:
                    dve.wait_ge(rows_in[m % 2], ROW_AT[m])
                    dve.scalar_tensor_tensor(out=agg[:, m % 2, :, 0:w], in0=acc(m)[:, :, 0:w], scalar=unscale,
                                             in1=scale_row(m, w).unsqueeze(1).to_broadcast([128, 2, w]),
                                             op0=ALU.mult, op1=ALU.mult).then_inc(S["agg_ready"], 1)

            def stage(p, r, s, wide):
                t0, nt = RANGES[r]
                if s == "O" and p in (0, 3, 5):
                    for k in range(nt):
                        t = t0 + k
                        dve.wait_ge(S["gates"], GATE_AT[p, r, k])
                        g, n = gate[0:P, k % 2, 0:D], gate[0:P, k % 2, D:2 * D]
                        if p == 0:
                            h = Bn[2][:, t]
                            link(dve.tensor_tensor(h, h, n, ALU.subtract))
                            link(dve.tensor_tensor(h, h, g, ALU.mult))
                            dve.tensor_tensor(h, h, n, ALU.add).then_inc(S["gate_used"], 1)
                            dve.wait_ge(S["gate_used"], GATE_AT[p, r, k])
                            link(dve.tensor_tensor(Xn[:, t], Xn[:, t], h, ALU.add))
                        else:
                            dve.tensor_tensor(Xn[:, t], Xn[:, t], g, ALU.add).then_inc(S["gate_used"], 1)
                            dve.wait_ge(S["gate_used"], GATE_AT[p, r, k])
                        link(dve.bn_stats(bn6[:, k], Xn[:, t]))
                        last = dve.bn_aggr(mv[:, k], bn6[:, k])
                        if k == nt - 1:
                            last.then_inc(S["mv_ready"], 1)
                if s == "N" and p in (0, 3, 5):
                    dve.wait_ge(S["std_ready"], NORM_AT[p, r])
                    link(dve.reciprocal(rstd[:, 0:nt], std[:, 0:nt]))
                    for k in range(nt):
                        last = dve.tensor_scalar(Xn[:, t0 + k], Xn[:, t0 + k], mv[:, k, 0:1], rstd[:, k:k + 1], ALU.subtract, ALU.mult)
                    last.then_inc(S["norm_ready"], 1)
                if s == "X" and 1 <= p <= 5:
                    dve.wait_ge(S["nat_ready"], NAT_AT[p, r, nt - 1])
                    v = SRC[p + 1][:, t0:t0 + nt]
                    link(dve.tensor_reduce(top[:, r:r + 1], v, AX.XY, ALU.max))
                    link(dve.tensor_reduce(low_, v, AX.XY, ALU.min))
                    link(dve.tensor_scalar(top[:, NR + r:NR + r + 1], low_, -1.0, None, ALU.mult))
                if s == "A" and p == 6:
                    w = nt * P
                    dve.wait_ge(S["agr_ready"], AGR_AT[p, r])
                    for hh in range(2):
                        link(dve.bn_stats(st6[:, hh, r], outT[:, hh, t0 * P:t0 * P + w]))

            def degrees():
                dve.wait_ge(S["tab_in"], 16 * SUMS)
                for q in range(1, SUMS):
                    dve.tensor_tensor(tab[0], tab[0], tab[q], ALU.add).then_inc(S["deg_step"], 1)
                    dve.wait_ge(S["deg_step"], q)
                dve.tensor_copy(deg, tab[0][:, :, EA]).then_inc(S["deg_step"], 1)
                dve.wait_ge(S["deg_step"], SUMS)
                dve.tensor_scalar(inv_deg, deg, 1.0, None, ALU.max).then_inc(S["deg_step"], 1)
                dve.wait_ge(S["deg_step"], SUMS + 1)
                dve.reciprocal(inv_deg, inv_deg).then_inc(S["deg_step"], 1)
                dve.wait_ge(S["stat"], 4)
                dve.reciprocal(dinv, root).then_inc(S["deg_step"], 1)
                dve.wait_ge(S["tr_done"], TR_AT["deg"])
                dve.tensor_copy(degT_s[:, :, 0:P], trp[0:NT, 0:2, 0:P]).then_inc(S["tr_read"], 1)
                dve.tensor_reduce(top1, top_count, AX.X, ALU.max).then_inc(S["deg_step"], 1)
                dve.wait_ge(S["tr_done"], TR_AT["most"])
                link(dve.tensor_reduce(most[0:1, :], trp[0:1, 0, 0:P], AX.X, ALU.max))
                dve.tensor_copy(flag[0:1, :], most[0:1, :]).then_inc(S["flag_ready"], 1)
                dve.sem_inc(S["tr_read"], 1)

            def piece(m, j, wide):
                p, r, what = STEPS[m]
                if what == "in":
                    q = (m // 2) * PIECES + j
                    dve.wait_ge(S["count_copied"], q + 1)
                    dve.tensor_reduce(top_count[:, q:q + 1], count_s[:, q % 2, :, 0:RANGES[r][1] * P], AX.XY, ALU.max).then_inc(S["count_max"], 1)

            def begin(p, wide):
                if p > 1:
                    dve.tensor_reduce(top1, top, AX.X, ALU.max).then_inc(S["max_ready"], 1)
                    dve.wait_ge(S["tr_done"], TR_AT["M", p, 0])
                    dve.tensor_reduce(most[0:1, :], trp[0:1, 0, 0:P], AX.X, ALU.max).then_inc(S["tr_read"], 1)
                    dve.wait_ge(S["tr_done"], TR_AT["M", p, 1])
                    dve.tensor_scalar(power, trp[:, 1, 0:1], 2.0 ** -60, 2.0 ** 60, ALU.max, ALU.min).then_inc(S["tr_read"], 1)
                    dve.wait_ge(S["tr_read"], TR_AT["M", p, 1])
                    bits = power.bitcast(I32)
                    link(dve.tensor_scalar(bits, bits, 0x7F800000, None, ALU.bitwise_and))
                    inv = (unused if wide else scale)
                    link(dve.tensor_scalar(inv.bitcast(I32), bits, -1.0, float(254 << 23), ALU.mult, ALU.add))
                    link(dve.tensor_scalar(inv, inv, 2.0 ** 14, None, ALU.mult))
                    dve.tensor_scalar(unused if wide else unscale, power, 2.0 ** -14, None, ALU.mult).then_inc(S["scale_ready"], 1)
                elif wide:
                    dve.memset(scale, 1.0)
                    dve.memset(unscale, 1.0).then_inc(S["scale_ready"], 1)
                else:
                    dve.memset(unused, 0.0).then_inc(S["scale_ready"], 1)
                dve.wait_ge(S["scale_ready"], p)
                if p <= LAYERS:
                    dve.tensor_scalar(wE_s, wE[:, (p - 1) * D:p * D], scale[0:AW, :], None, ALU.mult).then_inc(S["wE_ready"], 1)
                if wide:
                    return
                for j in range(PIECES):
                    now = slice(j * ROWS, (j + 1) * ROWS)
                    f2 = lambda v: v.rearrange("p t f -> p (t f)")
                    dve.wait_ge(S["split_hi"], (p - 1) * PIECES + j + 1)
                    dve.scalar_tensor_tensor(out=f2(parts[:, 1, now]), in0=f2(SRC[p][:, now]), scalar=scale[0:P, :], in1=f2(parts[:, 0, now]),
                                             op0=ALU.mult, op1=ALU.subtract).then_inc(S["split_lo"], 1)

            def finish_layer3():
                for hh in range(2):
                    last = dve.bn_aggr(mv3[:, hh], st6[:, hh].rearrange("p r c -> p (r c)"))
                last.then_inc(S["fin_ready"], 1)
                dve.wait_ge(S["fin_ready"], 2)
                link(dve.reciprocal(scale3, std3))
                link(dve.tensor_tensor(scale3, scale3, c_gamma, ALU.mult))
                link(dve.tensor_tensor(shift3, mv3[:, :, 0], scale3, ALU.mult))
                dve.tensor_tensor(shift3, c_beta, shift3, ALU.subtract).then_inc(S["fin_ready"], 1)
                for r, (t0, nt) in enumerate(RANGES):
                    for k in range(nt):
                        t = t0 + k
                        dve.wait_ge(S["tr_done"], TR_AT["F", t])
                        dve.tensor_tensor(Xn[:, t], Xn[:, t], trp[0:P, t % 2, 0:D], ALU.add).then_inc(S["gate_used"], 1)
                        dve.wait_ge(S["gate_used"], len(GATE_AT) + t + 1)
                        link(dve.bn_stats(bn6[:, k], Xn[:, t]))
                        last = dve.bn_aggr(mv[:, k], bn6[:, k])
                    last.then_inc(S["mv_ready"], 1)
                    dve.wait_ge(S["std_ready"], len(NORM) + r + 1)
                    link(dve.reciprocal(rstd[:, 0:nt], std[:, 0:nt]))
                    for k in range(nt):
                        dve.tensor_scalar(Xn[:, t0 + k], Xn[:, t0 + k], mv[:, k, 0:1], rstd[:, k:k + 1], ALU.subtract, ALU.mult).then_inc(S["norm_ready"], 1)

            at_branch = [None]

            def begin_(p, wide):
                if p == 1:
                    if at_branch[0] is None:
                        at_branch[0] = links[0]
                    links[0] = at_branch[0]
                begin(p, wide)

            run_schedule(dve, piece, stage, finish, degrees, begin_, lambda wide: finish_layer3())


_INS = ['x', 'src', 'dst', 'edge_attr_64', 'edge_weight', 'edge_weight_n2', 'L0_gnn_gamma', 'L0_gnn_beta', 'L0_gnn_W_in',
        'L0_gnn_b_in', 'L0_gnn_W_out', 'L0_gnn_b_out', 'L0_gnn_W_x2i', 'L0_gnn_b_x2i', 'L0_gnn_W_h2h', 'L1_gnn_Wl',
        'L1_gnn_bl', 'L1_gnn_Wr', 'L1_gnn_We', 'L1_gnn_be', 'L2_gnn_W_pre', 'L2_gnn_b_pre', 'L2_gnn_W1', 'L2_gnn_b1',
        'L2_gnn_W2', 'L2_gnn_b2', 'L2_gnn_W_post', 'L2_gnn_b_post', 'L3_gnn_W', 'L3_gnn_b', 'L3_gnn_gamma', 'L3_gnn_beta']


def kernel(**inputs):
    import numpy as _np
    import concourse.bacc as _bacc
    from concourse import mybir as _mybir
    from concourse.bass_utils import run_bass_kernel_spmd as _run

    nc = _bacc.Bacc("TRN2", target_bir_lowering=False, num_devices=1)
    arrays, args = {}, []
    for name in _INS:
        a = _np.ascontiguousarray(inputs[name])
        arrays[f"in_{name}"] = a
        args.append(nc.dram_tensor(f"in_{name}", a.shape, _mybir.dt.from_np(a.dtype), kind="ExternalInput").ap())
    out = nc.dram_tensor("out_0", arrays["in_x"].shape, F32, kind="ExternalOutput").ap()
    build_gnn(nc, *args, out)
    r = _run(nc, [arrays], core_ids=[0])
    return r.results[0]["out_0"]
```

```python
import math
from contextlib import ExitStack

import concourse.bass as bass
from concourse import mybir

F32 = mybir.dt.float32
F16 = mybir.dt.float16
BF16 = mybir.dt.bfloat16
I32 = mybir.dt.int32
U32 = mybir.dt.uint32
ALU = mybir.AluOpType
ACT = mybir.ActivationFunctionType
AX = mybir.AxisListType

P = 125
EPS = 1e-5
WIDE = 4
EC = 8
QUAD = 4
PIECES = 5
SUMS = 5
SC = 10
EXACT = 2048




def places(events):
    return {e: n + 1 for n, e in enumerate(events)}


def build_gnn(nc, x, src, dst, edge_attr, edge_w, edge_w2, gamma0, beta0, W_in, b_in, W_out, b_out, W_x2i, b_x2i,
              W_h2h, Wl, bl, Wr, We, be, W_pre, b_pre, W1, b1, W2, b2, W_post, b_post, W3, b3, gamma3, beta3, out):
    N, D = x.shape
    NT = N // P
    E, EA = edge_attr.shape
    ET = E // P
    CH = ET // EC
    AW = EA + 1
    COLS = WIDE * P
    LAYERS = Wl.shape[0]
    HALVES = D // 128
    RANGES = [(r * WIDE, min(WIDE, NT - r * WIDE)) for r in range(-(-NT // WIDE))]
    NR = len(RANGES)
    ROWS = NT // PIECES
    ZERO, REPEAT = 1000, 6
    SLAB = 128 * ZERO * REPEAT

    CELLS = -(-(N * N + QUAD * P) // SLAB) * SLAB
    in_mat = nc.dram_tensor("in_mat", [CELLS, 2], F32, kind="Internal").ap()
    out_mat = nc.dram_tensor("out_mat", [CELLS, 1], F32, kind="Internal").ap()
    count_mat = nc.dram_tensor("count_mat", [N, N], F16, kind="Internal").ap()
    sum_tab = [nc.dram_tensor(f"sum_tab{q}", [N + P, AW], F32, kind="Internal").ap() for q in range(SUMS)]
    attr_val = nc.dram_tensor("attr_val", [P, ET * AW], F32, kind="Internal").ap()
    sums_T = nc.dram_tensor("sums_T", [AW, N], F32, kind="Internal").ap()
    deg_rows = nc.dram_tensor("deg_rows", [2, N], F32, kind="Internal").ap()

    STEPS = [(0, r, m) for r in range(NR) for m in ("in", "out")] + [(p, r, "count") for p in range(1, 7) for r in range(NR)]
    LAST_OF = {}
    for m, (p, r, _) in enumerate(STEPS):
        LAST_OF[p, r] = m
    EPI = [(p, r) for p in range(7) for r in range(NR)]
    OUTS = {0: ["O"], 1: ["O"], 2: ["O"], 3: ["O", "O2"], 4: ["O"], 5: ["O", "O2"], 6: []}
    TRS = {0: ["T"], 1: ["T"], 2: ["T"], 3: ["T", "T2"], 4: [], 5: ["T2"], 6: []}
    TR_AT = places(["w%d" % i for i in range(2 * LAYERS + LAYERS)] + [("feat", t) for t in range(NT)]
                   + ["peak", "peak2"] + [(0, r, "T") for r in range(NR)] + [("sums", r) for r in range(NR)] + ["deg", "most"]
                   + [e for q in range(1, 7) for e in (["W_pre", "fold"] if q == 2 else []) + ([("M", q, 0), ("M", q, 1)] if q > 1 else [])
                      + [(p, r, s) for p, r in EPI if p == q for s in TRS[p]]] + [("F", t) for t in range(NT)])
    OUT_AT = places(["mean", "var"] + [("feat", t) for t in range(NT)]
                    + [(p, r, s, k) for p, r in EPI for s in OUTS[p] for k in range(RANGES[r][1])])
    NORM = [(p, r) for p, r in EPI if p in (0, 3, 5)]
    GATE_AT = places([(p, r, k) for p, r in NORM for k in range(RANGES[r][1])])
    NORM_AT = places(NORM + [("F", t) for t in range(NT)])
    NAT_AT = places([("feat", t) for t in range(NT)]
                    + [(p, r, k) for p, r in EPI if 1 <= p <= 5 for k in range(RANGES[r][1])])
    AGR_AT = places([(p, r) for p, r in EPI if p >= 4])
    LOAD = {}
    for wide in (False, True):
        landed = [0] * PIECES
        for m, (p, _, _) in enumerate(STEPS):
            for j in range(PIECES):
                n = m * PIECES + j
                s = n % 2 if p == 0 or wide else j
                if p:
                    landed[s] += 16
                LOAD[wide, m, j] = (s, landed[s])
    ROW_AT = {}
    rows_landed = [0, 0]
    for m, (p, _, _) in enumerate(STEPS):
        if p:
            rows_landed[m % 2] += 32 if p <= LAYERS else 16
            ROW_AT[m] = rows_landed[m % 2]

    with ExitStack() as ctx:
        def sb(name, shape, dt=F32):
            return ctx.enter_context(nc.sbuf_tensor(name, shape, dt))

        def sem(name):
            return ctx.enter_context(nc.semaphore(name))

        psum = ctx.enter_context(nc.psum_tensor("psum", [128, 8, 512], F32))
        X = sb("X", [128, NT * D])
        B = [sb(f"B{i}", [128, NT * D]) for i in range(3)]
        ring = sb("ring", [128, 5 * ROWS * COLS])
        agg = sb("agg", [128, 2, 2, COLS])
        xT = sb("xT", [128, 2, COLS])
        rowbuf = sb("rowbuf", [128, 4 * COLS])
        wl0 = sb("wl0", [128, 8 * 512])
        wl1 = sb("wl1", [128, LAYERS * 4 * D])
        wE = sb("wE", [AW, LAYERS * D])
        brow = sb("brow", [96, 2 * D])
        ident = sb("ident", [128, 128])
        ident16 = sb("ident16", [128, 128], F16)
        gate = sb("gate", [128, 2, 512])
        cols = sb("cols", [128, 6, 2])
        small = sb("small", [128, 320])

        nat = lambda t_: t_[0:P, :].rearrange("p (t f) -> p t f", t=NT)
        Xn, Bn = nat(X), [nat(b) for b in B]
        CHUNK_STEPS = 7
        parts = B[2][0:P, :].bitcast(F16).rearrange("p (c t f) -> p c t f", c=2, t=NT)
        halves = [B[b][0:P, :].bitcast(F16).rearrange("p (t f c) -> p t f c", t=NT, c=2) for b in range(2)]
        hi_tmp = [agg[0:P, h].rearrange("p a n -> p (a n)")[:, 0:ROWS * D // 2].bitcast(F16).rearrange("p (t f) -> p t f", t=ROWS) for h in range(2)]
        outT = B[1][:, 0:2 * N].rearrange("p (h n) -> p h n", h=2)
        w3 = lambda t_, a, k, n: t_[:, a:a + k * n].rearrange("p (k n) -> p k n", k=k)
        w_io = w3(wl0, 0, 2, 512)
        w_x2i = w3(wl0, 1024, 4, 512)
        w_h2h = w3(wl0, 3072, 2, 512)
        w_pre, w_1, w_2, w_post = (w3(wl0, i * 512, 2, D) for i in range(4))
        w_3 = w3(wl0, 2048, 2, D)
        w_preT = w3(wl0, 2560, 2, D)
        w_fold = w_pre
        w_lT = [w3(wl1, (2 * l) * 512, 2, D) for l in range(LAYERS)]
        w_rT = [w3(wl1, (2 * l + 1) * 512, 2, D) for l in range(LAYERS)]
        bias_row = {"io": 0, "x2i": 1, 0: 2, 1: 3, 2: 4, "post": 5, "fold": 0}
        c_pre, c_1, c_2, c_3, c_gamma, c_beta = (cols[:, i, :] for i in range(6))
        bias16 = brow[:, :].bitcast(BF16)[:, 0:2 * D]
        so = [0]

        def tiny(n, parts=P):
            so[0] += n
            return small[0:parts, so[0] - n:so[0]]
        mv = tiny(2 * WIDE).rearrange("p (k c) -> p k c", c=2)
        bn6 = tiny(6 * WIDE).rearrange("p (k c) -> p k c", c=6)
        std, rstd = tiny(WIDE), tiny(WIDE)
        eps = tiny(1, 128)
        deg, inv_deg, root, dinv = tiny(NT), tiny(NT), tiny(NT), tiny(NT)
        st6_all = tiny(2 * NR * 6, 128)
        st6 = st6_all.rearrange("p (h r c) -> p h r c", h=2, c=6)
        peaks_f = st6_all[0:P, 0:4 * PIECES].rearrange("p (s g b) -> p s g b", s=2, b=2)
        peaks_w = st6_all[0:P, 4 * PIECES:4 * PIECES + 4].rearrange("p (s b) -> p s b", s=2)
        top = tiny(2 * NR)
        low_, most, top1 = tiny(1), tiny(1), tiny(1)
        scale, unscale, power, no_scale = tiny(1, 128), tiny(1, 128), tiny(1, 128), tiny(1, 128)
        last_mv = [mv, st6_all[0:P, 0:2 * WIDE].rearrange("p (k c) -> p k c", c=2)]
        last_std, last_rstd, last_shift = ([st6_all[0:P, (a + h) * WIDE:(a + h + 1) * WIDE] for h in range(2)] for a in (2, 4, 6))
        peak, power2 = tiny(2), tiny(2, 128)
        scale0 = tiny(2, 128)
        ROOM = 2.0 ** -max(0, math.ceil(math.log2(2 * E / 65504)))
        pick = tiny(3, 96).bitcast(BF16)
        flag = tiny(1).bitcast(I32)
        at_sum_now = [tiny(SC).bitcast(U32) for _ in range(2)]
        mv3 = gate[:, 0, 0:4].rearrange("p (h c) -> p h c", c=2)
        std3, scale3, shift3 = gate[:, 0, 4:6], gate[:, 0, 6:8], gate[:, 0, 8:10]

        acc = lambda m: psum[:, 2 * (m % 2):2 * (m % 2) + 2, 0:COLS]
        trp = psum[:, 4:6, 0:512]
        outp = lambda n: psum[0:P, 6 + n % 2, :]

        ro = [0]

        def carve(n):
            ro[0] += n
            return ring[0:P, ro[0] - n:ro[0]]
        by_tile = lambda a: a.rearrange("p (k n) -> p k n", k=EC)
        src_i, dst_i = carve(ET).bitcast(I32), carve(ET).bitcast(I32)
        weights = carve(5 * ET).bitcast(BF16).rearrange("p (t c) -> p t c", c=10)
        src_f, dst_f, cell_in, cell_out, dump_in, dump_out, dump_dst = (carve(ET) for _ in range(7))
        cell_b, dst_b, same_dst = (by_tile(carve(EC * P)) for _ in range(3))
        before_cell, before_dst = (by_tile(carve(EC * P // 2).bitcast(BF16)) for _ in range(2))
        attr = [by_tile(carve(EC * AW)) for _ in range(2)]
        val_attr = [carve(EC * AW) for _ in range(2)]
        val_in = [by_tile(carve(EC * 2)) for _ in range(2)]
        val_out = [carve(EC) for _ in range(2)]
        at_in = [carve(EC).bitcast(U32) for _ in range(2)]
        at_out = [carve(EC).bitcast(U32) for _ in range(2)]
        go_in, go_out, go_dst, own = carve(EC), carve(EC), carve(EC), carve(1)
        upper = carve(P // 2 + 1).bitcast(BF16)[:, 0:P]
        upper_f = xT[0:P, 0, 0:P]
        same_cell = agg[0:P].rearrange("p a b n -> p (a b n)")[:, 0:EC * QUAD * P // 2].bitcast(BF16).rearrange("p (k j n) -> p k j n", j=QUAD, n=P)
        w_e1, w_e2 = gate[0:P, 0, 0:ET], gate[0:P, 1, 0:ET]
        sc_val = [rowbuf[0:P, h * SC * AW:(h + 1) * SC * AW] for h in range(2)]
        zero_block = rowbuf[:, 0:ZERO]
        at_sum = rowbuf[0:P, 2 * SC * AW:2 * SC * AW + ET].bitcast(U32)
        scale_row = lambda m, w: rowbuf[:, (m % 2) * COLS:(m % 2) * COLS + w]
        sums_row = lambda m, w: rowbuf[0:AW, (2 + m % 2) * COLS:(2 + m % 2) * COLS + w]
        cellT = psum[0:P, 0:2, 0:4 * P].rearrange("p b (k n) -> p b k n", k=4)
        dstT = psum[0:P, 2:4, 0:4 * P].rearrange("p b (k n) -> p b k n", k=4)
        sum_attr = psum[0:P, 4:6, 0:4 * AW].rearrange("p b (k n) -> p b k n", k=4)
        sum_w = [psum[0:P, 6 + h, 0:10 * EC].rearrange("p (k n) -> p k n", k=EC) for h in range(2)]
        n_dst = [psum[0:P, 6 + h, 10 * EC:11 * EC] for h in range(2)]
        raw_l = B[1][:, 0:LAYERS * 512].rearrange("p (l h n) -> p l h n", l=LAYERS, h=2)
        raw_r = B[1][:, LAYERS * 512:2 * LAYERS * 512].rearrange("p (l h n) -> p l h n", l=LAYERS, h=2)
        raw_e = B[1][:, 2 * LAYERS * 512:2 * LAYERS * 512 + LAYERS * 2 * EA].rearrange("p (l h n) -> p l h n", l=LAYERS, h=2)
        ones = agg[0:P, 0, 0, 0:P]
        gamma_b, beta_b, mean_b, var_b = agg[0:P, 1, 0, 0:D], agg[0:P, 1, 1, 0:D], agg[0:P, 0, 1, 0:D], agg[0:P, 0, 0, 128:128 + D]
        hT = lambda t: xT[:, t % 2, 0:2 * P].rearrange("p (h n) -> p h n", h=2)
        SLOT0, LAST_W = 2 * ROWS * COLS, 2 * ROWS * RANGES[-1][1] * P
        tab = [ring[0:P, a:a + NT * AW].rearrange("p (t a) -> p t a", a=AW)
               for a in (h * SLOT0 + LAST_W + q * NT * AW for h in range(2) for q in range(2))]
        tab.append(rowbuf[0:P, 0:NT * AW].rearrange("p (t a) -> p t a", a=AW))
        sumsT_s = ring[0:AW, SLOT0 + LAST_W:SLOT0 + LAST_W + N]
        degT_s = B[0][0:NT, 0:2 * 128].rearrange("p (c n) -> p c n", c=2)
        count_s = ring[0:P, 4 * ROWS * COLS:5 * ROWS * COLS].bitcast(F16).rearrange("p (c t n) -> p c t n", c=2, t=ROWS)
        top_count = small[0:P, 320 - NR * PIECES:320]
        wE_s = gate[0:AW, 0, 256:512]

        def row_slots(m, j):
            r = STEPS[m][1]
            one = 2 * COLS if r < NR - 1 else 2 * RANGES[r][1] * P
            base = LOAD[False, m, j][0] * 2 * ROWS * COLS
            return ring[0:P, base:base + ROWS * one].rearrange("p (t x) -> p t x", t=ROWS)

        def slot(m, j, wide=False):
            p, r, what = STEPS[m]
            s, w = LOAD[wide, m, j][0], RANGES[r][1] * P
            if p and wide:
                a = ring[0:P, s * 2 * ROWS * COLS:s * 2 * ROWS * COLS + 2 * ROWS * w]
                return a.rearrange("p (t n c) -> p t n c", t=ROWS, c=2)
            if p == 0:
                a = row_slots(m, j)
                return a.rearrange("p t (n c) -> p t n c", c=2)[:, :, 0:w] if what == "in" else a[:, :, 0:w]
            base = s * ROWS * COLS
            return ring[0:P, base:base + ROWS * COLS].bitcast(F16)[:, 0:ROWS * w].rearrange("p (t n) -> p t n", t=ROWS)

        def split_slot(m, j):
            p, r, what = STEPS[m]
            w, a = RANGES[r][1] * P, row_slots(m, j)
            if what == "in":
                return a.bitcast(F16).rearrange("p t (n c) -> p t n c", c=4)[:, :, 0:w, 0:2]
            half = a.shape[2] // 2
            return a[:, :, half:half + w].bitcast(F16).rearrange("p t (c n) -> p t n c", c=2)

        names = ("zeros zero_in zero_out edges_in x_in w_in raw_in row_in mask_step masks prep edges_ready bcast cell_T eq_ready "
                 "sums_done vals_ready at_ready eq_step in_done out_sc_done sc_at w2_in link_s tr_done tr_read "
                 "out_done out_read agg_ready piece_used gates gate_used nat_ready agr_ready mv_ready std_ready norm_ready ident16_ready "
                 "ones_ready stat count_copied tab_in deg_step deg_rows_out outT_ready fin_ready y_stored "
                 "zero_sum ocol count_max flag_ready split_hi split_lo scale_ready wE_ready max_ready w_step feat_hi feat_split hi_ready lo_ready scale0_ready peak_ready row_used bias_ready last_scales").split()
        S = {n: sem(n) for n in names}
        row_in = [sem(f"row_in{k}") for k in range(2 * ROWS)]
        count_stored = [sem(f"count_stored{h}") for h in range(2)]
        attr_stored = [sem(f"attr_stored{h}") for h in range(2)]
        attr_in = [sem(f"attr_in{h}") for h in range(2)]
        sc_in = [sem(f"sc_in{h}") for h in range(2)]
        sc_done = [sem(f"sc_done{q}") for q in range(SUMS)]
        load_in = [sem(f"load_in{s}") for s in range(PIECES)]
        rows_in = [sem(f"rows_in{s}") for s in range(2)]
        edge_attr_v = edge_attr.rearrange("(p t) a -> p t a", p=P)
        in_v = in_mat[0:N * N, :].rearrange("(t p d) c -> p t (d c)", p=P, d=N)
        out_v = out_mat[0:N * N, :].rearrange("(t p d) c -> p t (d c)", p=P, d=N)
        count_v = count_mat.rearrange("(t p) d -> p t d", p=P)
        wv = lambda w: w.rearrange("(k p) n -> p k n", p=128)

        def run_schedule(eng, piece, stage, finish=None, degrees=None, begin=None, end=None):
            def steps(passes, wide):
                before_ = None
                for m, (p, r, what) in enumerate(STEPS):
                    if p not in passes:
                        continue
                    if p and r == 0 and begin:
                        begin(p, wide)
                    for j in range(PIECES):
                        if piece:
                            piece(m, j, wide)
                        if before_:
                            for s in {0: ("A", "T"), 1: ("O",), 2: ("N",), 3: ("T2",)}.get(j, ()):
                                stage(*before_, s, wide)
                    if finish:
                        finish(m)
                    if before_:
                        for s in ("O2", "X"):
                            stage(*before_, s, wide)
                    before_ = (p, r) if m == LAST_OF[p, r] else None
                    if before_ and r == NR - 1:
                        for s in ("A", "T", "O", "N", "T2", "O2", "X"):
                            stage(*before_, s, wide)
                        before_ = None

            steps((0,), False)
            if degrees:
                degrees()
            eng.wait_ge(S["flag_ready"], 1)
            largest = eng.value_load(flag[0:1, 0:1], min_val=0, max_val=E)
            with eng.If(largest < EXACT):
                steps(range(1, 7), False)
                if end:
                    end(False)
            with eng.Else():
                steps(range(1, 7), True)
                if end:
                    end(True)

        def ahead(work, m, j):
            n = m * PIECES + j
            for k in ([0, 1] if n == 0 else [n + 1]):
                if n < 2 * NR * PIECES and k < 2 * NR * PIECES:
                    work(*divmod(k, PIECES))

        SRC = {1: Xn, 2: Bn[0], 3: Bn[1], 4: Bn[0], 5: Bn[1], 6: Bn[0]}
        block = ctx.enter_context(nc.Block())
        Z_IN, Z_OUT = 2 * CELLS // SLAB, CELLS // SLAB

        @block.sync
        def _(sp):
            for a, b in ((src_i, src), (dst_i, dst), (w_e1, edge_w), (w_e2, edge_w2)):
                sp.dma_start(a, b.rearrange("(p t) -> p t", p=P)).then_inc(S["edges_in"], 16)
            sp.dma_start(Xn, x.rearrange("(t p) f -> p t f", p=P)).then_inc(S["x_in"], 16)
            sp.dma_start(gamma_b, gamma0.unsqueeze(0).to_broadcast([P, D])).then_inc(S["x_in"], 16)
            sp.dma_start(beta_b, beta0.unsqueeze(0).to_broadcast([P, D])).then_inc(S["x_in"], 16)
            for a, w in ((w_io[:, :, 0:D], W_in), (w_io[:, :, D:2 * D], W_out), (w_x2i, W_x2i), (w_h2h, W_h2h)):
                sp.dma_start(a, wv(w)).then_inc(S["w_in"], 16)
            for l in range(LAYERS):
                sp.dma_start(raw_l[:, l], wv(Wl[l])).then_inc(S["raw_in"], 16)
                sp.dma_start(raw_r[:, l], wv(Wr[l])).then_inc(S["raw_in"], 16)
                sp.dma_start(raw_e[:, l], wv(We[l])).then_inc(S["raw_in"], 16)
            r1 = lambda v: v.unsqueeze(0)
            sp.wait_ge(S["ones_ready"], 2)
            for q in (0, 32, 64):
                row = lambda b: brow[q + b:q + b + 1, 0:D]
                for a, v in ((row(0), b_in), (brow[q:q + 1, D:2 * D], b_out), (brow[q + 1:q + 2, :], b_x2i),
                             (row(2), bl[0]), (row(3), bl[1]), (row(4), bl[2]), (row(5), b_post)):
                    sp.dma_start(a, r1(v)).then_inc(S["w_in"], 16)
            sp.dma_start(wE[EA:AW, :], be.rearrange("(a l) d -> a (l d)", a=1)).then_inc(S["w_in"], 16)
            def chunk(c, h, first):
                if not first:
                    sp.wait_ge(S["sums_done"], c - 1)
                sp.dma_start(attr[h][:, :, 0:EA], edge_attr_v[:, bass.ds(EC * c, EC), :]).then_inc(attr_in[h], 16)
            sp.wait_ge(S["prep"], 3)
            for h in range(2):
                chunk(h, h, True)
            with sp.Fori(1, CH // 2) as i:
                for h in range(2):
                    chunk(i * 2 + h, h, False)
            def load_tables():
                for q in range(SUMS):
                    sp.wait_ge(sc_done[q], 16 * ET // SUMS)
                for q in range(SUMS):
                    sp.dma_start(tab[q], sum_tab[q][0:N, :].rearrange("(t p) a -> p t a", p=P)).then_inc(S["tab_in"], 16)

            def piece(m, j, wide):
                p, r, what = STEPS[m]
                t0, nt = RANGES[r]
                c0, w = t0 * P, nt * P
                if (m, j) == (0, 0):
                    sp.wait_ge(S["in_done"], 16 * ET)
                    sp.wait_ge(S["out_sc_done"], 16 * ET)
                    for h in range(2):
                        sp.wait_ge(attr_stored[h], 8 * CH)
                if p and j == 0:
                    if m >= 2 and STEPS[m - 2][0] >= 1:
                        sp.wait_ge(S["agg_ready"], m - 1)
                        sp.wait_ge(S["piece_used"], (m - 1) * PIECES)
                    row = 0 if p <= LAYERS else 1
                    sp.dma_start(scale_row(m, w), deg_rows[row:row + 1, c0:c0 + w].to_broadcast([128, w])).then_inc(rows_in[m % 2], 16)
                    if p <= LAYERS:
                        sp.dma_start(sums_row(m, w), sums_T[:, c0:c0 + w]).then_inc(rows_in[m % 2], 16)
                n = m * PIECES + j
                to = slot(m, j, wide)
                if p == 0:
                    view = in_v if what == "in" else out_v
                    for i_ in range(ROWS):
                        if n >= 2:
                            if i_ < ROWS - 1:
                                sp.wait_ge(S["row_used"], (n - 2) * (ROWS - 1) + i_ + 1)
                            else:
                                sp.wait_ge(S["piece_used"], n - 1)
                        if what == "in":
                            a, cc, ww = to[:, i_].rearrange("p n c -> p (n c)"), 2 * c0, 2 * w
                        else:
                            a, cc, ww = to[:, i_], c0, w
                        sp.dma_start(a, view[:, j * ROWS + i_, cc:cc + ww]).then_inc(row_in[(n % 2) * ROWS + i_], 16)
                    return
                back = 2 if wide else PIECES
                if not ((p, r) == (1, 0) and j < back):
                    sp.wait_ge(S["piece_used"], n - back + 1)
                view = in_v if wide else count_v
                if wide:
                    to, c0, w = to.rearrange("p t n c -> p t (n c)"), 2 * c0, 2 * w
                sp.dma_start(to, view[:, j * ROWS:(j + 1) * ROWS, c0:c0 + w]).then_inc(load_in[LOAD[wide, m, j][0]], 16)

            def degrees():
                load_tables()
                for c in range(2):
                    sp.wait_ge(count_stored[c], 16 * ((NR * PIECES + 1 - c) // 2))
                sp.wait_ge(S["piece_used"], 2 * NR * PIECES)
                sp.wait_ge(S["tr_read"], TR_AT["deg"])
                sp.dma_start(sums_T, sumsT_s).then_inc(S["deg_rows_out"], 16)
                for c in range(2):
                    sp.dma_start(deg_rows[c].rearrange("(t p) -> t p", p=P), degT_s[:, c, 0:P]).then_inc(S["deg_rows_out"], 16)
                sp.wait_ge(S["deg_rows_out"], 48)
                sp.wait_ge(S["out_done"], OUT_AT[0, NR - 1, "O", RANGES[-1][1] - 1])
                for a, wt in ((w_pre, W_pre), (w_1, W1), (w_2, W2), (w_post, W_post), (w_3, W3)):
                    sp.dma_start(a, wv(wt)).then_inc(S["w2_in"], 16)

            def end(wide):
                for t in range(NT):
                    sp.wait_ge(S["norm_ready"], NORM_AT["F", t])
                    sp.dma_start(out[t * P:(t + 1) * P, :], Xn[:, t]).then_inc(S["y_stored"], 16)
                sp.wait_ge(S["y_stored"], 16 * NT)

            run_schedule(sp, piece, lambda *_: None, degrees=degrees, end=end)

        @block.gpsimd
        def _(pool):
            pool.memset(ident[:, :], 0.0).then_inc(S["mask_step"], 1)
            pool.memset(upper_f, 1.0).then_inc(S["mask_step"], 1)
            pool.iota(own, pattern=[[0, 1]], base=0, channel_multiplier=1, allow_small_or_imprecise_dtypes=True).then_inc(S["masks"], 1)
            pool.wait_ge(S["mask_step"], 2)
            pool.affine_select(out=ident[:, :], in_=ident[:, :], compare_op=ALU.not_equal, fill=1.0,
                               base=0, pattern=[[-1, 128]], channel_multiplier=1).then_inc(S["masks"], 1)
            pool.affine_select(out=upper_f, in_=upper_f, compare_op=ALU.is_gt, fill=0.0,
                               base=0, pattern=[[1, P]], channel_multiplier=-1).then_inc(S["masks"], 1)
            pool.wait_ge(S["masks"], 3)
            pool.tensor_copy(upper, upper_f).then_inc(S["ident16_ready"], 1)
            pool.tensor_copy(ident16[:, :], ident[:, :]).then_inc(S["ident16_ready"], 1)
            pool.wait_ge(S["zero_in"], 16 * Z_IN)
            pool.wait_ge(S["zero_out"], 16 * Z_OUT)

            def chunk(c, h, first):
                turn = pool.to_reg(c * 5 + 5)
                done = [pool.to_reg(c * (16 * EC) + 16 * k) for k in range(0, EC, QUAD)]
                pool.wait_ge(S["masks"], 3)
                pool.wait_ge(S["at_ready"], turn)
                for quad in range(EC // QUAD):
                    for s, mat, at, v in (("in_done", in_mat, at_in, val_in[h]),
                                          ("out_sc_done", out_mat, at_out, val_out[h].unsqueeze(2))):
                        if quad or h or not first:
                            pool.wait_ge(S["masks"], 3)
                            pool.wait_ge(S[s], done[quad])
                        for k in range(QUAD * quad, QUAD * quad + QUAD):
                            pool.indirect_dma_start(out=mat, out_offset=bass.IndirectOffsetOnAxis(ap=at[h][:, k:k + 1], axis=0),
                                                    in_=v[:, k], in_offset=None, compute_op=ALU.add).then_inc(S[s], 16)
            for h in range(2):
                chunk(h, h, True)
            with pool.Fori(1, CH // 2) as i:
                for h in range(2):
                    chunk(i * 2 + h, h, False)

            for h in range(2):
                pool.wait_ge(attr_stored[h], 8 * CH)
            pool.wait_ge(S["zero_sum"], 16 * SUMS)
            pool.dma_start(sc_val[0], attr_val[:, 0:SC * AW]).then_inc(sc_in[0], 16)

            def sums(c, h, first, last):
                done = [pool.to_reg(c * (16 * SC // SUMS) + 16 * g) for g in range(SC // SUMS)]
                here, turn = pool.to_reg((c + (2 - h)) * 8), pool.to_reg(c + 1)
                pool.wait_ge(S["masks"], 3)
                pool.wait_ge(sc_in[h], here)
                pool.wait_ge(S["sc_at"], turn)
                for k in range(SC):
                    if k >= SUMS or h or not first:
                        pool.wait_ge(S["masks"], 3)
                        pool.wait_ge(sc_done[k % SUMS], done[k // SUMS])
                    pool.indirect_dma_start(out=sum_tab[k % SUMS],
                                            out_offset=bass.IndirectOffsetOnAxis(ap=at_sum_now[h][:, k:k + 1], axis=0),
                                            in_=sc_val[h][:, k * AW:(k + 1) * AW], in_offset=None,
                                            compute_op=ALU.add).then_inc(sc_done[k % SUMS], 16)
                    if k == SUMS - 1 and not last:
                        pool.dma_start(sc_val[1 - h], attr_val[:, bass.ds((c + 1) * (SC * AW), SC * AW)]).then_inc(sc_in[1 - h], 16)
                        pool.tensor_copy(at_sum_now[1 - h], at_sum[:, bass.ds((c + 1) * SC, SC)]).then_inc(S["sc_at"], 1)
            pool.tensor_copy(at_sum_now[0], at_sum[:, 0:SC]).then_inc(S["sc_at"], 1)
            for h in range(2):
                sums(h, h, True, False)
            with pool.Fori(1, ET // SC // 2 - 1) as i:
                for h in range(2):
                    sums(i * 2 + h, h, False, False)
            for h in range(2):
                sums(ET // SC - 2 + h, h, False, h == 1)

        @block.scalar
        def _(act):
            act.wait_ge(S["raw_in"], 16 * 3 * LAYERS)
            act.wait_ge(S["zeros"], 1)
            for mat, n, s in ((in_mat, Z_IN, "zero_in"), (out_mat, Z_OUT, "zero_out")):
                flat = mat.rearrange("a b -> (a b)")
                for j in range(n):
                    act.dma_start(flat[j * SLAB:(j + 1) * SLAB].rearrange("(p k a) -> p k a", p=128, k=REPEAT),
                                  zero_block.unsqueeze(1).to_broadcast([128, REPEAT, ZERO])).then_inc(S[s], 16)
            for i_, v in enumerate((b_pre, b1, b2, b3, gamma3, beta3)):
                act.dma_start(cols[:, i_, :], v.rearrange("(h p) -> p h", p=128), allow_slow_non_contiguous=True).then_inc(S["ocol"], 16)
            for i_ in range(2 * LAYERS):
                act.wait_ge(S["tr_done"], TR_AT["w%d" % i_])
                wt = (w_lT if i_ < LAYERS else w_rT)[i_ % LAYERS]
                act.activation(wt, trp[:, i_ % 2, :].rearrange("p (k n) -> p k n", k=2), ACT.Copy).then_inc(S["tr_read"], 1)
            for l in range(LAYERS):
                act.wait_ge(S["tr_done"], TR_AT["w%d" % (2 * LAYERS + l)])
                act.activation(wE[0:EA, l * D:(l + 1) * D], trp[0:EA, l % 2, 0:D], ACT.Copy).then_inc(S["tr_read"], 1)
            act.wait_ge(S["stat"], 1)
            act.activation(var_b, var_b, ACT.Sqrt, bias=eps[0:P, :]).then_inc(S["stat"], 1)
            for t in range(NT):
                act.wait_ge(S["tr_done"], TR_AT["feat", t])
                act.activation(hT(t), trp[:, t % 2, 0:2 * P].rearrange("p (h n) -> p h n", h=2), ACT.Copy).then_inc(S["tr_read"], 1)
                act.wait_ge(S["out_done"], OUT_AT["feat", t])
                act.activation(Bn[0][:, t], outp(t)[:, 0:D], ACT.Copy).then_inc(S["nat_ready"], 1)
                act.activation(Bn[1][:, t], outp(t)[:, D:2 * D], ACT.Copy).then_inc(S["out_read"], 1)
            act.wait_ge(S["edges_ready"], 1)

            def spread(c):
                now = bass.ds(EC * c, EC)
                act.activation(cell_b, cell_in[:, now].unsqueeze(2).to_broadcast([P, EC, P]), ACT.Copy).then_inc(S["bcast"], 1)
                act.activation(dst_b, dst_f[:, now].unsqueeze(2).to_broadcast([P, EC, P]), ACT.Copy).then_inc(S["bcast"], 1)

            def chunk(c, h, first, last=False):
                if not last:
                    act.wait_ge(S["cell_T"], c + 1)
                    spread(c + 1)
                act.wait_ge(S["sums_done"], c + 1)
                if not first:
                    act.wait_ge(attr_stored[h], (c - h) * 8)
                act.activation(val_attr[h].rearrange("p (b k n) -> p b k n", b=2, k=4), sum_attr, ACT.Copy).then_inc(S["vals_ready"], 1)
                act.wait_ge(S["vals_ready"], c + 1)
                act.dma_start(attr_val[:, bass.ds(c * (EC * AW), EC * AW)], val_attr[h]).then_inc(attr_stored[h], 16)
            spread(0)
            for h in range(2):
                chunk(h, h, True)
            with act.Fori(1, CH // 2 - 1) as i:
                for h in range(2):
                    chunk(i * 2 + h, h, False)
            for h in range(2):
                chunk(CH - 2 + h, h, False, h == 1)

            def high_parts(m, j):
                p, r, what = STEPS[m]
                w, c0 = RANGES[r][1] * P, RANGES[r][0] * P
                n = m * PIECES + j
                values = slot(m, j)[:, :, :, 1] if what == "in" else slot(m, j)
                q = (m // 2) * PIECES + j
                if what == "in" and q >= 2:
                    act.wait_ge(count_stored[q % 2], 16 * (q // 2))
                    act.wait_ge(S["count_max"], q - 1)
                def landed_(i_):
                    act.wait_ge(row_in[(n % 2) * ROWS + i_], 16 * (n // 2 + 1))

                def count(i_):
                    landed_(i_)
                    act.activation(count_s[:, q % 2, i_, 0:w], slot(m, j)[:, i_, :, 0], ACT.Copy).then_inc(S["count_copied"], 1)

                for i_ in range(ROWS):
                    if what == "in":
                        for k in ((0, 1) if i_ == 0 else (i_ + 1,)):
                            if k < ROWS:
                                count(k)
                        act.wait_ge(S["count_copied"], q * ROWS + i_ + 1)
                    else:
                        landed_(i_)
                    act.activation(split_slot(m, j)[:, i_, :, 0], values[:, i_], ACT.Copy, scale=scale0[0:P, 1:2]).then_inc(S["hi_ready"], 1)
                if what == "in":
                    act.wait_ge(S["count_copied"], (q + 1) * ROWS)
                    act.dma_start(count_v[:, j * ROWS:(j + 1) * ROWS, c0:c0 + w], count_s[:, q % 2, :, 0:w]).then_inc(count_stored[q % 2], 16)

            def piece(m, j, wide):
                ahead(high_parts, m, j)

            def evac_T(p, r, s, to, col=None):
                w = RANGES[r][1] * P
                act.wait_ge(S["tr_done"], TR_AT[p, r, s])
                if col is None:
                    act.activation(to[:, :, 0:w], trp[:, :, 0:w], ACT.Copy).then_inc(S["tr_read"], 1)
                else:
                    act.activation(to[:, 0, 0:w], trp[:, 0, 0:w], ACT.Identity, bias=col[:, 0:1])
                    act.activation(to[:, 1, 0:w], trp[:, 1, 0:w], ACT.Identity, bias=col[:, 1:2]).then_inc(S["tr_read"], 1)

            def stage(p, r, s, wide):
                t0, nt = RANGES[r]
                m = LAST_OF[p, r]
                w = nt * P
                if s == "A" and p in (4, 5):
                    act.wait_ge(S["agg_ready"], m + 1)
                    if (p, r) == (4, 0):
                        act.wait_ge(S["ocol"], 16 * 6)
                    c = c_1 if p == 4 else c_2
                    act.activation(agg[:, m % 2, 0, 0:w], agg[:, m % 2, 0, 0:w], ACT.Relu, bias=c[:, 0:1])
                    act.activation(agg[:, m % 2, 1, 0:w], agg[:, m % 2, 1, 0:w], ACT.Relu, bias=c[:, 1:2]).then_inc(S["agr_ready"], 1)
                if s == "A" and p == 6:
                    act.wait_ge(S["agg_ready"], m + 1)
                    for hh in range(2):
                        last = act.activation(outT[:, hh, t0 * P:t0 * P + w], agg[:, m % 2, hh, 0:w], ACT.Identity, bias=c_3[:, hh:hh + 1])
                    last.then_inc(S["agr_ready"], 1)
                if s == "T" and p <= 3:
                    evac_T(p, r, "T", xT)
                if s == "O" and p <= 5:
                    for k in range(nt):
                        n = OUT_AT[p, r, "O", k]
                        act.wait_ge(S["out_done"], n)
                        o = outp(n)
                        if p in (0, 3, 5):
                            g = GATE_AT[p, r, k]
                            if g > 2:
                                act.wait_ge(S["gate_used"], g - 2)
                        if p == 0:
                            act.activation(gate[0:P, k % 2, 0:D], o[:, 0:D], ACT.Sigmoid)
                            act.activation(gate[0:P, k % 2, D:2 * D], o[:, D:2 * D], ACT.Tanh).then_inc(S["gates"], 1)
                        elif p in (3, 5):
                            act.activation(gate[0:P, k % 2, 0:D], o[:, 0:D], ACT.Relu if p == 3 else ACT.Copy).then_inc(S["gates"], 1)
                        elif p in (1, 2):
                            act.activation(Bn[p - 1][:, t0 + k], o[:, 0:D], ACT.Relu).then_inc(S["nat_ready"], 1)
                        else:
                            act.activation(Bn[1][:, t0 + k], o[:, 0:D], ACT.Copy, scale=dinv[:, t0 + k:t0 + k + 1]).then_inc(S["nat_ready"], 1)
                if s == "N" and p in (0, 3, 5):
                    act.wait_ge(S["mv_ready"], NORM_AT[p, r])
                    act.activation(std[:, 0:nt], mv[:, 0:nt, 1], ACT.Sqrt, bias=eps[0:P, :]).then_inc(S["std_ready"], 1)
                if s == "T2" and p in (3, 5):
                    evac_T(p, r, "T2", xT)
                if s == "O2" and p in (3, 5):
                    for k in range(nt):
                        n = OUT_AT[p, r, "O2", k]
                        act.wait_ge(S["out_done"], n)
                        act.activation(Bn[0][:, t0 + k], outp(n)[:, 0:D], ACT.Copy, scale=dinv[:, t0 + k:t0 + k + 1]).then_inc(S["nat_ready"], 1)

            def degrees():
                for r, (t0, nt) in enumerate(RANGES):
                    act.wait_ge(S["tr_done"], TR_AT["sums", r])
                    act.activation(sumsT_s[:, t0 * P:(t0 + nt) * P], trp[0:AW, r % 2, 0:nt * P], ACT.Copy).then_inc(S["tr_read"], 1)
                act.wait_ge(S["deg_step"], SUMS)
                act.activation(root, deg, ACT.Sqrt, bias=1.0).then_inc(S["stat"], 1)

            def begin(p, wide):
                if p == 2:
                    act.wait_ge(S["tr_done"], TR_AT["W_pre"])
                    act.activation(w_preT, trp[:, :, 0:D], ACT.Copy).then_inc(S["tr_read"], 1)
                    act.wait_ge(S["tr_done"], TR_AT["fold"])
                    act.activation(w_fold, trp[:, :, 0:D], ACT.Copy).then_inc(S["tr_read"], 1)
                if wide:
                    return
                if p == 1:
                    act.wait_ge(S["norm_ready"], NORM_AT[0, NR - 1])
                else:
                    act.wait_ge(S["nat_ready"], NAT_AT[p - 1, NR - 1, RANGES[-1][1] - 1])
                act.wait_ge(S["scale_ready"], p)
                act.wait_ge(S["piece_used"], (7 * (p - 1) + 14) * PIECES)
                for j in range(PIECES):
                    now = slice(j * ROWS, (j + 1) * ROWS)
                    act.activation(parts[:, 0, now], SRC[p][:, now], ACT.Copy, scale=scale[0:P, :]).then_inc(S["split_hi"], 1)

            def end(wide):
                act.wait_ge(S["fin_ready"], 1)
                act.activation(std3, mv3[:, :, 1], ACT.Sqrt, bias=eps).then_inc(S["fin_ready"], 1)
                act.wait_ge(S["fin_ready"], 3)
                for r, (t0, nt) in enumerate(RANGES):
                    for hh in range(2):
                        v = outT[:, hh, t0 * P:(t0 + nt) * P]
                        last = act.activation(v, v, ACT.Relu, bias=shift3[:, hh:hh + 1], scale=scale3[:, hh:hh + 1])
                    last.then_inc(S["outT_ready"], 1)
                def normalise(r):
                    t0, nt = RANGES[r]
                    act.wait_ge(S["last_scales"], r + 1)
                    for k in range(nt):
                        act.activation(Xn[:, t0 + k], Xn[:, t0 + k], ACT.Identity, bias=last_shift[r % 2][:, k:k + 1],
                                       scale=last_rstd[r % 2][:, k:k + 1]).then_inc(S["norm_ready"], 1)
                for r, (t0, nt) in enumerate(RANGES):
                    act.wait_ge(S["mv_ready"], len(NORM) + r + 1)
                    act.activation(last_std[r % 2][:, 0:nt], last_mv[r % 2][:, 0:nt, 1], ACT.Sqrt, bias=eps[0:P, :]).then_inc(S["std_ready"], 1)
                    if r:
                        normalise(r - 1)
                normalise(NR - 1)

            for q in range(SUMS):
                half = (N + P) * AW // P // 2
                act.dma_start(sum_tab[q].rearrange("(p a) b -> p (a b)", p=P).rearrange("p (k a) -> p k a", k=2),
                              zero_block[0:P, 0:half].unsqueeze(1).to_broadcast([P, 2, half])).then_inc(S["zero_sum"], 16)
            act.wait_ge(S["scale0_ready"], 1)
            for n in range(2 * PIECES):
                if n >= 2:
                    act.wait_ge(S["feat_split"], n - 1)
                b, g = divmod(n, PIECES)
                act.activation(hi_tmp[n % 2], Bn[b][:, g * ROWS:(g + 1) * ROWS], ACT.Copy, scale=scale0[0:P, 0:1]).then_inc(S["feat_hi"], 1)

            run_schedule(act, piece, stage, degrees=degrees, begin=begin, end=end)

        @block.tensor
        def _(pe):
            pe.wait_ge(S["masks"], 3)
            pe.wait_ge(S["ident16_ready"], 2)
            pe.wait_ge(S["raw_in"], 16 * 3 * LAYERS)
            for i_ in range(2 * LAYERS):
                raw = (raw_l if i_ < LAYERS else raw_r)[:, i_ % LAYERS]
                if i_ >= 2:
                    pe.wait_ge(S["tr_read"], i_ - 1)
                for k in range(2):
                    for o in range(2):
                        last = pe.transpose(trp[:, i_ % 2, k * D + o * 128:k * D + (o + 1) * 128], raw[:, o, k * 128:(k + 1) * 128], ident[:, :])
                last.then_inc(S["tr_done"], 1)
            for l in range(LAYERS):
                pe.wait_ge(S["tr_read"], 2 * LAYERS + l - 1)
                for o in range(2):
                    last = pe.transpose(trp[0:EA, l % 2, o * 128:(o + 1) * 128], raw_e[:, l, o, :], ident[:, :])
                last.then_inc(S["tr_done"], 1)
            pe.wait_ge(S["ones_ready"], 1)
            pe.wait_ge(S["x_in"], 48)
            for t in range(NT):
                last = pe.matmul(outp(0)[:, 0:D], ones, Xn[:, t], start=t == 0, stop=t == NT - 1)
            last.then_inc(S["out_done"], 1)
            pe.wait_ge(S["ones_ready"], 3)
            for t in range(NT):
                last = pe.matmul(outp(1)[:, 0:D], ones, Bn[1][:, t], start=t == 0, stop=t == NT - 1)
            last.then_inc(S["out_done"], 1)
            pe.wait_ge(S["stat"], 3)
            pe.wait_ge(S["w_in"], 16 * 26)
            pe.wait_ge(S["bias_ready"], 1)
            for t in range(NT + 1):
                if t < NT:
                    if t < 2:
                        pe.wait_ge(S["tr_read"], 3 * LAYERS)
                    else:
                        pe.wait_ge(S["tr_read"], TR_AT["feat", t - 2])
                    for hh in range(2):
                        last = pe.transpose(trp[:, t % 2, hh * P:(hh + 1) * P], Bn[2][:, t, hh * 128:(hh + 1) * 128], ident[0:P, 0:P])
                    last.then_inc(S["tr_done"], 1)
                if t:
                    u = t - 1
                    pe.wait_ge(S["tr_read"], TR_AT["feat", u])
                    if u >= 2:
                        pe.wait_ge(S["out_read"], u - 1)
                    for hh in range(2):
                        pe.matmul(outp(u), hT(u)[:, hh], w_io[:, hh], start=hh == 0, stop=False)
                    pe.matmul(outp(u), pick[:, 0:1].to_broadcast([96, P]), bias16[:, :], start=False, stop=True).then_inc(S["out_done"], 1)

            pe.wait_ge(S["out_read"], NT)
            def chunk(c, h, first):
                pe.wait_ge(S["bcast"], c * 2 + 2)
                if h or not first:
                    pe.wait_ge(S["eq_ready"], c)
                    pe.wait_ge(S["eq_step"], c * CHUNK_STEPS)
                for k in range(EC):
                    pe.transpose(cellT[:, k // 4, k % 4], cell_b[:, k], ident[0:P, 0:P])
                for k in range(EC):
                    last = pe.transpose(dstT[:, k // 4, k % 4], dst_b[:, k], ident[0:P, 0:P])
                last.then_inc(S["cell_T"], 1)
                if not first:
                    pe.wait_ge(S["at_ready"], (c - 1) * 5)
                for a in range(EC):
                    q = a // QUAD * QUAD
                    if a == q:
                        pe.wait_ge(S["eq_step"], c * CHUNK_STEPS + 1 + a // QUAD)
                    for b in range(q, q + QUAD):
                        n = 10 if b < a else 9
                        pe.matmul(sum_w[h][:, a, 0:n], same_cell[:, b, a - q], weights[:, bass.ds(EC * c + b, 1), 0:n],
                                  start=(a == 0 and b == 0), stop=False, skip_group_check=True)
                pe.wait_ge(S["eq_ready"], c + 1)
                pe.wait_ge(attr_in[h], (c + (2 - h)) * 8)
                if h or not first:
                    pe.wait_ge(S["vals_ready"], c)
                for k in range(EC):
                    pe.matmul(sum_attr[:, k // 4, k % 4], same_dst[:, k], attr[h][:, k], start=(k % 4 == 0), stop=True, skip_group_check=True)
                pe.wait_ge(S["eq_step"], c * CHUNK_STEPS + 4)
                for k in range(EC):
                    pe.matmul(sum_w[h][:, k, 9:10], before_cell[:, k], weights[:, 0, 0:1], start=False, stop=True, skip_group_check=True)
                    last = pe.matmul(n_dst[h][:, k:k + 1], before_dst[:, k], weights[:, 0, 0:1], start=False, stop=True, skip_group_check=True)
                last.then_inc(S["sums_done"], 1)
            for h in range(2):
                chunk(h, h, True)
            with pe.Fori(1, CH // 2) as i:
                for h in range(2):
                    chunk(i * 2 + h, h, False)
            pe.wait_ge(S["vals_ready"], CH)
            pe.wait_ge(S["at_ready"], 5 * CH)
            pe.wait_ge(S["tr_read"], TR_AT["feat", NT - 1])
            pe.wait_ge(S["peak_ready"], 1)
            for b in range(2):
                last = pe.transpose(trp[0:1, b, 0:P], peak[:, b:b + 1], ident[0:P, 0:P])
            last.then_inc(S["tr_done"], 1)
            pe.wait_ge(S["tr_read"], TR_AT["peak"])
            pe.matmul(trp[:, 0, 0:2], ident[0:1, 0:1].to_broadcast([1, 128]), power2[0:1, :], start=True, stop=True).then_inc(S["tr_done"], 1)

            def piece(m, j, wide):
                p, r, what = STEPS[m]
                t0, nt = RANGES[r]
                w = nt * P
                source = None if p == 0 else SRC[p]
                if j == 0:
                    if m >= 2:
                        pe.wait_ge(S["agg_ready"], m - 1)
                    if r == 0 and p == 1 and wide:
                        pe.wait_ge(S["norm_ready"], NORM_AT[0, NR - 1])
                    elif r == 0 and p > 1 and wide:
                        pe.wait_ge(S["nat_ready"], NAT_AT[p - 1, NR - 1, RANGES[-1][1] - 1])
                if p:
                    s, v = LOAD[wide, m, j]
                    pe.wait_ge(load_in[s], v)
                elif r == 0:
                    pe.wait_ge(S["feat_split"], j + 1 + (PIECES if what == "out" else 0))
                a = acc(m)
                rhs = slot(m, j, wide)
                if p and r == 0 and not wide:
                    pe.wait_ge(S["split_lo"], (p - 1) * PIECES + j + 1)
                for i_ in range(ROWS):
                    t = j * ROWS + i_
                    if p == 0:
                        pe.wait_ge(S["lo_ready"], m * NT + t + 1)
                    for hh in range(2):
                        f = slice(hh * 128, (hh + 1) * 128)
                        if p == 0:
                            for k, (c, d) in enumerate(((0, 0), (0, 1), (1, 0))):
                                last = pe.matmul(a[:, hh, 0:w], halves[what == "out"][:, t, f, c], split_slot(m, j)[:, i_, :, d],
                                                 start=t == 0 and k == 0, stop=t == NT - 1 and k == 2, skip_group_check=True)
                        elif not wide:
                            for c in range(2):
                                last = pe.matmul(a[:, hh, 0:w], parts[:, c, t, f], rhs[:, i_, :],
                                                 start=t == 0 and c == 0, stop=t == NT - 1 and c == 1, skip_group_check=True)
                        else:
                            last = pe.matmul(a[:, hh, 0:w], source[:, t, f], rhs[:, i_, :, 0],
                                             start=t == 0, stop=t == NT - 1, skip_group_check=True)
                    if p == 0 and i_ < ROWS - 1:
                        last.then_inc(S["row_used"], 1)
                    if t == NT - 2 and p >= 4:
                        for hh in range(2):
                            for k in range(nt):
                                f = slice(hh * 128, (hh + 1) * 128)
                                for own_rows, one in ([(source[:, t0 + k, f], ident)] if wide else
                                                      [(parts[:, c, t0 + k, f], ident16) for c in range(2)]):
                                    pe.matmul(a[:, hh, k * P:(k + 1) * P], own_rows, one[0:P, 0:P],
                                              start=False, stop=False, skip_group_check=True)
                    if t == NT - 2 and 1 <= p <= LAYERS:
                        pe.wait_ge(rows_in[m % 2], ROW_AT[m])
                        pe.wait_ge(S["wE_ready"], p)
                        for hh in range(2):
                            pe.matmul(a[:, hh, 0:w], wE_s[:, hh * 128:(hh + 1) * 128], sums_row(m, w),
                                      start=False, stop=False, skip_group_check=True)
                last.then_inc(S["piece_used"], 1)

            def transposes(p, r, s, from_):
                t0, nt = RANGES[r]
                pe.wait_ge(S["tr_read"], TR_AT[p, r, s] - 1)
                for hh in range(2):
                    for k in range(nt):
                        last = pe.transpose(trp[:, hh, k * P:(k + 1) * P], from_[:, t0 + k, hh * 128:(hh + 1) * 128], ident[0:P, 0:P])
                last.then_inc(S["tr_done"], 1)

            def stage(p, r, s, wide):
                t0, nt = RANGES[r]
                m = LAST_OF[p, r]
                w = nt * P
                if s == "T" and p <= 3:
                    transposes(p, r, s, Bn[2] if p == 0 else SRC[p])
                if s == "T2" and p in (3, 5):
                    pe.wait_ge(S["norm_ready"], NORM_AT[p, r])
                    transposes(p, r, s, Xn)
                if s in OUTS[p]:
                    ag = agg[:, m % 2]
                    bias = None
                    if p == 0:
                        pe.wait_ge(S["agg_ready"], m + 1)
                        pe.wait_ge(S["tr_read"], TR_AT[p, r, "T"])
                        ops = [(agg[:, 0, hh], w_x2i[:, hh]) for hh in range(2)] + [(agg[:, 1, hh], w_x2i[:, 2 + hh]) for hh in range(2)] \
                            + [(xT[:, hh], w_h2h[:, hh]) for hh in range(2)]
                        bias = "x2i"
                    elif p <= 3 and s == "O":
                        pe.wait_ge(S["agg_ready"], m + 1)
                        pe.wait_ge(S["tr_read"], TR_AT[p, r, "T"])
                        ops = [(ag[:, hh], w_lT[p - 1][:, hh]) for hh in range(2)] + [(xT[:, hh], w_rT[p - 1][:, hh]) for hh in range(2)]
                        bias = p - 1
                    elif p == 3:
                        pe.wait_ge(S["tr_read"], TR_AT[p, r, "T2"])
                        ops = [(xT[:, hh], w_fold[:, hh]) for hh in range(2)]
                        bias = "fold"
                    elif p == 4:
                        pe.wait_ge(S["agr_ready"], AGR_AT[p, r])
                        ops = [(ag[:, hh], w_2[:, hh]) for hh in range(2)]
                    elif s == "O":
                        pe.wait_ge(S["agr_ready"], AGR_AT[p, r])
                        ops = [(ag[:, hh], w_post[:, hh]) for hh in range(2)]
                        bias = "post"
                    else:
                        pe.wait_ge(S["tr_read"], TR_AT[p, r, "T2"])
                        ops = [(xT[:, hh], w_3[:, hh]) for hh in range(2)]
                    n_out = 2 * D if p == 0 else D
                    for k in range(nt):
                        n = OUT_AT[p, r, s, k]
                        wait_out(n)
                        o = outp(n)[:, 0:n_out]
                        for q, (a, wt) in enumerate(ops):
                            last = pe.matmul(o, a[:, k * P:(k + 1) * P], wt, start=q == 0, stop=bias is None and q == len(ops) - 1)
                        if bias is not None:
                            b = bias_row[bias]
                            last = pe.matmul(o, pick[:, b:b + 1].to_broadcast([96, P]), bias16[:, 0:n_out], start=False, stop=True)
                        last.then_inc(S["out_done"], 1)

            readers = {}
            for (p_, r_, s_, k_) in [e for e in OUT_AT if isinstance(e, tuple) and len(e) == 4]:
                n_ = OUT_AT[p_, r_, s_, k_]
                readers[n_] = ("gates", GATE_AT[p_, r_, k_]) if s_ == "O" and p_ in (0, 3, 5) else ("nat_ready", NAT_AT[p_, r_, k_])

            def wait_out(n):
                if n - 2 in readers:
                    s_, v_ = readers[n - 2]
                    pe.wait_ge(S[s_], v_)

            def degrees():
                for r, (t0, nt) in enumerate(RANGES):
                    pe.wait_ge(S["tr_read"], TR_AT["sums", r] - 2)
                    if r == 0:
                        pe.wait_ge(S["deg_step"], SUMS - 1)
                    for k in range(nt):
                        last = pe.transpose(trp[0:AW, r % 2, k * P:(k + 1) * P], tab[0][:, t0 + k], ident[0:P, 0:P])
                    last.then_inc(S["tr_done"], 1)
                pe.wait_ge(S["deg_step"], SUMS + 3)
                pe.wait_ge(S["tr_read"], TR_AT["sums", NR - 1])
                pe.transpose(trp[0:NT, 0, 0:P], inv_deg, ident[0:P, 0:P])
                pe.transpose(trp[0:NT, 1, 0:P], dinv, ident[0:P, 0:P]).then_inc(S["tr_done"], 1)
                pe.wait_ge(S["tr_read"], TR_AT["deg"])
                pe.wait_ge(S["deg_step"], SUMS + 4)
                pe.transpose(trp[0:1, 0, 0:P], top1, ident[0:P, 0:P]).then_inc(S["tr_done"], 1)

            def begin(p, wide):
                if p == 1:
                    return
                if p == 2:
                    pe.wait_ge(S["tr_read"], TR_AT["W_pre"] - 1)
                    pe.wait_ge(S["w2_in"], 16 * 5)
                    pe.wait_ge(S["ocol"], 16 * 6)
                    for a in range(2):
                        for b in range(2):
                            last = pe.transpose(trp[:, b, a * 128:(a + 1) * 128], w_pre[:, a, b * 128:(b + 1) * 128], ident[:, :])
                    last.then_inc(S["tr_done"], 1)
                    pe.wait_ge(S["tr_read"], TR_AT["W_pre"])
                    for a in range(2):
                        for b in range(2):
                            pe.matmul(trp[:, a, 0:D], w_preT[:, b, a * 128:(a + 1) * 128], w_1[:, b], start=b == 0, stop=b == 1)
                    for b in range(2):
                        last = pe.matmul(trp[0:96, 0, D:2 * D], c_pre[:, b:b + 1].to_broadcast([128, 96]), w_1[:, b], start=b == 0, stop=b == 1)
                    last.then_inc(S["tr_done"], 1)
                    pe.wait_ge(S["bias_ready"], 2)
                pe.wait_ge(S["tr_read"], TR_AT["M", p, 0] - 1)
                pe.wait_ge(S["max_ready"], p - 1)
                pe.transpose(trp[0:1, 0, 0:P], top1, ident[0:P, 0:P]).then_inc(S["tr_done"], 1)
                pe.wait_ge(S["tr_read"], TR_AT["M", p, 0])
                pe.matmul(trp[:, 1, 0:1], ident[0:1, 0:1].to_broadcast([1, 128]), most[0:1, :], start=True, stop=True).then_inc(S["tr_done"], 1)

            def end(wide):
                for t in range(NT):
                    r = t // WIDE
                    pe.wait_ge(S["outT_ready"], r + 1)
                    if t < 2:
                        pe.wait_ge(S["tr_read"], TR_AT["F", 0] - 1)
                    else:
                        pe.wait_ge(S["gate_used"], len(GATE_AT) + t - 1)
                    for hh in range(2):
                        last = pe.transpose(trp[0:P, t % 2, hh * 128:(hh + 1) * 128], outT[:, hh, t * P:(t + 1) * P], ident[:, :])
                    last.then_inc(S["tr_done"], 1)

            run_schedule(pe, piece, stage, degrees=degrees, begin=begin, end=end)

        @block.vector
        def _(dve):
            links, links_at_branch = [0], []

            def link(ins):
                links[0] += 1
                ins.then_inc(S["link_s"], 1)
                dve.wait_ge(S["link_s"], links[0])

            dve.memset(zero_block, 0.0).then_inc(S["zeros"], 1)
            dve.memset(ones, 1.0).then_inc(S["ones_ready"], 1)
            dve.memset(eps, EPS)
            dve.memset(brow[:, :], 0.0).then_inc(S["ones_ready"], 1)
            dve.memset(weights, 0.0).then_inc(S["w_step"], 1)
            dve.wait_ge(S["w_step"], 1)
            dve.memset(weights[:, :, 0:10:9], 1.0).then_inc(S["prep"], 1)
            dve.memset(attr[0][:, :, EA], 1.0).then_inc(S["prep"], 1)
            dve.memset(attr[1][:, :, EA], 1.0).then_inc(S["prep"], 1)
            dve.wait_ge(S["edges_in"], 64)
            dve.tensor_copy(src_f, src_i).then_inc(S["prep"], 1)
            dve.tensor_copy(dst_f, dst_i).then_inc(S["prep"], 1)
            for b, w_e in enumerate((w_e1, w_e2)):
                dve.tensor_reduce(peaks_w[:, 0, b:b + 1], w_e, AX.X, ALU.max)
                last = dve.tensor_reduce(peaks_w[:, 1, b:b + 1], w_e, AX.X, ALU.min)
            link(last)
            link(dve.tensor_scalar(peaks_w[:, 1], peaks_w[:, 1], -1.0, None, ALU.mult))
            step = 1
            for part in range(3):
                for w_e, col in ((w_e1, 3 + part), (w_e2, 6 + part)):
                    dve.tensor_copy(weights[:, :, col], w_e).then_inc(S["w_step"], 1)
                dve.wait_ge(S["w_step"], step + 2)
                if part < 2:
                    for w_e, col in ((w_e1, 3 + part), (w_e2, 6 + part)):
                        dve.tensor_tensor(w_e, w_e, weights[:, :, col], ALU.subtract).then_inc(S["w_step"], 1)
                    dve.wait_ge(S["w_step"], step + 4)
                step += 4
            dve.wait_ge(S["prep"], 5)
            dve.scalar_tensor_tensor(out=cell_in, in0=src_f, scalar=float(N), in1=dst_f, op0=ALU.mult, op1=ALU.add).then_inc(S["prep"], 1)
            dve.scalar_tensor_tensor(out=cell_out, in0=dst_f, scalar=float(N), in1=src_f, op0=ALU.mult, op1=ALU.add).then_inc(S["prep"], 1)
            dve.wait_ge(S["prep"], 7)
            dve.wait_ge(S["masks"], 3)
            for d, k, base in ((dump_in, cell_in, N * N), (dump_out, cell_out, N * N), (dump_dst, dst_f, N)):
                dve.tensor_scalar(d, k, -1.0, float(base), ALU.mult, ALU.add).then_inc(S["prep"], 1)
            dve.wait_ge(S["prep"], 10)
            for d in (dump_in, dump_out):
                for q in range(QUAD):
                    dq = d.rearrange("p (t q) -> p t q", q=QUAD)[:, :, q]
                    dve.tensor_scalar(dq, dq, own, float(P * q), ALU.add, ALU.add).then_inc(S["prep"], 1)
            dve.tensor_scalar(dump_dst, dump_dst, own, None, ALU.add).then_inc(S["prep"], 1)
            dve.wait_ge(S["prep"], 11 + 2 * QUAD)
            dve.wait_ge(S["w_in"], 16 * 26)
            part16 = [B[0][0:96, k * D:(k + 1) * D].bitcast(BF16) for k in range(3)]
            rest, pick_f = B[0][0:96, 3 * D:5 * D], B[0][0:96, 5 * D:5 * D + 6]
            link(dve.tensor_copy(part16[0], brow[:, :]))
            link(dve.tensor_tensor(rest, brow[:, :], part16[0], ALU.subtract))
            link(dve.tensor_copy(part16[1], rest))
            link(dve.tensor_tensor(rest, rest, part16[1], ALU.subtract))
            link(dve.tensor_copy(part16[2], rest))
            for k in range(3):
                dve.tensor_copy(bias16[32 * k:32 * k + 32, :], part16[k][32 * k:32 * k + 32, :])
            link(dve.tensor_tensor(pick_f, ident[0:96, 0:6], ident[0:96, 32:38], ALU.add))
            dve.tensor_tensor(pick, pick_f, ident[0:96, 64:70], ALU.add).then_inc(S["bias_ready"], 1)
            over = lambda v: v.unsqueeze(1).to_broadcast([P, NT, D])
            dve.wait_ge(S["out_done"], 1)
            link(dve.tensor_scalar(mean_b, outp(0)[:, 0:D], 1.0 / N, None, ALU.mult))
            link(dve.tensor_tensor(Bn[2], Xn, over(mean_b), ALU.subtract))
            dve.wait_ge(S["tr_done"], 3 * LAYERS)
            dve.tensor_tensor(Bn[1], Bn[2], Bn[2], ALU.mult).then_inc(S["ones_ready"], 1)
            dve.wait_ge(S["out_done"], 2)
            dve.tensor_scalar(var_b, outp(1)[:, 0:D], 1.0 / N, None, ALU.mult).then_inc(S["stat"], 1)
            dve.wait_ge(S["stat"], 2)
            link(dve.reciprocal(mean_b, var_b))
            link(dve.tensor_tensor(mean_b, mean_b, gamma_b, ALU.mult))
            link(dve.tensor_tensor(Bn[2], Bn[2], over(mean_b), ALU.mult))
            dve.tensor_tensor(Bn[2], Bn[2], over(beta_b), ALU.add).then_inc(S["stat"], 1)
            dve.wait_ge(S["stat"], 3)

            def feature_peaks(g):
                dve.wait_ge(S["nat_ready"], NAT_AT["feat", (g + 1) * ROWS - 1])
                dve.wait_ge(S["out_read"], (g + 1) * ROWS)
                for b in range(2):
                    v = Bn[b][:, g * ROWS:(g + 1) * ROWS]
                    dve.tensor_reduce(peaks_f[:, 0, g, b:b + 1], v, AX.XY, ALU.max)
                    last = dve.tensor_reduce(peaks_f[:, 1, g, b:b + 1], v, AX.XY, ALU.min)
                link(last)
            for g in range(PIECES - 1):
                feature_peaks(g)
            dve.memset(go_in, 0.0).then_inc(S["edges_ready"], 1)

            def chunk(c, h, first):
                now = bass.ds(EC * c, EC)
                dve.wait_ge(S["cell_T"], c + 1)
                if h or not first:
                    dve.wait_ge(S["sums_done"], c)
                for q in range(EC // QUAD):
                    own_cell = cell_in[:, bass.ds(EC * c + QUAD * q, QUAD)].unsqueeze(2).unsqueeze(3).to_broadcast([P, QUAD, QUAD, P])
                    dve.tensor_tensor(same_cell[:, QUAD * q:QUAD * q + QUAD], cellT[:, q].unsqueeze(1).to_broadcast([P, QUAD, QUAD, P]),
                                      own_cell, ALU.is_equal).then_inc(S["eq_step"], 1)
                dve.tensor_tensor(same_dst.rearrange("p (b k) n -> p b k n", b=2), dstT,
                                  dst_f[:, now].rearrange("p (b k) -> p b k", b=2).unsqueeze(3).to_broadcast([P, 2, 4, P]),
                                  ALU.is_equal).then_inc(S["eq_ready"], 1)
                dve.wait_ge(S["eq_step"], c * CHUNK_STEPS + 2)
                own_tile = same_cell.rearrange("p (q k) j n -> p q (k j) n", q=2)[:, :, 0:QUAD * QUAD:QUAD + 1]
                dve.tensor_tensor(before_cell.rearrange("p (q k) n -> p q k n", q=2), own_tile,
                                  upper.unsqueeze(1).unsqueeze(1).to_broadcast([P, 2, QUAD, P]), ALU.mult).then_inc(S["eq_step"], 1)
                dve.wait_ge(S["eq_ready"], c + 1)
                dve.tensor_tensor(before_dst, same_dst, upper.unsqueeze(1).to_broadcast([P, EC, P]), ALU.mult).then_inc(S["eq_step"], 1)
                dve.wait_ge(S["sums_done"], c + 1)
                n_cell = sum_w[h][:, :, 9]
                dve.scalar_tensor_tensor(out=go_in, in0=n_cell, scalar=1.0, in1=dump_in[:, now], op0=ALU.min, op1=ALU.mult).then_inc(S["eq_step"], 1)
                dve.scalar_tensor_tensor(out=go_out, in0=n_cell, scalar=1.0, in1=dump_out[:, now], op0=ALU.min, op1=ALU.mult).then_inc(S["eq_step"], 1)
                dve.scalar_tensor_tensor(out=go_dst, in0=n_dst[h], scalar=1.0, in1=dump_dst[:, now], op0=ALU.min, op1=ALU.mult).then_inc(S["eq_step"], 1)
                if not first:
                    dve.wait_ge(S["in_done"], (c - 1) * (16 * EC))
                    dve.wait_ge(S["out_sc_done"], (c - 1) * (16 * EC))
                dve.tensor_reduce(val_in[h], sum_w[h][:, :, 0:6].rearrange("p k (c i) -> p k c i", i=3), AX.X, ALU.add).then_inc(S["at_ready"], 1)
                dve.tensor_reduce(val_out[h], sum_w[h][:, :, 6:9], AX.X, ALU.add).then_inc(S["at_ready"], 1)
                dve.wait_ge(S["eq_step"], c * CHUNK_STEPS + 7)
                dve.tensor_tensor(at_in[h], go_in, cell_in[:, now], ALU.add).then_inc(S["at_ready"], 1)
                dve.tensor_tensor(at_out[h], go_out, cell_out[:, now], ALU.add).then_inc(S["at_ready"], 1)
                dve.tensor_tensor(at_sum[:, now], go_dst, dst_f[:, now], ALU.add).then_inc(S["at_ready"], 1)
                dve.wait_ge(S["at_ready"], c * 5 + 5)
            for h in range(2):
                chunk(h, h, True)
            with dve.Fori(1, CH // 2) as i:
                for h in range(2):
                    chunk(i * 2 + h, h, False)

            feature_peaks(PIECES - 1)
            link(dve.tensor_scalar(peaks_f[:, 1], peaks_f[:, 1], -1.0, None, ALU.mult))
            dve.tensor_reduce(peak[:, 0:1], st6_all[0:P, 0:4 * PIECES], AX.X, ALU.max)
            dve.tensor_reduce(peak[:, 1:2], st6_all[0:P, 4 * PIECES:4 * PIECES + 4], AX.X, ALU.max).then_inc(S["peak_ready"], 1)
            dve.wait_ge(S["tr_done"], TR_AT["peak"])
            dve.tensor_reduce(power2[0:1, :], trp[0:1, 0:2, 0:P], AX.X, ALU.max).then_inc(S["tr_read"], 1)
            dve.wait_ge(S["tr_done"], TR_AT["peak2"])
            dve.tensor_scalar(power2, trp[:, 0, 0:2], 2.0 ** -60, 2.0 ** 60, ALU.max, ALU.min).then_inc(S["tr_read"], 1)
            dve.wait_ge(S["tr_read"], TR_AT["peak2"])
            link(dve.tensor_scalar(power2.bitcast(I32), power2.bitcast(I32), 0x7F800000, None, ALU.bitwise_and))
            link(dve.tensor_scalar(scale0.bitcast(I32), power2.bitcast(I32), -1.0, float(254 << 23), ALU.mult, ALU.add))
            dve.tensor_scalar(unscale, power2[:, 0:1], power2[:, 1:2], 2.0 ** -14 / ROOM, ALU.mult, ALU.mult)
            dve.tensor_scalar(scale0[:, 0:1], scale0[:, 0:1], 2.0 ** 14, None, ALU.mult)
            link(dve.tensor_scalar(scale0[:, 1:2], scale0[:, 1:2], ROOM, None, ALU.mult))
            dve.sem_inc(S["scale0_ready"], 1)
            for n in range(2 * PIECES):
                b, g = divmod(n, PIECES)
                now = slice(g * ROWS, (g + 1) * ROWS)
                dve.wait_ge(S["feat_hi"], n + 1)
                link(dve.scalar_tensor_tensor(out=halves[b][:, now, :, 1], in0=Bn[b][:, now], scalar=scale0[0:P, 0:1], in1=hi_tmp[n % 2],
                                              op0=ALU.mult, op1=ALU.subtract))
                dve.tensor_copy(halves[b][:, now, :, 0], hi_tmp[n % 2]).then_inc(S["feat_split"], 1)

            def low_parts(m, j):
                what = STEPS[m][2]
                values = slot(m, j)[:, :, :, 1] if what == "in" else slot(m, j)
                parts_ = split_slot(m, j)
                for i_ in range(ROWS):
                    dve.wait_ge(S["hi_ready"], m * NT + j * ROWS + i_ + 1)
                    dve.scalar_tensor_tensor(out=parts_[:, i_, :, 1], in0=values[:, i_], scalar=scale0[0:P, 1:2], in1=parts_[:, i_, :, 0],
                                             op0=ALU.mult, op1=ALU.subtract).then_inc(S["lo_ready"], 1)

            def finish(m):
                p, r, what = STEPS[m]
                w = RANGES[r][1] * P
                dve.wait_ge(S["piece_used"], (m + 1) * PIECES)
                if m >= 2:
                    p2, r2, _ = STEPS[m - 2]
                    if p2 == 0:
                        if r2 < r or p != 0:
                            dve.wait_ge(S["out_done"], OUT_AT[0, r2, "O", RANGES[r2][1] - 1])
                    elif p2 < 6:
                        dve.wait_ge(S["out_done"], OUT_AT[p2, r2, OUTS[p2][-1], RANGES[r2][1] - 1])
                    else:
                        dve.wait_ge(S["agr_ready"], AGR_AT[p2, r2])
                if p == 0:
                    dve.tensor_scalar(agg[:, m % 2, :, 0:w], acc(m)[:, :, 0:w], unscale, None, ALU.mult).then_inc(S["agg_ready"], 1)
                else:
                    dve.wait_ge(rows_in[m % 2], ROW_AT[m])
                    dve.scalar_tensor_tensor(out=agg[:, m % 2, :, 0:w], in0=acc(m)[:, :, 0:w], scalar=unscale,
                                             in1=scale_row(m, w).unsqueeze(1).to_broadcast([128, 2, w]),
                                             op0=ALU.mult, op1=ALU.mult).then_inc(S["agg_ready"], 1)

            def stage(p, r, s, wide):
                t0, nt = RANGES[r]
                if s == "O" and p in (0, 3, 5):
                    for k in range(nt):
                        t = t0 + k
                        dve.wait_ge(S["gates"], GATE_AT[p, r, k])
                        g, n = gate[0:P, k % 2, 0:D], gate[0:P, k % 2, D:2 * D]
                        if p == 0:
                            h = Bn[2][:, t]
                            link(dve.tensor_tensor(h, h, n, ALU.subtract))
                            link(dve.tensor_tensor(h, h, g, ALU.mult))
                            dve.tensor_tensor(h, h, n, ALU.add).then_inc(S["gate_used"], 1)
                            dve.wait_ge(S["gate_used"], GATE_AT[p, r, k])
                            link(dve.tensor_tensor(Xn[:, t], Xn[:, t], h, ALU.add))
                        else:
                            dve.tensor_tensor(Xn[:, t], Xn[:, t], g, ALU.add).then_inc(S["gate_used"], 1)
                            dve.wait_ge(S["gate_used"], GATE_AT[p, r, k])
                        link(dve.bn_stats(bn6[:, k], Xn[:, t]))
                        last = dve.bn_aggr(mv[:, k], bn6[:, k])
                        if k == nt - 1:
                            last.then_inc(S["mv_ready"], 1)
                if s == "N" and p in (0, 3, 5):
                    dve.wait_ge(S["std_ready"], NORM_AT[p, r])
                    link(dve.reciprocal(rstd[:, 0:nt], std[:, 0:nt]))
                    for k in range(nt):
                        last = dve.tensor_scalar(Xn[:, t0 + k], Xn[:, t0 + k], mv[:, k, 0:1], rstd[:, k:k + 1], ALU.subtract, ALU.mult)
                    last.then_inc(S["norm_ready"], 1)
                if s == "X" and 1 <= p <= 5:
                    dve.wait_ge(S["nat_ready"], NAT_AT[p, r, nt - 1])
                    v = SRC[p + 1][:, t0:t0 + nt]
                    link(dve.tensor_reduce(top[:, r:r + 1], v, AX.XY, ALU.max))
                    link(dve.tensor_reduce(low_, v, AX.XY, ALU.min))
                    link(dve.tensor_scalar(top[:, NR + r:NR + r + 1], low_, -1.0, None, ALU.mult))
                if s == "A" and p == 6:
                    w = nt * P
                    dve.wait_ge(S["agr_ready"], AGR_AT[p, r])
                    for hh in range(2):
                        link(dve.bn_stats(st6[:, hh, r], outT[:, hh, t0 * P:t0 * P + w]))

            def degrees():
                dve.wait_ge(S["tab_in"], 16 * SUMS)
                for q in range(1, SUMS):
                    dve.tensor_tensor(tab[0], tab[0], tab[q], ALU.add).then_inc(S["deg_step"], 1)
                    dve.wait_ge(S["deg_step"], q)
                dve.tensor_copy(deg, tab[0][:, :, EA]).then_inc(S["deg_step"], 1)
                dve.wait_ge(S["deg_step"], SUMS)
                dve.tensor_scalar(inv_deg, deg, 1.0, None, ALU.max).then_inc(S["deg_step"], 1)
                dve.wait_ge(S["deg_step"], SUMS + 1)
                dve.reciprocal(inv_deg, inv_deg).then_inc(S["deg_step"], 1)
                dve.wait_ge(S["stat"], 4)
                dve.reciprocal(dinv, root).then_inc(S["deg_step"], 1)
                dve.wait_ge(S["tr_done"], TR_AT["deg"])
                dve.tensor_copy(degT_s[:, :, 0:P], trp[0:NT, 0:2, 0:P]).then_inc(S["tr_read"], 1)
                dve.tensor_reduce(top1, top_count, AX.X, ALU.max).then_inc(S["deg_step"], 1)
                dve.wait_ge(S["tr_done"], TR_AT["most"])
                link(dve.tensor_reduce(most[0:1, :], trp[0:1, 0, 0:P], AX.X, ALU.max))
                dve.tensor_copy(flag[0:1, :], most[0:1, :]).then_inc(S["flag_ready"], 1)
                dve.sem_inc(S["tr_read"], 1)

            def piece(m, j, wide):
                p, r, what = STEPS[m]
                ahead(low_parts, m, j)
                if what == "in":
                    q = (m // 2) * PIECES + j
                    dve.wait_ge(S["count_copied"], (q + 1) * ROWS)
                    dve.tensor_reduce(top_count[:, q:q + 1], count_s[:, q % 2, :, 0:RANGES[r][1] * P], AX.XY, ALU.max).then_inc(S["count_max"], 1)

            def degrees_and_count():
                degrees()
                links_at_branch.append(links[0])

            def begin(p, wide):
                if p == 1:
                    links[0] = links_at_branch[0]
                if p == 2:
                    v, rest2 = trp[0:96, 0, D:2 * D], gate[0:96, 1, D:2 * D]
                    a16 = [gate[0:96, 1, k * 128:(k + 1) * 128].bitcast(BF16) for k in range(2)]
                    dve.wait_ge(S["tr_done"], TR_AT["fold"])
                    dve.wait_ge(S["tr_read"], TR_AT["fold"])
                    link(dve.tensor_copy(a16[0], v))
                    link(dve.tensor_tensor(rest2, v, a16[0], ALU.subtract))
                    link(dve.tensor_copy(a16[1], rest2))
                    link(dve.tensor_tensor(rest2, rest2, a16[1], ALU.subtract))
                    dve.tensor_copy(bias16[0:1, 0:D], a16[0][0:1, :])
                    dve.tensor_copy(bias16[32:33, 0:D], a16[1][32:33, :])
                    dve.tensor_copy(bias16[64:65, 0:D], rest2[64:65, :]).then_inc(S["bias_ready"], 1)
                if p > 1:
                    dve.tensor_reduce(top1, top, AX.X, ALU.max).then_inc(S["max_ready"], 1)
                    dve.wait_ge(S["tr_done"], TR_AT["M", p, 0])
                    dve.tensor_reduce(most[0:1, :], trp[0:1, 0, 0:P], AX.X, ALU.max).then_inc(S["tr_read"], 1)
                    dve.wait_ge(S["tr_done"], TR_AT["M", p, 1])
                    dve.tensor_scalar(power, trp[:, 1, 0:1], 2.0 ** -60, 2.0 ** 60, ALU.max, ALU.min).then_inc(S["tr_read"], 1)
                    dve.wait_ge(S["tr_read"], TR_AT["M", p, 1])
                    bits = power.bitcast(I32)
                    link(dve.tensor_scalar(bits, bits, 0x7F800000, None, ALU.bitwise_and))
                    inv = no_scale if wide else scale
                    link(dve.tensor_scalar(inv.bitcast(I32), bits, -1.0, float(254 << 23), ALU.mult, ALU.add))
                    link(dve.tensor_scalar(inv, inv, 2.0 ** 14, None, ALU.mult))
                    dve.tensor_scalar(no_scale if wide else unscale, power, 2.0 ** -14, None, ALU.mult).then_inc(S["scale_ready"], 1)
                elif wide:
                    dve.memset(scale, 1.0)
                    dve.memset(unscale, 1.0).then_inc(S["scale_ready"], 1)
                else:
                    dve.memset(scale, 1024.0)
                    dve.memset(unscale, 1.0 / 1024.0).then_inc(S["scale_ready"], 1)
                dve.wait_ge(S["scale_ready"], p)
                if p <= LAYERS:
                    dve.tensor_scalar(wE_s, wE[:, (p - 1) * D:p * D], scale[0:AW, :], None, ALU.mult).then_inc(S["wE_ready"], 1)
                if wide:
                    return
                for j in range(PIECES):
                    now = slice(j * ROWS, (j + 1) * ROWS)
                    f2 = lambda v: v.rearrange("p t f -> p (t f)")
                    dve.wait_ge(S["split_hi"], (p - 1) * PIECES + j + 1)
                    dve.scalar_tensor_tensor(out=f2(parts[:, 1, now]), in0=f2(SRC[p][:, now]), scalar=scale[0:P, :], in1=f2(parts[:, 0, now]),
                                             op0=ALU.mult, op1=ALU.subtract).then_inc(S["split_lo"], 1)

            def end(wide):
                for hh in range(2):
                    last = dve.bn_aggr(mv3[:, hh], st6[:, hh].rearrange("p r c -> p (r c)"))
                last.then_inc(S["fin_ready"], 1)
                dve.wait_ge(S["fin_ready"], 2)
                link(dve.reciprocal(scale3, std3))
                link(dve.tensor_tensor(scale3, scale3, c_gamma, ALU.mult))
                link(dve.tensor_tensor(shift3, mv3[:, :, 0], scale3, ALU.mult))
                dve.tensor_tensor(shift3, c_beta, shift3, ALU.subtract).then_inc(S["fin_ready"], 1)
                def scales(r):
                    nt, h = RANGES[r][1], r % 2
                    dve.wait_ge(S["std_ready"], len(NORM) + r + 1)
                    if r >= 2:
                        dve.wait_ge(S["norm_ready"], NORM_AT["F", sum(RANGES[r - 2]) - 1])
                    link(dve.reciprocal(last_rstd[h][:, 0:nt], last_std[h][:, 0:nt]))
                    dve.scalar_tensor_tensor(out=last_shift[h][:, 0:nt], in0=last_mv[h][:, 0:nt, 0], scalar=-1.0, in1=last_rstd[h][:, 0:nt],
                                             op0=ALU.mult, op1=ALU.mult).then_inc(S["last_scales"], 1)
                for r, (t0, nt) in enumerate(RANGES):
                    for k in range(nt):
                        t = t0 + k
                        dve.wait_ge(S["tr_done"], TR_AT["F", t])
                        dve.tensor_tensor(Xn[:, t], Xn[:, t], trp[0:P, t % 2, 0:D], ALU.add).then_inc(S["gate_used"], 1)
                        dve.wait_ge(S["gate_used"], len(GATE_AT) + t + 1)
                        link(dve.bn_stats(bn6[:, k], Xn[:, t]))
                        last = dve.bn_aggr(last_mv[r % 2][:, k], bn6[:, k])
                    last.then_inc(S["mv_ready"], 1)
                    if r:
                        scales(r - 1)
                scales(NR - 1)

            run_schedule(dve, piece, stage, finish, degrees_and_count, begin, end)


_INS = ['x', 'src', 'dst', 'edge_attr_64', 'edge_weight', 'edge_weight_n2', 'L0_gnn_gamma', 'L0_gnn_beta', 'L0_gnn_W_in',
        'L0_gnn_b_in', 'L0_gnn_W_out', 'L0_gnn_b_out', 'L0_gnn_W_x2i', 'L0_gnn_b_x2i', 'L0_gnn_W_h2h', 'L1_gnn_Wl',
        'L1_gnn_bl', 'L1_gnn_Wr', 'L1_gnn_We', 'L1_gnn_be', 'L2_gnn_W_pre', 'L2_gnn_b_pre', 'L2_gnn_W1', 'L2_gnn_b1',
        'L2_gnn_W2', 'L2_gnn_b2', 'L2_gnn_W_post', 'L2_gnn_b_post', 'L3_gnn_W', 'L3_gnn_b', 'L3_gnn_gamma', 'L3_gnn_beta']


def kernel(**inputs):
    import numpy as _np
    import concourse.bacc as _bacc
    from concourse import mybir as _mybir
    from concourse.bass_utils import run_bass_kernel_spmd as _run

    nc = _bacc.Bacc("TRN2", target_bir_lowering=False, num_devices=1)
    arrays, args = {}, []
    for name in _INS:
        a = _np.ascontiguousarray(inputs[name])
        arrays[f"in_{name}"] = a
        args.append(nc.dram_tensor(f"in_{name}", a.shape, _mybir.dt.from_np(a.dtype), kind="ExternalInput").ap())
    out = nc.dram_tensor("out_0", arrays["in_x"].shape, F32, kind="ExternalOutput").ap()
    build_gnn(nc, *args, out)
    r = _run(nc, [arrays], core_ids=[0])
    return r.results[0]["out_0"]
```
